# Optimizing a Trainium2 kernel written in Bass

```python
import numpy as np
import jax
import jax.numpy as jnp

def _softmax(x, axis=-1):
    return jax.nn.softmax(x, axis=axis)

def _gelu(x):
    return jax.nn.gelu(x, approximate=True)

def _silu(x):
    return jax.nn.silu(x)

def _sigmoid(x):
    return jax.nn.sigmoid(x)

def _layernorm(x, axis=-1, eps=1e-05):
    m = jnp.mean(x, axis=axis, keepdims=True)
    v = jnp.var(x, axis=axis, keepdims=True)
    return (x - m) / jnp.sqrt(v + eps)

def _scatter_add(tgt, idx, src, axis=0):
    return tgt.at[idx].add(src)

def _segment_sum(src, seg, n):
    return jax.ops.segment_sum(src, seg, n)
kernel_name = 'mk_xattn_ffn_d2_seqx_r8_94c3e8'

def setup_inputs(seed: int=0):
    np.random.seed(seed)
    _w = jnp.asarray

    def _rec_inputs():
        import jax
        import jax.numpy as jnp
        _rk = jax.random.key(seed)
        x = 0.0002279 + 0.9999 * jax.random.normal(jax.random.fold_in(_rk, 1), (2, 512, 128), jnp.float32)
        _lenS = 512 - jax.random.randint(jax.random.fold_in(_rk, 7), (2,), 0, max(1, 512 // 4) + 1, jnp.int32)
        _lenS2 = 77 - jax.random.randint(jax.random.fold_in(_rk, 8), (2,), 0, max(1, 77 // 4) + 1, jnp.int32)
        _ctx_1024P = jax.random.normal(jax.random.fold_in(_rk, 11), (2, 16, 128), jnp.float32)
        _ctx_1024c = jax.random.dirichlet(jax.random.fold_in(_rk, 511), 0.3 * jnp.ones((16,), jnp.float32), (2, 77))
        _ctx_1024t = jnp.einsum('bsk,bkd->bsd', _ctx_1024c, _ctx_1024P)
        _ctx_1024t = _ctx_1024t * jax.lax.rsqrt(jnp.mean(jnp.square(_ctx_1024t)) + 1e-12) * 0.953939
        ctx_1024 = -0.000392918 + 0.999932 * (_ctx_1024t + 0.3 * jax.random.normal(jax.random.fold_in(_rk, 611), (2, 77, 128), jnp.float32))
        fside_Bx16_0 = 0.119436 + 0.907674 * jax.random.normal(jax.random.fold_in(_rk, 12), (2, 16), jnp.float32)
        return (x, ctx_1024, fside_Bx16_0)
    x, ctx_1024, fside_Bx16_0 = _rec_inputs()

    def _L0_xattn_setup():
        import jax, jax.numpy as jnp
        import numpy as np
        DIM = 128
        HEADS = 16
        DIM_HEAD = 64
        INNER = HEADS * DIM_HEAD
        EPS = 1e-05

        def layernorm(x, w, b):
            mu = jnp.mean(x, axis=-1, keepdims=True)
            var = jnp.mean(jnp.square(x - mu), axis=-1, keepdims=True)
            return (x - mu) * jax.lax.rsqrt(var + EPS) * w + b
        key = jax.random.key(seed)
        ks = jax.random.split(key, 9)
        b, n1, n2 = (4, 512, 32)
        x = jax.random.normal(ks[0], (b, n1, DIM), dtype=jnp.float32)
        latents = jax.random.normal(ks[1], (b, n2, DIM), dtype=jnp.float32)
        shift = jax.random.normal(ks[2], (b, HEADS), dtype=jnp.float32)
        scale = jax.random.normal(ks[3], (b, HEADS), dtype=jnp.float32)
        s = 1.0 / np.sqrt(DIM)
        Wq = jax.random.normal(ks[4], (DIM, INNER), dtype=jnp.float32) * s
        Wkv = jax.random.normal(ks[5], (DIM, 2 * INNER), dtype=jnp.float32) * s
        Wout = jax.random.normal(ks[6], (INNER, DIM), dtype=jnp.float32) * (1.0 / np.sqrt(INNER))
        ln1_w = jnp.ones((DIM,), jnp.float32)
        ln1_b = jnp.zeros((DIM,), jnp.float32)
        ln2_w = jnp.ones((DIM,), jnp.float32)
        ln2_b = jnp.zeros((DIM,), jnp.float32)
        return {'x': x, 'latents': latents, 'shift': shift, 'scale': scale, 'ln1_w': ln1_w, 'ln1_b': ln1_b, 'ln2_w': ln2_w, 'ln2_b': ln2_b, 'Wq': Wq, 'Wkv': Wkv, 'Wout': Wout}
    _L0_xattn_all = _L0_xattn_setup()
    _L0_xattn_in = {k: v for k, v in _L0_xattn_all.items() if k in ('ln1_w', 'ln1_b', 'ln2_w', 'ln2_b', 'Wq', 'Wkv', 'Wout')}
    del _L0_xattn_all

    def _L0_ffn_setup():
        import jax, jax.numpy as jnp
        import numpy as np
        CAPACITY_FACTOR = 1.0
        key = jax.random.key(seed)
        ks = jax.random.split(key, 5)
        B, S, D, E, F = (2, 256, 128, 8, 512)
        x = jax.random.normal(ks[0], (B, S, D), dtype=jnp.float32)
        Ws = jax.random.normal(ks[1], (D, E), dtype=jnp.float32) * (1.0 / np.sqrt(D))
        bs = jnp.zeros((E,), dtype=jnp.float32)
        W1 = jax.random.normal(ks[2], (E, D, F), dtype=jnp.float32) * (1.0 / np.sqrt(D))
        b1 = jnp.zeros((E, F), dtype=jnp.float32)
        W2 = jax.random.normal(ks[3], (E, F, D), dtype=jnp.float32) * (1.0 / np.sqrt(F))
        b2 = jnp.zeros((E, D), dtype=jnp.float32)
        return {'x': x, 'Ws': Ws, 'bs': bs, 'W1': W1, 'b1': b1, 'W2': W2, 'b2': b2}
    _L0_ffn_all = _L0_ffn_setup()
    _L0_ffn_in = {k: v for k, v in _L0_ffn_all.items() if k in ('Ws', 'bs', 'W1', 'b1', 'W2', 'b2')}
    del _L0_ffn_all

    def _L1_xattn_setup():
        import jax, jax.numpy as jnp
        import numpy as np
        B, SQ, SK, D = (4, 256, 256, 128)
        key = jax.random.key(seed)
        ks = jax.random.split(key, 8)
        s = 1.0 / np.sqrt(D)
        return {'input_seq': jax.random.normal(ks[0], (B, SQ, D), jnp.float32), 'condition_seq': jax.random.normal(ks[1], (B, SK, D), jnp.float32), 'Wq': jax.random.normal(ks[2], (D, D), jnp.float32) * s, 'bq': jnp.zeros((D,), jnp.float32), 'Wk': jax.random.normal(ks[3], (D, D), jnp.float32) * s, 'bk': jnp.zeros((D,), jnp.float32), 'Wv': jax.random.normal(ks[4], (D, D), jnp.float32) * s, 'bv': jnp.zeros((D,), jnp.float32)}
    _L1_xattn_all = _L1_xattn_setup()
    _L1_xattn_in = {k: v for k, v in _L1_xattn_all.items() if k in ('Wq', 'bq', 'Wk', 'bk', 'Wv', 'bv')}
    del _L1_xattn_all

    def _L1_ffn_setup():
        import jax, jax.numpy as jnp
        import numpy as np
        from jax import lax
        B, S, H = (2, 128, 128)
        I = 64
        E = 32
        TOP_K = 4
        N_GROUP = 4
        TOPK_GROUP = 2
        SCALE = 2.5
        N_SHARED = 2
        SH_I = I * N_SHARED

        def _route(tokens, router_weight, router_bias):
            logits = tokens.astype(jnp.float32) @ router_weight.astype(jnp.float32).T
            scores = jax.nn.sigmoid(logits)
            sfc = scores + router_bias[None, :]
            T = tokens.shape[0]
            grp = sfc.reshape(T, N_GROUP, E // N_GROUP)
            group_scores = lax.top_k(grp, 2)[0].sum(-1)
            _, gidx = lax.top_k(group_scores, TOPK_GROUP)
            gmask = jax.nn.one_hot(gidx, N_GROUP, dtype=sfc.dtype).sum(1)
            smask = jnp.broadcast_to(gmask[:, :, None], (T, N_GROUP, E // N_GROUP)).reshape(T, E)
            tmp = jnp.where(smask > 0, sfc, 0.0)
            _, topk_idx = lax.top_k(tmp, TOP_K)
            topk_w = jnp.take_along_axis(scores, topk_idx, axis=1)
            topk_w = topk_w / (topk_w.sum(-1, keepdims=True) + 1e-20)
            topk_w = topk_w * SCALE
            return (topk_idx, topk_w)
        key = jax.random.key(seed)
        ks = jax.random.split(key, 10)
        std = 0.02
        return {'hidden_states': jax.random.normal(ks[0], (B, S, H), jnp.float32), 'router_weight': jax.random.normal(ks[1], (E, H), jnp.float32) * std, 'router_bias': jnp.zeros((E,), jnp.float32), 'gate_w': jax.random.normal(ks[2], (E, I, H), jnp.float32) * std, 'up_w': jax.random.normal(ks[3], (E, I, H), jnp.float32) * std, 'down_w': jax.random.normal(ks[4], (E, H, I), jnp.float32) * std, 'shared_gate_w': jax.random.normal(ks[5], (SH_I, H), jnp.float32) * std, 'shared_up_w': jax.random.normal(ks[6], (SH_I, H), jnp.float32) * std, 'shared_down_w': jax.random.normal(ks[7], (H, SH_I), jnp.float32) * std}
    _L1_ffn_all = _L1_ffn_setup()
    _L1_ffn_in = {k: v for k, v in _L1_ffn_all.items() if k in ('router_weight', 'router_bias', 'gate_w', 'up_w', 'down_w', 'shared_gate_w', 'shared_up_w', 'shared_down_w')}
    del _L1_ffn_all
    return {'x': x, 'ctx_1024': ctx_1024, 'fside_Bx16_0': fside_Bx16_0, 'L0_xattn_ln1_w': _L0_xattn_in['ln1_w'], 'L0_xattn_ln1_b': _L0_xattn_in['ln1_b'], 'L0_xattn_ln2_w': _L0_xattn_in['ln2_w'], 'L0_xattn_ln2_b': _L0_xattn_in['ln2_b'], 'L0_xattn_Wq': _L0_xattn_in['Wq'], 'L0_xattn_Wkv': _L0_xattn_in['Wkv'], 'L0_xattn_Wout': _L0_xattn_in['Wout'], 'L0_ffn_Ws': _L0_ffn_in['Ws'], 'L0_ffn_bs': _L0_ffn_in['bs'], 'L0_ffn_W1': _L0_ffn_in['W1'], 'L0_ffn_b1': _L0_ffn_in['b1'], 'L0_ffn_W2': _L0_ffn_in['W2'], 'L0_ffn_b2': _L0_ffn_in['b2'], 'L1_xattn_Wq': _L1_xattn_in['Wq'], 'L1_xattn_bq': _L1_xattn_in['bq'], 'L1_xattn_Wk': _L1_xattn_in['Wk'], 'L1_xattn_bk': _L1_xattn_in['bk'], 'L1_xattn_Wv': _L1_xattn_in['Wv'], 'L1_xattn_bv': _L1_xattn_in['bv'], 'L1_ffn_router_weight': _L1_ffn_in['router_weight'], 'L1_ffn_router_bias': _L1_ffn_in['router_bias'], 'L1_ffn_gate_w': _L1_ffn_in['gate_w'], 'L1_ffn_up_w': _L1_ffn_in['up_w'], 'L1_ffn_down_w': _L1_ffn_in['down_w'], 'L1_ffn_shared_gate_w': _L1_ffn_in['shared_gate_w'], 'L1_ffn_shared_up_w': _L1_ffn_in['shared_up_w'], 'L1_ffn_shared_down_w': _L1_ffn_in['shared_down_w']}

def reference(x, ctx_1024, fside_Bx16_0, L0_xattn_ln1_w, L0_xattn_ln1_b, L0_xattn_ln2_w, L0_xattn_ln2_b, L0_xattn_Wq, L0_xattn_Wkv, L0_xattn_Wout, L0_ffn_Ws, L0_ffn_bs, L0_ffn_W1, L0_ffn_b1, L0_ffn_W2, L0_ffn_b2, L1_xattn_Wq, L1_xattn_bq, L1_xattn_Wk, L1_xattn_bk, L1_xattn_Wv, L1_xattn_bv, L1_ffn_router_weight, L1_ffn_router_bias, L1_ffn_gate_w, L1_ffn_up_w, L1_ffn_down_w, L1_ffn_shared_gate_w, L1_ffn_shared_up_w, L1_ffn_shared_down_w):
    import jax
    import jax.numpy as jnp

    def _L0_xattn_ref(x, latents, shift, scale, ln1_w, ln1_b, ln2_w, ln2_b, Wq, Wkv, Wout):
        import jax, jax.numpy as jnp
        import numpy as np
        DIM = 128
        HEADS = 16
        DIM_HEAD = 64
        INNER = HEADS * DIM_HEAD
        EPS = 1e-05

        def layernorm(x, w, b):
            mu = jnp.mean(x, axis=-1, keepdims=True)
            var = jnp.mean(jnp.square(x - mu), axis=-1, keepdims=True)
            return (x - mu) * jax.lax.rsqrt(var + EPS) * w + b
        b = x.shape[0]
        xn = layernorm(x, ln1_w, ln1_b)
        ln = layernorm(latents, ln2_w, ln2_b)
        q = ln @ Wq
        kv = xn @ Wkv
        k, v = jnp.split(kv, 2, axis=-1)
        q = q.reshape(b, -1, HEADS, DIM_HEAD)
        k = k.reshape(b, -1, HEADS, DIM_HEAD)
        v = v.reshape(b, -1, HEADS, DIM_HEAD)
        q = q * (1.0 + scale[:, None, :, None]) + shift[:, None, :, None]
        attn_scale = DIM_HEAD ** (-0.5)
        qk = jnp.einsum('bihd,bjhd->bhij', q.astype(jnp.float32), k.astype(jnp.float32)) * attn_scale
        attn = jax.nn.softmax(qk, axis=-1).astype(v.dtype)
        out = jnp.einsum('bhij,bjhd->bihd', attn, v)
        out = out.reshape(b, -1, INNER)
        return out @ Wout

    def _L0_ffn_ref(x, Ws, bs, W1, b1, W2, b2):
        import jax, jax.numpy as jnp
        import numpy as np
        CAPACITY_FACTOR = 1.0
        B, S, D = x.shape
        E = Ws.shape[1]
        N = B * S
        k = int(CAPACITY_FACTOR * N / E)
        xf = x.reshape(N, D)
        route_prob = jax.nn.softmax(xf @ Ws + bs, axis=-1).T
        route_vals, routes = jax.lax.top_k(route_prob, k)
        xin = xf[routes]
        h = jax.nn.gelu(jnp.einsum('ekd,edf->ekf', xin, W1) + b1[:, None, :])
        out = jnp.einsum('ekf,efd->ekd', h, W2) + b2[:, None, :]
        out = out * route_vals[..., None]
        final = jnp.zeros((N, D), dtype=x.dtype).at[routes.reshape(-1)].add(out.reshape(-1, D))
        return final.reshape(B, S, D)

    def _L1_xattn_ref(input_seq, condition_seq, Wq, bq, Wk, bk, Wv, bv):
        import jax, jax.numpy as jnp
        import numpy as np
        B, SQ, SK, D = (4, 256, 256, 128)
        q = jnp.einsum('bsd,ed->bse', input_seq, Wq) + bq
        k = jnp.einsum('btd,ed->bte', condition_seq, Wk) + bk
        v = jnp.einsum('btd,ed->bte', condition_seq, Wv) + bv
        scores = jnp.einsum('bse,bte->bst', q, k)
        attn = jax.nn.softmax(scores, axis=-1)
        attended = jnp.einsum('bst,bte->bse', attn, v)
        return attended

    def _L1_ffn_ref(hidden_states, router_weight, router_bias, gate_w, up_w, down_w, shared_gate_w, shared_up_w, shared_down_w):
        import jax, jax.numpy as jnp
        import numpy as np
        from jax import lax
        B, S, H = (2, 128, 128)
        I = 64
        E = 32
        TOP_K = 4
        N_GROUP = 4
        TOPK_GROUP = 2
        SCALE = 2.5
        N_SHARED = 2
        SH_I = I * N_SHARED

        def _route(tokens, router_weight, router_bias):
            logits = tokens.astype(jnp.float32) @ router_weight.astype(jnp.float32).T
            scores = jax.nn.sigmoid(logits)
            sfc = scores + router_bias[None, :]
            T = tokens.shape[0]
            grp = sfc.reshape(T, N_GROUP, E // N_GROUP)
            group_scores = lax.top_k(grp, 2)[0].sum(-1)
            _, gidx = lax.top_k(group_scores, TOPK_GROUP)
            gmask = jax.nn.one_hot(gidx, N_GROUP, dtype=sfc.dtype).sum(1)
            smask = jnp.broadcast_to(gmask[:, :, None], (T, N_GROUP, E // N_GROUP)).reshape(T, E)
            tmp = jnp.where(smask > 0, sfc, 0.0)
            _, topk_idx = lax.top_k(tmp, TOP_K)
            topk_w = jnp.take_along_axis(scores, topk_idx, axis=1)
            topk_w = topk_w / (topk_w.sum(-1, keepdims=True) + 1e-20)
            topk_w = topk_w * SCALE
            return (topk_idx, topk_w)
        tokens = hidden_states.reshape(-1, H)
        topk_idx, topk_w = _route(tokens, router_weight, router_bias)
        gate_vals = jax.nn.silu(jnp.einsum('th,eih->tei', tokens, gate_w))
        up_vals = jnp.einsum('th,eih->tei', tokens, up_w)
        hidden_vals = gate_vals * up_vals
        expert_out = jnp.einsum('tei,ehi->teh', hidden_vals, down_w)
        sel = jnp.take_along_axis(expert_out, topk_idx[:, :, None], axis=1)
        mixed = (sel * topk_w[:, :, None].astype(sel.dtype)).sum(1)
        mixed = mixed.reshape(hidden_states.shape)
        sg = jax.nn.silu(jnp.einsum('bsh,ih->bsi', hidden_states, shared_gate_w))
        su = jnp.einsum('bsh,ih->bsi', hidden_states, shared_up_w)
        shared = jnp.einsum('bsi,hi->bsh', sg * su, shared_down_w)
        return mixed + shared
    x = x + _L0_xattn_ref(ctx_1024, _layernorm(x, axis=-1), fside_Bx16_0, fside_Bx16_0, L0_xattn_ln1_w, L0_xattn_ln1_b, L0_xattn_ln2_w, L0_xattn_ln2_b, L0_xattn_Wq, L0_xattn_Wkv, L0_xattn_Wout)
    x = x + _L0_ffn_ref(_layernorm(x, axis=-1), L0_ffn_Ws, L0_ffn_bs, L0_ffn_W1, L0_ffn_b1, L0_ffn_W2, L0_ffn_b2)
    x = x + _L1_xattn_ref(_layernorm(x, axis=-1), ctx_1024, L1_xattn_Wq, L1_xattn_bq, L1_xattn_Wk, L1_xattn_bk, L1_xattn_Wv, L1_xattn_bv)
    x = x + _L1_ffn_ref(_layernorm(x, axis=-1), L1_ffn_router_weight, L1_ffn_router_bias, L1_ffn_gate_w, L1_ffn_up_w, L1_ffn_down_w, L1_ffn_shared_gate_w, L1_ffn_shared_up_w, L1_ffn_shared_down_w)
    return x

_drawn_inputs = setup_inputs


def setup_inputs(seed=0):
    import zlib

    import numpy as np

    out = dict(_drawn_inputs(seed))
    spreads = {'L0_xattn_ln1_w': (1.0, 0.2),
     'L0_xattn_ln1_b': (0.0, 0.1),
     'L0_xattn_ln2_w': (1.0, 0.2),
     'L0_xattn_ln2_b': (0.0, 0.1),
     'L0_ffn_bs': (0.0, 0.1),
     'L0_ffn_b1': (0.0, 0.1),
     'L0_ffn_b2': (0.0, 0.1),
     'L1_xattn_bq': (0.0, 0.1),
     'L1_xattn_bk': (0.0, 0.8),
     'L1_xattn_bv': (0.0, 0.1),
     'L1_ffn_router_bias': (0.0, 0.8)}
    factors = {'L1_ffn_router_weight': 8.0,
     'L1_ffn_gate_w': 8.0,
     'L1_ffn_up_w': 8.0,
     'L1_ffn_down_w': 8.0,
     'L1_ffn_shared_gate_w': 8.0,
     'L1_ffn_shared_up_w': 8.0,
     'L1_ffn_shared_down_w': 8.0}
    for name, (base, spread) in spreads.items():
        noise = np.random.default_rng([zlib.crc32(name.encode()), seed]).standard_normal(out[name].shape)
        drawn = base * np.exp(spread * noise) if base else spread * noise
        out[name] = jnp.asarray(drawn.astype(out[name].dtype))
    for name, factor in factors.items():
        out[name] = (out[name] * factor).astype(out[name].dtype)
    return out
```

```python
from contextlib import ExitStack

import concourse.bass as bass
from concourse import mybir

ALU = mybir.AluOpType
ACT = mybir.ActivationFunctionType
X = mybir.AxisListType.X
F32 = mybir.dt.float32
BF16 = mybir.dt.bfloat16
I32 = mybir.dt.int32

P = 128
B = 2
T = 8
TB = T // B
N = T * P
J = 77
BJ = B * J
H, DH = 16, 64
PAIRS = H // 2
JM, JR = 64, J - 64
RG = 8 * JR
NC = PAIRS + 2
HB = [6, 6, 4]
E0, F0 = 8, 512
FC = F0 // P
CAP = N // E0
SEARCH = 10
NM = 7
E1, I1 = 32, 64
NG, GE = 4, 8
CH = E1 * I1 // P
CHS = CH + 1
EPS = 1e-5


def block_kernel(nc, x, ctx, ctx_t, cols, f_pair, f_head, row, w_kv, wq_t, w_out, w1, w2, b2, l1w, gate, up, down,
                 out):
    es = ExitStack()
    with es:
        def sb(name, shape, dt=F32):
            return es.enter_context(nc.sbuf_tensor(name, shape, dt))

        def sem(name):
            return es.enter_context(nc.semaphore(name))

        ps = es.enter_context(nc.psum_tensor("ps", [P, 8, 512], F32))

        def bank(b, a=0, n=512, p=P):
            return ps[0:p, b, a:a + n]

        def bank16(b):
            return ps[:, b, :].bitcast(BF16)

        xs = sb("xs", [P, T, P])
        z = sb("z", [P, T, P])
        zT = sb("zT", [P, N])
        st = sb("st", [P, T, 6])
        mv = sb("mv", [P, T, 2])
        veps = sb("veps", [P, T])
        rstd = sb("rstd", [P, T])
        rsq = sb("rsq", [P, T])
        rstd2 = sb("rstd2", [P, T])
        neghalf = sb("neghalf", [P, T])
        ident = sb("ident", [P, P])
        ident16 = sb("ident16", [P, P], BF16)
        ones16 = sb("ones16", [P, P], BF16)
        ones_row = sb("ones_row", [1, P])
        tri16 = sb("tri16", [P, P], BF16)
        slot_no = sb("slot_no", [P, P], BF16)
        pair_sel = sb("pair_sel", [2, P])
        digit_i = sb("digit_i", [P, NM], I32)
        digits = sb("digits", [P, SEARCH, NM], I32)
        esel = sb("esel", [3 * E1, CH * P], BF16)
        earlier = sb("earlier", [P, NG, NG])
        scan_keep = sb("scan_keep", [P, TB, E1])
        c_nat = sb("c_nat", [J, B, P])
        cT = sb("cT", [P, BJ])
        cl = sb("cl", [P, 6 + E0 * FC])
        fp = sb("fp", [2, 2 * PAIRS])
        fh = sb("fh", [H, B])
        rw = sb("rw", [P, E0 + P + E1])
        bs_b, bv_b, rb_b = rw[:, 0:E0], rw[:, E0:E0 + P], rw[:, E0 + P:E0 + P + E1]
        wk = sb("wk", [P, H * DH])
        wv = sb("wv", [P, H * DH])
        wqT = sb("wqT", [P, PAIRS, P])
        wo = sb("wo", [P, PAIRS, P])
        lw = sb("lw", [P, 3 * P + E1 + E0])
        l1q, l1kT, l1vT, rwT = lw[:, 0:P], lw[:, P:2 * P], lw[:, 2 * P:3 * P], lw[:, 3 * P:3 * P + E1]
        rwS = lw[:, 3 * P + E1:3 * P + E1 + E0]
        w1s = sb("w1s", [P, E0, F0])
        w2s = sb("w2s", [P, E0, FC, P])
        b2s = sb("b2s", [P, E0, P])
        gs = sb("gs", [P, CHS * P])
        us = sb("us", [P, CHS * P])
        dn = sb("dn", [P, CHS * P])
        region = sb("region", [P, 2 * T * E0 * P // 2])

        def part_of(at, size, pattern, dt=F32, **dims):
            return region[:, at:at + size].bitcast(dt).rearrange(pattern, **dims)

        stc = sb("stc", [J, B, 6])
        mvc = sb("mvc", [J, B, 2])
        rstdc = sb("rstdc", [J, B])
        zc = sb("zc", [J, B, P])
        xnT = sb("xnT", [P, BJ])
        scl = sb("scl", [P, PAIRS, B])
        kT = sb("kT", [P, PAIRS, B, J])
        wks = sb("wks", [P, H])
        cr = sb("cr", [H, 3, B, J])
        crp = sb("crp", [H, 3, B, J], BF16)
        crow = sb("crow", [3, B, H, J], BF16)
        vmain = part_of(0, PAIRS * B * P, "p (c b k) -> p c b k", c=PAIRS, b=B)
        vrem = part_of(PAIRS * B * P, 2 * B * 5 * RG, "p (q b k) -> p q b k", q=2, b=B)
        M = sb("M", [P, B, H, J])
        U = sb("U", [P, B, NC, P])
        mx1 = sb("mx1", [P, 2, H])
        sm1 = sb("sm1", [P, 2, H])
        rc1 = sb("rc1", [P, 2, H])
        pe_ = part_of(0, 2 * H * J, "p (s h j) -> p s h j", s=2, h=H)
        pn = part_of(2 * H * J, 2 * H * J, "p (s k) -> p s k", s=2)
        pT = part_of(4 * H * J, 2 * NC * P, "p (s c q) -> p s c q", s=2, c=NC)
        lg = sb("lg", [P, T, E0])
        pr = sb("pr", [P, T, E0])
        sm8 = sb("sm8", [P, 3, T])
        prr = sb("prr", [P, 2, T, E0])
        prp = sb("prp", [P, T, E0, 3], BF16)
        zr = sb("zr", [P, T, P])
        zp = sb("zp", [P, 3, T, P], BF16)
        cand = sb("cand", [P, NM, E0], I32)
        best = sb("best", [P, 2, NM + 1, E0])
        cmp = sb("cmp", [P, NM, T, E0], BF16)
        ge = sb("ge", [P, 2, T, E0], BF16)
        need = sb("need", [P, E0])
        ceq = sb("ceq", [P, T, E0])
        q1 = sb("q1", [P, T, E0])
        q2 = sb("q2", [P, T, E0])
        slot = sb("slot", [P, T, E0])
        S = part_of(0, T * E0 * P // 2, "p (t e s) -> p t e s", BF16, t=T, e=E0)
        ST = part_of(T * E0 * P // 2, T * E0 * P // 2, "p (t e s) -> p t e s", BF16, t=T, e=E0)
        xin = sb("xin", [P, E0, P])
        pv = sb("pv", [P, E0])
        hg = sb("hg", [P, 2, FC, P])
        y1 = sb("y1", [P, P])
        y2 = sb("y2", [P, P])
        y3 = sb("y3", [P, P])
        yp = sb("yp", [P, 2, 3, P], BF16)
        k1T = sb("k1T", [P, BJ])
        c1 = sb("c1", [1, BJ])
        M1 = sb("M1", [P, BJ])
        v1 = sb("v1", [J, B, P])
        p1 = sb("p1", [P, TB, J])
        p1T = sb("p1T", [J, TB * P])
        sm4 = sb("sm4", [P, 3, TB])
        sc = sb("sc", [P, TB, E1])
        sf = sb("sf", [P, TB, E1])
        a4 = sb("a4", [P, 2, TB, NG, 4])
        a2 = sb("a2", [P, 4, TB, NG, 2])
        a1 = sb("a1", [P, 4, TB, NG])
        gg = sb("gg", [P, 2, TB, NG, NG])
        gm = sb("gm", [P, 2, TB, NG])
        top8 = sb("top8", [P, TB, 8])
        r1 = sb("r1", [P, TB, E1])
        r2 = sb("r2", [P, TB, E1])
        r3 = sb("r3", [P, TB, E1])
        n4 = sb("n4", [P, 2, TB])
        wp = sb("wp", [P, TB, 3, E1], BF16)
        wT = sb("wT", [3 * E1, N], BF16)
        sg = part_of(0 * 2 * TB * P, 2 * TB * P, "p (s q) -> p s q", s=2)
        hu = part_of(1 * 2 * TB * P, 2 * TB * P, "p (s q) -> p s q", s=2)
        hw = part_of(2 * 2 * TB * P, 2 * TB * P, "p (s q) -> p s q", s=2)
        yT = region[:, 6 * TB * P:7 * TB * P]

        ld = {k: sem("ld_" + k) for k in ("x", "ctx", "ctx_t", "cols", "fp", "fh", "row", "wk", "wv", "wq", "wo",
                                          "l1w", "w1", "w2", "b2", "gate", "up", "down")}
        pool_step = sem("pool_step")
        consts_ready = sem("consts_ready")
        moe_consts_ready = sem("moe_consts_ready")
        dve_step = sem("dve_step")
        act_step = sem("act_step")
        ctx_stats = sem("ctx_stats")
        ctx_rstd = sem("ctx_rstd")
        ln_stats = sem("ln_stats")
        ln_rstd = sem("ln_rstd")
        z_ready = sem("z_ready")
        fexp_done = sem("fexp_done")
        zc_ready = sem("zc_ready")
        zcT_done = sem("zcT_done")
        scl_ready = sem("scl_ready")
        xnT_ready = sem("xnT_ready")
        k_done = sem("k_done")
        kT_ready = sem("kT_ready")
        v_done = sem("v_done")
        vmain_ready = sem("vmain_ready")
        vrem_ready = sem("vrem_ready")
        vzero = sem("vzero")
        wks_ready = sem("wks_ready")
        ks_done = sem("ks_done")
        ks_read = sem("ks_read")
        crp_ready = sem("crp_ready")
        crow_ready = sem("crow_ready")
        zT_done = sem("zT_done")
        zT_ready = sem("zT_ready")
        m_done = sem("m_done")
        m_even = sem("m_even")
        m_odd = sem("m_odd")
        u_done = sem("u_done")
        u_main = sem("u_main")
        u_rem = sem("u_rem")
        s_done = sem("s_done")
        sub_done = sem("sub_done")
        exp_done = sem("exp_done")
        rc_ready = sem("rc_ready")
        nrm_done = sem("nrm_done")
        t_done = sem("t_done")
        pT_ready = sem("pT_ready")
        pv_done = sem("pv_done")
        x1_ready = sem("x1_ready")
        l1k_done = sem("l1k_done")
        l1k_ready = sem("l1k_ready")
        l1v_done = sem("l1v_done")
        l1v_ready = sem("l1v_ready")
        l1m_done = sem("l1m_done")
        l1m_ready = sem("l1m_ready")
        lg_done = sem("lg_done")
        lgs_ready = sem("lgs_ready")
        lge_ready = sem("lge_ready")
        pr_ready = sem("pr_ready")
        zp_ready = sem("zp_ready")
        prp_ready = sem("prp_ready")
        cmp_ready = sem("cmp_ready")
        cnt_done = sem("cnt_done")
        ge_ready = sem("ge_ready")
        rank_done = sem("rank_done")
        S_ready = sem("S_ready")
        st_done = sem("st_done")
        ST_ready = sem("ST_ready")
        gather_done = sem("gather_done")
        xin_ready = sem("xin_ready")
        pv_sum = sem("pv_sum")
        h_done = sem("h_done")
        hg_ready = sem("hg_ready")
        y_done = sem("y_done")
        yp_ready = sem("yp_ready")
        sc_done = sem("sc_done")
        x2_ready = sem("x2_ready")
        s1_done = sem("s1_done")
        p1s_ready = sem("p1s_ready")
        p1_ready = sem("p1_ready")
        p1T_done = sem("p1T_done")
        p1T_ready = sem("p1T_ready")
        pv1_done = sem("pv1_done")
        x3_ready = sem("x3_ready")
        rl_done = sem("rl_done")
        sig_ready = sem("sig_ready")
        wp_ready = sem("wp_ready")
        wt_done = sem("wt_done")
        wT_ready = sem("wT_ready")
        g_done = sem("g_done")
        u1_done = sem("u1_done")
        wb_done = sem("wb_done")
        sg_ready = sem("sg_ready")
        hu_ready = sem("hu_ready")
        hw_ready = sem("hw_ready")
        dn_done = sem("dn_done")
        yT_ready = sem("yT_ready")
        yt_done = sem("yt_done")
        yo_ready = sem("yo_ready")
        stored = sem("stored")

        block = es.enter_context(nc.Block())

        @block.sync
        def _(sp):
            sp.dma_start(c_nat[:], ctx.rearrange("b j d -> j b d")).then_inc(ld["ctx"], 16)
            sp.dma_start(cl[:], cols).then_inc(ld["cols"], 16)
            sp.dma_start(fp[:], f_pair).then_inc(ld["fp"], 16)
            sp.dma_start(wk[:], w_kv[:, 0:H * DH]).then_inc(ld["wk"], 16)
            sp.dma_start(wqT[:], wq_t.rearrange("(c p) d -> p c d", p=P)).then_inc(ld["wq"], 16)
            sp.dma_start(fh[:], f_head).then_inc(ld["fh"], 16)
            sp.dma_start(cT[:], ctx_t).then_inc(ld["ctx_t"], 16)
            sp.dma_start(lw[:], l1w).then_inc(ld["l1w"], 16)
            sp.wait_ge(crp_ready, 1)
            for part in range(3):
                for b in range(B):
                    sp.dma_start(crow[part:part + 1, b, :, :], crp[:, part, b, :]).then_inc(crow_ready, 16)
            sp.dma_start(rw[:], row.broadcast_to([P, E0 + P + E1])).then_inc(ld["row"], 16)
            sp.dma_start(w1s[:], w1.rearrange("p (e f) -> p e f", e=E0)).then_inc(ld["w1"], 16)
            sp.dma_start(w2s[:], w2.rearrange("p (e c d) -> p e c d", e=E0, c=FC)).then_inc(ld["w2"], 16)
            sp.dma_start(b2s[:].rearrange("p e d -> p (e d)"), b2.broadcast_to([P, E0 * P])).then_inc(ld["b2"], 16)
            sp.dma_start(gs[:], gate).then_inc(ld["gate"], 16)
            sp.dma_start(us[:], up).then_inc(ld["up"], 16)
            sp.dma_start(dn[:], down).then_inc(ld["down"], 16)
            for b in range(B):
                sp.wait_ge(yo_ready, b + 1)
                sp.dma_start(out[b].rearrange("(t p) d -> p t d", p=P), xs[:, TB * b:TB * b + TB, :])\
                  .then_inc(stored, 16)
            sp.wait_ge(stored, 16 * B)

        @block.gpsimd
        def _(pool):
            n = [0]

            def link(ins):
                n[0] += 1
                ins.then_inc(pool_step, 1)
                pool.wait_ge(pool_step, n[0])

            g = nc.gpsimd
            link(g.memset(ident[:], 0.0))
            link(g.affine_select(out=ident[:], in_=ident[:], compare_op=ALU.not_equal, fill=1.0, base=0,
                                 pattern=[[-1, P]], channel_multiplier=1))
            link(g.memset(pair_sel[:], 1.0))
            link(g.affine_select(out=pair_sel[:], in_=pair_sel[:], compare_op=ALU.is_ge, fill=0.0, base=0,
                                 pattern=[[1, P]], channel_multiplier=-DH))
            link(g.affine_select(out=pair_sel[:], in_=pair_sel[:], compare_op=ALU.is_ge, fill=0.0, base=DH - 1,
                                 pattern=[[-1, P]], channel_multiplier=DH))
            link(g.memset(neghalf[:], -0.5))
            g.tensor_copy(ident16[:], ident[:])
            g.memset(ones_row[:], 1.0)
            g.memset(ones16[:], 1.0).then_inc(consts_ready, 1)

            pool.wait_ge(ctx_stats, 1)
            link(g.tensor_scalar(rstdc[:], mvc[:, :, 1], EPS, None, ALU.add))
            g.tensor_tensor(rstdc[:], rstdc[:], neghalf[0:J, 0:B], ALU.pow).then_inc(ctx_rstd, 1)

            def ln(a, b, count):
                pool.wait_ge(ln_stats, count)
                link(g.tensor_scalar(veps[:, a:b], mv[:, a:b, 1], EPS, None, ALU.add))
                return g.tensor_tensor(rstd[:, a:b], veps[:, a:b], neghalf[:, a:b], ALU.pow)

            link(ln(0, T, 1))
            link(g.tensor_tensor(rsq[:], rstd[:], rstd[:], ALU.mult))
            link(g.tensor_tensor(rsq[:], rsq[:], mv[:, :, 1], ALU.mult))
            link(g.tensor_scalar(rsq[:], rsq[:], EPS, None, ALU.add))
            link(g.tensor_tensor(rstd2[:], rsq[:], neghalf[:], ALU.pow))
            g.tensor_tensor(rstd[:], rstd[:], rstd2[:], ALU.mult).then_inc(ln_rstd, 1)

            link(g.memset(tri16[:], 1.0))
            g.affine_select(out=tri16[:], in_=tri16[:], compare_op=ALU.is_ge, fill=0.0, base=0,
                            pattern=[[1, P]], channel_multiplier=-1)
            g.iota(slot_no[:], [[1, P]], base=1, channel_multiplier=0, allow_small_or_imprecise_dtypes=True)
            g.iota(digit_i[:], [[1, NM]], base=1, channel_multiplier=0)
            link(g.memset(earlier[:], 1.0))
            g.affine_select(out=earlier[:], in_=earlier[:], compare_op=ALU.is_gt, fill=0.0, base=0,
                            pattern=[[1, NG], [-1, NG]], channel_multiplier=0)
            link(g.memset(scan_keep[:], 1.0))
            link(g.memset(scan_keep[:, :, 0:1], 0.0))
            link(g.memset(esel[:], 1.0))
            for part in range(3):
                e = esel[part * E1:(part + 1) * E1, :]
                link(g.affine_select(out=e, in_=e, compare_op=ALU.is_ge, fill=0.0, base=0,
                                     pattern=[[1, CH * P]], channel_multiplier=-I1))
                link(g.affine_select(out=e, in_=e, compare_op=ALU.is_ge, fill=0.0, base=I1 - 1,
                                     pattern=[[-1, CH * P]], channel_multiplier=I1))
            g.memset(veps[:], 0.0).then_inc(moe_consts_ready, 1)

            for i in range(T):
                s = i % 2
                pool.wait_ge(rc_ready, i + 1)
                pool.wait_ge(exp_done, 2 * i + 2)
                if i >= 2:
                    pool.wait_ge(t_done, 3 * (i - 1))
                for j0, nj, at in ((0, JM, 0), (JM, JR, H * JM)):
                    ins = g.tensor_tensor(pn[:, s, at:at + H * nj].rearrange("p (h j) -> p h j", h=H),
                                          pe_[:, s, :, j0:j0 + nj],
                                          rc1[:, s].unsqueeze(2).broadcast_to([P, H, nj]), ALU.mult)
                ins.then_inc(nrm_done, 1)
            ln(0, T, 2).then_inc(ln_rstd, 1)

            pool.wait_ge(z_ready, 2 * T)
            for part in range(2):
                src = z if part == 0 else zr
                link(g.tensor_copy(zp[:, part], src[:]))
                link(g.tensor_tensor(zr[:], src[:], zp[:, part], ALU.subtract))
            g.tensor_copy(zp[:, 2], zr[:]).then_inc(zp_ready, 1)
            pool.wait_ge(pr_ready, 1)
            for part in range(2):
                src = pr[:] if part == 0 else prr[:, 0]
                link(g.tensor_copy(prp[:, :, :, part], src))
                link(g.tensor_tensor(prr[:, 0], src, prp[:, :, :, part], ALU.subtract))
            g.tensor_copy(prp[:, :, :, 2], prr[:, 0]).then_inc(prp_ready, 1)

            for k in range(2):
                for b in range(B):
                    ln(TB * b, TB * b + TB, 3 + 2 * k + b).then_inc(ln_rstd, 1)

        @block.scalar
        def _(act):
            a = nc.scalar
            act.dma_start(xs[:], x).then_inc(ld["x"], 16)
            act.dma_start(wv[:], w_kv[:, H * DH:2 * H * DH]).then_inc(ld["wv"], 16)
            act.dma_start(wo[:], w_out.rearrange("(c p) d -> p c d", p=P)).then_inc(ld["wo"], 16)

            act.wait_ge(vzero, 1)
            for k in range(4):
                act.wait_ge(v_done, k + 1)
                for h2 in range(2):
                    r = slice(DH * h2, DH * h2 + DH)
                    src = ps[r, 3 + k, 0:2 * BJ].rearrange("p (c b j) -> p c b j", c=2, b=B)
                    ins = a.activation(vmain[r, 2 * k:2 * k + 2, :, JM * h2:JM * h2 + JM], src[:, :, :, 0:JM], ACT.Copy)
                ins.then_inc(vmain_ready, 1)
            act.wait_ge(ld["cols"], 16)
            for half in range(2):
                act.wait_ge(zT_done, half + 1)
                a.activation(zT[:, 512 * half:512 * half + 512], bank(7), ACT.Identity, bias=cl[:, 3:4],
                             scale=cl[:, 2:3]).then_inc(zT_ready, 1)
            for k in range(3):
                act.wait_ge(m_done, 2 * k + 1)
                nh = min(3, 8 - 3 * k)
                for b in range(B):
                    src = bank(k, 0, nh * BJ).rearrange("p (h b j) -> p h b j", h=nh, b=B)
                    ins = a.activation(M[:, b, 6 * k:6 * k + 2 * nh:2, :], src[:, :, b, :], ACT.Copy)
                ins.then_inc(m_even, 1)
            for b in range(B):
                for half in range(2):
                    act.wait_ge(u_done, 2 * b + half + 1)
                    a.activation(U[:, b, 4 * half:4 * half + 4, :],
                                 bank([6, 7, 3, 4][2 * b + half]).rearrange("p (c d) -> p c d", c=4), ACT.Copy)\
                     .then_inc(u_main, 1)

            def exps(i):
                s = i % 2
                act.wait_ge(sub_done, 2 * i + 1)
                a.activation(pe_[:, s, 0:12, :], pe_[:, s, 0:12, :], ACT.Exp).then_inc(exp_done, 1)
                act.wait_ge(sub_done, 2 * i + 2)
                a.activation(pe_[:, s, 12:16, :], pe_[:, s, 12:16, :], ACT.Exp).then_inc(exp_done, 1)

            def evac(i):
                s = i % 2
                if i >= 2:
                    act.wait_ge(pv_done, i - 1)
                for k in range(3):
                    act.wait_ge(t_done, 3 * i + k + 1)
                    if k < 2:
                        a.activation(pT[:, s, 4 * k:4 * k + 4, :], bank(3 + k).rearrange("p (c q) -> p c q", c=4),
                                     ACT.Copy).then_inc(pT_ready, 1)
                    else:
                        a.activation(pT[0:RG, s, 8:10, :],
                                     bank(5, 0, 256, RG).rearrange("p (c q) -> p c q", c=2),
                                     ACT.Copy).then_inc(pT_ready, 1)

            for i in range(T + 1):
                if i < T:
                    exps(i)
                if i > 0:
                    evac(i - 1)

            def zcopy(half, k):
                act.wait_ge(zT_done, 2 * k + half + 1)
                a.activation(zT[:, 512 * half:512 * half + 512], bank(half), ACT.Copy).then_inc(zT_ready, 1)

            for half in range(2):
                zcopy(half, 1)
            act.wait_ge(lgs_ready, 1)
            a.activation(lg[:], lg[:], ACT.Exp).then_inc(lge_ready, 1)
            for t in range(T):
                act.wait_ge(st_done, t + 1)
                a.activation(ST[:, t].rearrange("p e s -> p (e s)"), bank16(3 + t % 2), ACT.Copy)\
                 .then_inc(ST_ready, 1)
            act.wait_ge(gather_done, 1)
            for half in range(2):
                a.activation(xin[:, 4 * half:4 * half + 4, :], bank(half).rearrange("p (e s) -> p e s", e=4),
                             ACT.Copy).then_inc(xin_ready, 1)
            for e in range(E0):
                act.wait_ge(h_done, e + 1)
                if e >= 2:
                    act.wait_ge(y_done, e - 1)
                for f in range(FC):
                    ins = a.activation(hg[:, e % 2, f, :], bank(5 + e % 2, P * f, P), ACT.Gelu_apprx_tanh,
                                       bias=cl[:, 6 + FC * e + f:7 + FC * e + f])
                ins.then_inc(hg_ready, 1)

            for b in range(B):
                zcopy(b, 2)
                act.wait_ge(p1s_ready, b + 1)
                a.activation(p1[:], p1[:], ACT.Exp).then_inc(p1_ready, 1)
                act.wait_ge(p1T_done, b + 1)
                a.activation(p1T[:], bank(3, 0, TB * P, J), ACT.Copy).then_inc(p1T_ready, 1)
            for b in range(B):
                zcopy(b, 3)
            for b in range(B):
                act.wait_ge(rl_done, b + 1)
                if b == 1:
                    act.wait_ge(wp_ready, 1)
                a.activation(sc[:], bank(7, 0, TB * E1).rearrange("p (t e) -> p t e", t=TB), ACT.Sigmoid)\
                 .then_inc(sig_ready, 1)
                act.wait_ge(wt_done, b + 1)
                a.activation(wT[:, 512 * b:512 * b + 512], bank16(7)[0:3 * E1, 512:1024], ACT.Copy)\
                 .then_inc(wT_ready, 1)
                for c in range(CHS):
                    n = CHS * b + c
                    act.wait_ge(g_done, n + 1)
                    if n >= 2:
                        act.wait_ge(hu_ready, n - 1)
                    a.activation(sg[:, n % 2, :], bank(n % 2), ACT.Silu).then_inc(sg_ready, 1)

        @block.tensor
        def _(pe):
            mm = nc.tensor.matmul
            tr = nc.tensor.transpose
            pe.wait_ge(consts_ready, 1)
            pe.wait_ge(ld["fp"], 16)
            mm(bank(7, 0, 16), pair_sel[:], fp[:], start=True, stop=True).then_inc(fexp_done, 1)
            pe.wait_ge(zc_ready, 1)
            pe.wait_ge(scl_ready, 1)
            for b in range(B):
                ins = tr(bank(7, 64 + J * b, J), zc[:, b, :], ident[0:J, 0:J])
            ins.then_inc(zcT_done, 1)
            pe.wait_ge(xnT_ready, 1)
            pe.wait_ge(ld["wk"], 16)
            for k in range(3):
                for c in range(3 * k, min(3 * k + 3, PAIRS)):
                    ins = mm(bank(k, BJ * (c - 3 * k), BJ), wk[:, P * c:P * c + P], xnT[:], start=True, stop=True)
                ins.then_inc(k_done, 1)
            pe.wait_ge(wks_ready, 1)
            mm(bank(7, 0, BJ, H), wks[:], xnT[:], start=True, stop=True).then_inc(ks_done, 1)
            pe.wait_ge(ld["wv"], 16)
            for k in range(4):
                for c in range(2 * k, 2 * k + 2):
                    ins = mm(bank(3 + k, BJ * (c - 2 * k), BJ), wv[:, P * c:P * c + P], xnT[:], start=True, stop=True)
                ins.then_inc(v_done, 1)

            def trans_half(half, b, count):
                pe.wait_ge(z_ready, count)
                for t in range(4):
                    ins = tr(bank(b, P * t, P), z[:, 4 * half + t, :], ident[:])
                ins.then_inc(zT_done, 1)

            pe.wait_ge(ks_read, 1)
            trans_half(0, 7, 4)
            pe.wait_ge(zT_ready, 1)
            trans_half(1, 7, 8)
            pe.wait_ge(kT_ready, 3)
            pe.wait_ge(ld["wq"], 16)
            for k in range(3):
                for h2 in range(2):
                    if h2 == 1:
                        pe.wait_ge(vmain_ready, k + 1)
                        pe.wait_ge(vrem_ready, k + 1)
                    r = slice(DH * h2, DH * h2 + DH)
                    for c in range(3 * k, min(3 * k + 3, PAIRS)):
                        ins = mm(bank(3 * h2 + k, BJ * (c - 3 * k), BJ), wqT[r, c, :],
                                 kT[r, c].rearrange("p b j -> p (b j)"), start=True, stop=True)
                    ins.then_inc(m_done, 1)
            pe.wait_ge(ld["wo"], 16)
            pe.wait_ge(vmain_ready, 4)
            pe.wait_ge(vrem_ready, 4)
            pe.wait_ge(zT_ready, 2)
            for b in range(B):
                for half in range(2):
                    if b == 1:
                        pe.wait_ge(m_odd, half + 1)
                    for c in range(4):
                        p = 4 * half + c
                        ins = mm(bank([6, 7, 3, 4][2 * b + half], P * c, P), vmain[:, p, b, :], wo[:, p, :],
                                 start=True, stop=True)
                    ins.then_inc(u_done, 1)
            pe.wait_ge(m_odd, 3)
            for b in range(B):
                for q in range(2):
                    for c in range(4):
                        ins = mm(bank(5, P * (2 * b + q), P, RG), vrem[:, q, b, RG * c:RG * c + RG], wo[:, 4 * q + c, :],
                                 start=(c == 0), stop=(c == 3))
            ins.then_inc(u_done, 1)

            pe.wait_ge(m_even, 3)
            pe.wait_ge(crow_ready, 16 * 6)

            def scores(i):
                b = i // TB
                if i > 0:
                    pe.wait_ge(sub_done, 2 * i)
                h0 = 0
                for k, nh in enumerate(HB):
                    mm(bank(k, 0, nh * J), zT[:, P * i:P * i + P], M[:, b, h0:h0 + nh, :].rearrange("p h j -> p (h j)"),
                       start=True, stop=False)
                    ins = mm(bank(k, 0, nh * J), ones16[0:3, :],
                             crow[:, b, h0:h0 + nh, :].rearrange("p h j -> p (h j)"), start=False, stop=True)
                    if k >= 1:
                        ins.then_inc(s_done, 1)
                    h0 += nh

            def turn(i):
                s = i % 2
                pe.wait_ge(nrm_done, i + 1)
                if i == 0:
                    pe.wait_ge(u_main, 4)
                    pe.wait_ge(u_rem, 1)
                else:
                    pe.wait_ge(pT_ready, 3 * i)
                for k in range(3):
                    for c in range(4 * k, min(4 * k + 4, NC)):
                        if c < PAIRS:
                            ins = tr(bank(3 + k, P * (c % 4), P), pn[:, s, P * c:P * c + P], ident[:])
                        else:
                            q = c - PAIRS
                            ins = tr(bank(5, P * q, P, RG), pn[:, s, H * JM + RG * q:H * JM + RG * q + RG], ident[:])
                    ins.then_inc(t_done, 1)

            def attend(i):
                s, b = i % 2, i // TB
                if i >= 2:
                    pe.wait_ge(x1_ready, i - 1)
                for c in range(NC):
                    if c % 4 == 0:
                        pe.wait_ge(pT_ready, 3 * i + c // 4 + 1)
                    r = P if c < PAIRS else RG
                    ins = mm(bank(6 + s, 0, P), pT[0:r, s, c, :], U[0:r, b, c, :], start=(c == 0), stop=(c == NC - 1))
                ins.then_inc(pv_done, 1)

            for i in range(T + 1):
                if i < T:
                    scores(i)
                if i > 0:
                    turn(i - 1)
                    attend(i - 1)

            pe.wait_ge(ld["l1w"], 16)
            pe.wait_ge(ld["ctx_t"], 16)
            mm(bank(3, 0, BJ), l1kT, cT[:], start=True, stop=True).then_inc(l1k_done, 1)
            for b in range(B):
                ins = mm(bank(4, P * b, P, J), cT[:, J * b:J * b + J], l1vT, start=True, stop=True)
            ins.then_inc(l1v_done, 1)
            pe.wait_ge(l1k_ready, 1)
            mm(bank(5, 0, BJ), l1q, k1T[:], start=True, stop=True)
            mm(bank(5, 256, BJ, 1), cl[:, 4:5], k1T[:], start=True, stop=True).then_inc(l1m_done, 1)

            for half in range(2):
                trans_half(half, half, T + 4 * half + 4)
            pe.wait_ge(zT_ready, 4)
            for t in range(T):
                ins = mm(bank(2, E0 * t, E0), zT[:, P * t:P * t + P], rwS, start=True, stop=True)
            ins.then_inc(lg_done, 1)
            for k in range(SEARCH):
                pe.wait_ge(cmp_ready, k + 1)
                for t in range(T):
                    ins = mm(bank(7, 0, NM * E0), ones16[:], cmp[:, :, t, :], start=(t == 0), stop=(t == T - 1))
                ins.then_inc(cnt_done, 1)
            pe.wait_ge(ge_ready, 1)
            rank = bank(6, 0, 2 * T * E0).rearrange("p (g t e) -> p g t e", g=2, t=T)
            mm(rank, tri16[:], ge[:], start=True, stop=False, skip_group_check=True)
            for k in range(T - 1):
                for w in range(2):
                    mm(rank[:, w, k + 1:T, :], ones16[:],
                       ge[:, w, k, :].unsqueeze(1).broadcast_to([P, T - 1 - k, E0]),
                       start=False, stop=(k == T - 2), skip_group_check=True)
            for t in range(T):
                ins = mm(bank(7, 64, E0), ones16[:], ge[:, 0, t, :], start=(t == 0), stop=(t == T - 1))
            ins.then_inc(rank_done, 1)
            pe.wait_ge(zp_ready, 1)
            pe.wait_ge(prp_ready, 1)
            for t in range(T):
                pe.wait_ge(S_ready, t + 1)
                for half in range(2):
                    for part in range(3):
                        ins = mm(bank(half), zp[:, part, t, :],
                                 S[:, t, 4 * half:4 * half + 4, :].rearrange("p e s -> p (e s)"),
                                 start=(t == 0 and part == 0), stop=(t == T - 1 and part == 2))
                for e in range(E0):
                    ins = mm(bank(2, 3 * e, 3), S[:, t, e, :], prp[:, t, e, :], start=(t == 0 and e == 0),
                             stop=(t == T - 1), skip_group_check=True)
                if t == T - 1:
                    ins.then_inc(gather_done, 1)
                if t >= 2:
                    pe.wait_ge(ST_ready, t - 1)
                for e in range(E0):
                    ins = tr(bank16(3 + t % 2)[:, P * e:P * e + P], S[:, t, e, :], ident16[:])
                ins.then_inc(st_done, 1)

            def expert_h(e):
                if e == 0:
                    pe.wait_ge(ld["w1"], 16)
                pe.wait_ge(xin_ready, e // 4 + 1)
                if e >= 2:
                    pe.wait_ge(hg_ready, e - 1)
                for f in range(FC):
                    ins = mm(bank(5 + e % 2, P * f, P), w1s[:, e, P * f:P * f + P], xin[:, e, :], start=True, stop=True)
                ins.then_inc(h_done, 1)

            def expert_y(e):
                if e == 0:
                    pe.wait_ge(ld["w2"], 16)
                pe.wait_ge(hg_ready, e + 1)
                if e >= 1:
                    pe.wait_ge(yp_ready, e)
                for f in range(FC):
                    ins = mm(bank(7, 128, P), hg[:, e % 2, f, :], w2s[:, e, f, :], start=(f == 0), stop=(f == FC - 1))
                ins.then_inc(y_done, 1)

            def scatter(e):
                pe.wait_ge(yp_ready, e + 1)
                if e == 0:
                    pe.wait_ge(ST_ready, T)
                for t in range(T):
                    for part in range(3):
                        ins = mm(bank(3 + t // 4, P * (t % 4), P), ST[:, t, e, :], yp[:, e % 2, part, :],
                                 start=(e == 0 and part == 0 and t % 4 == 0), stop=(e == E0 - 1),
                                 skip_group_check=True)
                    if t % 4 == 3:
                        ins.then_inc(sc_done, 1)

            expert_h(0)
            for e in range(E0):
                if e + 1 < E0:
                    expert_h(e + 1)
                expert_y(e)
                if e > 0:
                    scatter(e - 1)
            scatter(E0 - 1)

            pe.wait_ge(l1m_ready, 1)
            pe.wait_ge(l1v_ready, 1)
            pe.wait_ge(x2_ready, 1)
            for b in range(B):
                trans_half(b, b, 2 * T + 4 * b + 4)
                pe.wait_ge(zT_ready, 5 + b)
                if b == 1:
                    pe.wait_ge(x3_ready, 1)
                for t in range(TB):
                    mm(bank(2, J * t, J), zT[:, P * (TB * b + t):P * (TB * b + t) + P], M1[:, J * b:J * b + J],
                       start=True, stop=False)
                    ins = mm(bank(2, J * t, J), ones_row[:], c1[:, J * b:J * b + J], start=False, stop=True)
                ins.then_inc(s1_done, 1)
                pe.wait_ge(p1_ready, b + 1)
                if b == 0:
                    pe.wait_ge(x2_ready, 1)
                for t in range(TB):
                    ins = tr(bank(3, P * t, P, J), p1[:, t, :], ident[:])
                ins.then_inc(p1T_done, 1)
                pe.wait_ge(p1T_ready, b + 1)
                for t in range(TB):
                    ins = mm(bank(5, P * t, P), p1T[:, P * t:P * t + P], v1[:, b, :], start=True, stop=True)
                ins.then_inc(pv1_done, 1)

            for b in range(B):
                trans_half(b, b, 3 * T + 4 * b + 4)
            pe.wait_ge(zT_ready, 8)
            pe.wait_ge(ld["gate"], 16)
            pe.wait_ge(ld["up"], 16)
            pe.wait_ge(ld["down"], 16)
            pe.wait_ge(moe_consts_ready, 1)

            def router(b):
                if b == 1:
                    pe.wait_ge(wT_ready, 1)
                for t in range(TB):
                    q = TB * b + t
                    ins = mm(bank(7, E1 * t, E1), zT[:, P * q:P * q + P], rwT, start=True, stop=True)
                ins.then_inc(rl_done, 1)

            def weights(b):
                pe.wait_ge(wp_ready, b + 1)
                for t in range(TB):
                    ins = tr(bank16(7)[0:3 * E1, 512 + P * t:512 + P * t + P],
                             wp[:, t].rearrange("p a e -> p (a e)"), ident16[:])
                ins.then_inc(wt_done, 1)

            def gate_up(b, c):
                n = CHS * b + c
                zb = zT[:, 512 * b:512 * b + 512]
                if n >= 2:
                    pe.wait_ge(sg_ready, n - 1)
                mm(bank(n % 2), gs[:, P * c:P * c + P], zb, start=True, stop=True).then_inc(g_done, 1)
                if n >= 2:
                    pe.wait_ge(hu_ready, n - 1)
                mm(bank(2 + n % 2), us[:, P * c:P * c + P], zb, start=True, stop=True).then_inc(u1_done, 1)

            def spread(b, c):
                if c == CH:
                    return
                n = CH * b + c
                if n >= 2:
                    pe.wait_ge(hw_ready, CHS * b + c - 1)
                pe.wait_ge(wT_ready, b + 1)
                mm(bank(4 + n % 2), esel[:, P * c:P * c + P], wT[:, 512 * b:512 * b + 512], start=True, stop=True)\
                    .then_inc(wb_done, 1)

            def down_mm(b, c):
                n = CHS * b + c
                pe.wait_ge(hw_ready, n + 1)
                if c == 0 and b == 1:
                    pe.wait_ge(yo_ready, 1)
                ins = mm(bank(6), dn[:, P * c:P * c + P], hw[:, n % 2, :], start=(c == 0), stop=(c == CHS - 1))
                ins.then_inc(dn_done, 1)

            for b in range(B):
                router(b)
                gate_up(b, 0)
                weights(b)
                spread(b, 0)
                for c in range(CHS):
                    if c + 1 < CHS:
                        gate_up(b, c + 1)
                        spread(b, c + 1)
                    down_mm(b, c)
                pe.wait_ge(yT_ready, b + 1)
                for t in range(TB):
                    ins = tr(bank(6, P * t, P), yT[:, P * t:P * t + P], ident[:])
                ins.then_inc(yt_done, 1)

        @block.vector
        def _(dve):
            v = nc.vector
            n = [0]

            def link(ins):
                n[0] += 1
                ins.then_inc(dve_step, 1)
                dve.wait_ge(dve_step, n[0])

            def stats(t0, t1):
                for t in range(t0, t1):
                    ins = v.bn_stats(st[:, t, :], xs[:, t, :])
                link(ins)
                for t in range(t0, t1):
                    ins = v.bn_aggr(mv[:, t, :], st[:, t, :])
                return ins

            def norm(t0, t1, r):
                for t in range(t0, t1):
                    v.tensor_scalar(z[:, t, :], xs[:, t, :], mv[:, t, 0:1], r[:, t:t + 1], ALU.subtract, ALU.mult)\
                     .then_inc(z_ready, 1)

            v.memset(vmain, 0.0)
            v.memset(vrem, 0.0).then_inc(vzero, 1)
            dve.wait_ge(ld["ctx"], 16)
            for b in range(B):
                ins = v.bn_stats(stc[:, b, :], c_nat[:, b, :])
            link(ins)
            for b in range(B):
                ins = v.bn_aggr(mvc[:, b, :], stc[:, b, :])
            ins.then_inc(ctx_stats, 1)
            dve.wait_ge(ld["x"], 16)
            stats(0, T).then_inc(ln_stats, 1)
            dve.wait_ge(ctx_rstd, 1)
            dve.wait_ge(ctx_stats, 1)
            for b in range(B):
                ins = v.tensor_scalar(zc[:, b, :], c_nat[:, b, :], mvc[:, b, 0:1], rstdc[:, b:b + 1], ALU.subtract,
                                      ALU.mult)
            ins.then_inc(zc_ready, 1)
            dve.wait_ge(fexp_done, 1)
            v.tensor_scalar(scl[:], bank(7, 0, 16).rearrange("p (c b) -> p c b", b=B), 1.0, DH ** -0.5, ALU.add,
                            ALU.mult).then_inc(scl_ready, 1)
            dve.wait_ge(ld["cols"], 16)
            dve.wait_ge(zcT_done, 1)
            v.tensor_scalar(xnT[:], bank(7, 64, BJ), cl[:, 0:1], cl[:, 1:2], ALU.mult, ALU.add).then_inc(xnT_ready, 1)
            dve.wait_ge(ld["wk"], 16)
            v.tensor_reduce(wks[:], wk[:].rearrange("p (h d) -> p h d", h=H), X, ALU.add).then_inc(wks_ready, 1)
            dve.wait_ge(ks_done, 1)
            dve.wait_ge(ld["fh"], 16)
            for b in range(B):
                ins = v.tensor_scalar(cr[:, 0, b, :], bank(7, J * b, J, H), fh[:, b:b + 1], DH ** -0.5, ALU.mult,
                                      ALU.mult)
            ins.then_inc(ks_read, 1)
            dve.wait_ge(ln_rstd, 1)
            norm(0, T, rstd)
            dve.wait_ge(scl_ready, 1)
            for k in range(3):
                dve.wait_ge(k_done, k + 1)
                c0, c1_ = 3 * k, min(3 * k + 3, PAIRS)
                v.tensor_tensor(kT[:, c0:c1_], bank(k, 0, BJ * (c1_ - c0)).rearrange("p (c b j) -> p c b j", b=B, j=J),
                                scl[:, c0:c1_, :].unsqueeze(3).broadcast_to([P, c1_ - c0, B, J]), ALU.mult)\
                 .then_inc(kT_ready, 1)
            dve.wait_ge(ks_read, 1)
            for part in range(2):
                link(v.tensor_copy(crp[:, part], cr[:, part]))
                link(v.tensor_tensor(cr[:, part + 1], cr[:, part], crp[:, part], ALU.subtract))
            v.tensor_copy(crp[:, 2], cr[:, 2]).then_inc(crp_ready, 1)
            for k in range(4):
                dve.wait_ge(vmain_ready, k + 1)
                for h2 in range(2):
                    r = slice(DH * h2, DH * h2 + DH)
                    src = ps[r, 3 + k, 0:2 * BJ].rearrange("p (c b j) -> p c b j", c=2, b=B)
                    for c in range(2):
                        pp = (2 * k + c) % 4
                        at = RG * pp + 2 * JR * pp + JR * h2
                        ins = v.tensor_copy(vrem[r, k // 2, :, at:at + JR], src[:, c, :, JM:J])
                ins.then_inc(vrem_ready, 1)
            for k in range(3):
                dve.wait_ge(m_done, 2 * k + 2)
                nh = min(3, 8 - 3 * k)
                for b in range(B):
                    src = bank(3 + k, 0, nh * BJ).rearrange("p (h b j) -> p h b j", h=nh, b=B)
                    ins = v.tensor_copy(M[:, b, 6 * k + 1:6 * k + 2 * nh:2, :], src[:, :, b, :])
                ins.then_inc(m_odd, 1)
            dve.wait_ge(u_done, 5)
            v.tensor_copy(U[0:RG, :, 8:10, :], bank(5, 0, 512, RG).rearrange("p (b q d) -> p b q d", b=B, q=2))\
             .then_inc(u_rem, 1)

            SG = [(0, 12), (12, 16)]

            def sbank(g):
                if g == 0:
                    return ps[:, 0:2, 0:6 * J].rearrange("p k (h j) -> p k h j", j=J)
                return ps[:, 2:3, 0:4 * J].rearrange("p k (h j) -> p k h j", j=J)

            def submax(i):
                s = i % 2
                for g, (a, b) in enumerate(SG):
                    dve.wait_ge(s_done, 2 * i + g + 1)
                    k = 2 - g
                    link(v.tensor_reduce(mx1[:, s, a:b].rearrange("p (k h) -> p k h", k=k), sbank(g), X, ALU.max))
                    if i >= 2:
                        dve.wait_ge(nrm_done, i - 1)
                    h = (b - a) // k
                    v.tensor_tensor(pe_[:, s, a:b, :].rearrange("p (k h) j -> p k h j", k=k), sbank(g),
                                    mx1[:, s, a:b].rearrange("p (k h) -> p k h", k=k).unsqueeze(3)
                                    .broadcast_to([P, k, h, J]), ALU.subtract).then_inc(sub_done, 1)

            def sums(i):
                s = i % 2
                dve.wait_ge(exp_done, 2 * i + 2)
                link(v.tensor_reduce(sm1[:, s, :], pe_[:, s], X, ALU.add))
                v.reciprocal(rc1[:, s, :], sm1[:, s, :]).then_inc(rc_ready, 1)

            def resid(i):
                dve.wait_ge(pv_done, i + 1)
                v.tensor_tensor(xs[:, i, :], xs[:, i, :], bank(6 + i % 2, 0, P), ALU.add).then_inc(x1_ready, 1)

            for i in range(T + 2):
                if i < T:
                    submax(i)
                if 1 <= i <= T:
                    sums(i - 1)
                if i >= 2:
                    resid(i - 2)
            dve.wait_ge(x1_ready, T)
            stats(0, T).then_inc(ln_stats, 1)

            dve.wait_ge(l1k_done, 1)
            v.tensor_scalar(k1T[:], bank(3, 0, BJ), cl[:, 5:6], None, ALU.add).then_inc(l1k_ready, 1)
            dve.wait_ge(l1v_done, 1)
            dve.wait_ge(ld["row"], 16)
            v.tensor_tensor(v1[:], bank(4, 0, 2 * P, J).rearrange("p (b d) -> p b d", b=B),
                            bv_b[0:J].unsqueeze(1).broadcast_to([J, B, P]), ALU.add).then_inc(l1v_ready, 1)
            dve.wait_ge(l1m_done, 1)
            v.tensor_copy(c1[:], bank(5, 256, BJ, 1))
            v.tensor_copy(M1[:], bank(5, 0, BJ)).then_inc(l1m_ready, 1)

            dve.wait_ge(ln_rstd, 2)
            norm(0, T, rstd)
            dve.wait_ge(moe_consts_ready, 1)
            for k in range(SEARCH):
                ins = v.tensor_scalar(digits[:, k, :], digit_i[:], 3 * (SEARCH - 1 - k), None, ALU.logical_shift_left)
            link(ins)
            link(v.memset(best[:], 0.0))
            dve.wait_ge(lg_done, 1)
            bt = lambda a: a.unsqueeze(2).broadcast_to([P, T, E0])
            link(v.tensor_tensor(lg[:], bank(2, 0, T * E0).rearrange("p (t e) -> p t e", t=T),
                                 bs_b.unsqueeze(1).broadcast_to([P, T, E0]), ALU.add))
            link(v.tensor_reduce(sm8[:, 0, :], lg[:], X, ALU.max))
            v.tensor_tensor(lg[:], lg[:], bt(sm8[:, 0, :]), ALU.subtract).then_inc(lgs_ready, 1)
            dve.wait_ge(lge_ready, 1)
            link(v.tensor_reduce(sm8[:, 1, :], lg[:], X, ALU.add))
            link(v.reciprocal(sm8[:, 2, :], sm8[:, 1, :]))
            v.tensor_tensor(pr[:], lg[:], bt(sm8[:, 2, :]), ALU.mult).then_inc(pr_ready, 1)
            dve.wait_ge(pr_ready, 1)
            for k in range(SEARCH):
                cur, nxt = best[:, k % 2], best[:, (k + 1) % 2]
                link(v.tensor_tensor(cand[:], cur[:, 0, :].bitcast(I32).unsqueeze(1).broadcast_to([P, NM, E0]),
                                     digits[:, k, :].unsqueeze(2).broadcast_to([P, NM, E0]), ALU.bitwise_or))
                for m in range(NM):
                    ins = v.tensor_tensor(cmp[:, m], pr[:], cand[:, m, :].bitcast(F32).unsqueeze(1)
                                          .broadcast_to([P, T, E0]), ALU.is_ge)
                ins.then_inc(cmp_ready, 1)
                dve.wait_ge(cnt_done, k + 1)
                link(v.scalar_tensor_tensor(out=cur[:, 1:NM + 1, :],
                                            in0=bank(7, 0, NM * E0).rearrange("p (m e) -> p m e", m=NM),
                                            scalar=float(CAP), in1=cand[:].bitcast(F32), op0=ALU.is_ge, op1=ALU.mult))
                link(v.tensor_reduce(nxt[:, 0, :], cur.rearrange("p m e -> p e m"), X, ALU.max))
            thr = best[:, SEARCH % 2, 0, :].unsqueeze(1).broadcast_to([P, T, E0])
            v.tensor_tensor(ge[:, 0], pr[:], thr, ALU.is_gt)
            v.tensor_tensor(ge[:, 1], pr[:], thr, ALU.is_equal).then_inc(ge_ready, 1)
            dve.wait_ge(rank_done, 1)
            dve.wait_ge(ge_ready, 1)
            rank = bank(6, 0, 2 * T * E0).rearrange("p (g t e) -> p g t e", g=2, t=T)
            link(v.tensor_scalar(need[:], bank(7, 64, E0), -1.0, float(CAP), ALU.mult, ALU.add))
            nb = need[:].unsqueeze(1).broadcast_to([P, T, E0])
            v.tensor_tensor(q1[:], rank[:, 1], nb, ALU.is_le)
            link(v.tensor_tensor(ceq[:], rank[:, 1], nb, ALU.min))
            v.tensor_tensor(q2[:], q1[:], ge[:, 1], ALU.mult)
            link(v.tensor_tensor(ceq[:], rank[:, 0], ceq[:], ALU.add))
            link(v.tensor_tensor(q2[:], q2[:], ge[:, 0], ALU.add))
            link(v.tensor_tensor(slot[:], q2[:], ceq[:], ALU.mult))
            for t in range(T):
                for e in range(E0):
                    ins = v.tensor_scalar(S[:, t, e, :], slot_no[:], slot[:, t, e:e + 1], None, ALU.is_equal)
                ins.then_inc(S_ready, 1)
            dve.wait_ge(gather_done, 1)
            v.tensor_reduce(pv[:], bank(2, 0, 3 * E0).rearrange("p (e a) -> p e a", a=3), X, ALU.add)\
             .then_inc(pv_sum, 1)
            dve.wait_ge(pv_sum, 1)
            dve.wait_ge(ld["b2"], 16)
            for e in range(E0):
                s = e % 2
                dve.wait_ge(y_done, e + 1)
                link(v.tensor_tensor(y1[:], bank(7, 128, P), b2s[:, e, :], ALU.add))
                link(v.tensor_scalar(y2[:], y1[:], pv[:, e:e + 1], None, ALU.mult))
                if e >= 2:
                    dve.wait_ge(sc_done, 2 * (e - 1))
                link(v.tensor_copy(yp[:, s, 0], y2[:]))
                link(v.tensor_tensor(y3[:], y2[:], yp[:, s, 0], ALU.subtract))
                link(v.tensor_copy(yp[:, s, 1], y3[:]))
                v.tensor_tensor(yp[:, s, 2], y3[:], yp[:, s, 1], ALU.subtract).then_inc(yp_ready, 1)
            for b in range(B):
                dve.wait_ge(sc_done, 2 * (E0 - 1) + b + 1)
                link(v.tensor_tensor(xs[:, TB * b:TB * b + TB, :], xs[:, TB * b:TB * b + TB, :],
                                     bank(3 + b).rearrange("p (t d) -> p t d", t=TB), ALU.add))
                stats(TB * b, TB * b + TB).then_inc(ln_stats, 1)
            v.memset(sm4[:], 0.0).then_inc(x2_ready, 1)

            for b in range(B):
                dve.wait_ge(ln_rstd, 3 + b)
                norm(TB * b, TB * b + TB, rstd)
            dve.wait_ge(x2_ready, 1)
            for b in range(B):
                dve.wait_ge(s1_done, b + 1)
                if b == 1:
                    dve.wait_ge(p1T_done, 1)
                s1 = bank(2, 0, TB * J).rearrange("p (t j) -> p t j", t=TB)
                link(v.tensor_reduce(sm4[:, 0, :], s1, X, ALU.max))
                v.tensor_tensor(p1[:], s1, sm4[:, 0, :].unsqueeze(2).broadcast_to([P, TB, J]), ALU.subtract)\
                 .then_inc(p1s_ready, 1)
                dve.wait_ge(p1_ready, b + 1)
                link(v.tensor_reduce(sm4[:, 1, :], p1[:], X, ALU.add))
                link(v.reciprocal(sm4[:, 2, :], sm4[:, 1, :]))
                dve.wait_ge(pv1_done, b + 1)
                for t in range(TB):
                    q = TB * b + t
                    ins = v.scalar_tensor_tensor(out=xs[:, q, :], in0=bank(5, P * t, P), scalar=sm4[:, 2, t:t + 1],
                                                 in1=xs[:, q, :], op0=ALU.mult, op1=ALU.add)
                ins.then_inc(x3_ready, 1)
                dve.wait_ge(x3_ready, b + 1)
                stats(TB * b, TB * b + TB).then_inc(ln_stats, 1)
            for b in range(B):
                dve.wait_ge(ln_rstd, 5 + b)
                norm(TB * b, TB * b + TB, rstd)

            def route(b):
                dve.wait_ge(sig_ready, b + 1)
                link(v.tensor_tensor(sf[:], sc[:], rb_b.unsqueeze(1).broadcast_to([P, TB, E1]), ALU.add))
                q = sf[:].rearrange("p t (g k) -> p (t g) k", g=NG)
                hi4 = a4[:, 0].rearrange("p t g k -> p (t g) k")
                lo4 = a4[:, 1].rearrange("p t g k -> p (t g) k")
                v.tensor_tensor(hi4, q[:, :, 0:4], q[:, :, 4:8], ALU.max)
                link(v.tensor_tensor(lo4, q[:, :, 0:4], q[:, :, 4:8], ALU.min))
                w2_ = [a2[:, k].rearrange("p t g k -> p (t g) k") for k in range(4)]
                v.tensor_tensor(w2_[0], hi4[:, :, 0:2], hi4[:, :, 2:4], ALU.max)
                v.tensor_tensor(w2_[1], hi4[:, :, 0:2], hi4[:, :, 2:4], ALU.min)
                link(v.tensor_tensor(w2_[2], lo4[:, :, 0:2], lo4[:, :, 2:4], ALU.max))
                link(v.tensor_tensor(w2_[1], w2_[1], w2_[2], ALU.max))
                w1_ = [a1[:, k].rearrange("p t g -> p (t g)").unsqueeze(2) for k in range(4)]
                v.tensor_tensor(w1_[0], w2_[0][:, :, 0:1], w2_[0][:, :, 1:2], ALU.max)
                v.tensor_tensor(w1_[1], w2_[0][:, :, 0:1], w2_[0][:, :, 1:2], ALU.min)
                link(v.tensor_tensor(w1_[2], w2_[1][:, :, 0:1], w2_[1][:, :, 1:2], ALU.max))
                link(v.tensor_tensor(w1_[1], w1_[1], w1_[2], ALU.max))
                link(v.tensor_tensor(w1_[0], w1_[0], w1_[1], ALU.add))
                mine = a1[:, 0].unsqueeze(3).broadcast_to([P, TB, NG, NG])
                other = a1[:, 0].unsqueeze(2).broadcast_to([P, TB, NG, NG])
                v.tensor_tensor(gg[:, 0], other, mine, ALU.is_gt)
                link(v.tensor_tensor(gg[:, 1], other, mine, ALU.is_equal))
                link(v.tensor_tensor(gg[:, 1], gg[:, 1], earlier[:].unsqueeze(1).broadcast_to([P, TB, NG, NG]),
                                     ALU.mult))
                link(v.tensor_tensor(gg[:, 0], gg[:, 0], gg[:, 1], ALU.add))
                link(v.tensor_reduce(gm[:, 0], gg[:, 0], X, ALU.add))
                link(v.tensor_scalar(gm[:, 1], gm[:, 0], 2.0, None, ALU.is_lt))
                link(v.tensor_tensor(q, q, gm[:, 1].rearrange("p t g -> p (t g)").unsqueeze(2)
                                     .broadcast_to([P, TB * NG, GE]), ALU.mult))
                for t in range(TB):
                    ins = v.max(top8[:, t, :], sf[:, t, :])
                link(ins)
                fourth = top8[:, :, 3:4].broadcast_to([P, TB, E1])
                v.tensor_tensor(r1[:], sf[:], fourth, ALU.is_gt)
                link(v.tensor_tensor(r2[:], sf[:], fourth, ALU.is_equal))
                v.tensor_reduce(n4[:, 0, :], r1[:], X, ALU.add)
                link(v.tensor_tensor_scan(r3[:].rearrange("p t e -> p (t e)"),
                                          scan_keep[:].rearrange("p t e -> p (t e)"),
                                          r2[:].rearrange("p t e -> p (t e)"), 0.0, ALU.mult, ALU.add))
                link(v.tensor_tensor(r3[:], r3[:], n4[:, 0, :].unsqueeze(2).broadcast_to([P, TB, E1]), ALU.add))
                link(v.scalar_tensor_tensor(out=r3[:], in0=r3[:], scalar=4.0, in1=r2[:], op0=ALU.is_le, op1=ALU.mult))
                link(v.tensor_tensor(r3[:], r3[:], r1[:], ALU.add))
                link(v.tensor_tensor(r3[:], r3[:], sc[:], ALU.mult))
                link(v.tensor_reduce(n4[:, 0, :], r3[:], X, ALU.add))
                link(v.tensor_scalar(n4[:, 0, :], n4[:, 0, :], 1e-20, None, ALU.add))
                link(v.reciprocal(n4[:, 1, :], n4[:, 0, :]))
                link(v.scalar_tensor_tensor(out=r3[:], in0=r3[:], scalar=2.5,
                                            in1=n4[:, 1, :].unsqueeze(2).broadcast_to([P, TB, E1]),
                                            op0=ALU.mult, op1=ALU.mult))
                if b == 1:
                    dve.wait_ge(wt_done, 1)
                link(v.tensor_copy(wp[:, :, 0, :], r3[:]))
                link(v.tensor_tensor(r1[:], r3[:], wp[:, :, 0, :], ALU.subtract))
                link(v.tensor_copy(wp[:, :, 1, :], r1[:]))
                v.tensor_tensor(wp[:, :, 2, :], r1[:], wp[:, :, 1, :], ALU.subtract).then_inc(wp_ready, 1)

            def mul_up(b, c):
                k = CHS * b + c
                dve.wait_ge(sg_ready, k + 1)
                dve.wait_ge(u1_done, k + 1)
                dst = hu if c < CH else hw
                if c == CH:
                    dve.wait_ge(dn_done, k - 1)
                v.tensor_tensor(dst[:, k % 2, :], sg[:, k % 2, :], bank(2 + k % 2), ALU.mult).then_inc(hu_ready, 1)

            def mul_w(b, c):
                k = CHS * b + c
                dve.wait_ge(hu_ready, k + 1)
                if c == CH:
                    v.tensor_copy(n4[:, 0, 0:1], n4[:, 1, 0:1]).then_inc(hw_ready, 1)
                    return
                dve.wait_ge(wb_done, CH * b + c + 1)
                if k >= 2:
                    dve.wait_ge(dn_done, k - 1)
                v.tensor_tensor(hw[:, k % 2, :], hu[:, k % 2, :], bank(4 + (CH * b + c) % 2), ALU.mult)\
                 .then_inc(hw_ready, 1)

            for b in range(B):
                route(b)
                mul_up(b, 0)
                for c in range(CHS):
                    mul_w(b, c)
                    if c + 1 < CHS:
                        mul_up(b, c + 1)
                dve.wait_ge(dn_done, CHS * (b + 1))
                v.tensor_copy(yT, bank(6)).then_inc(yT_ready, 1)
                dve.wait_ge(yt_done, b + 1)
                v.tensor_tensor(xs[:, TB * b:TB * b + TB, :], xs[:, TB * b:TB * b + TB, :],
                                bank(6).rearrange("p (t d) -> p t d", t=TB), ALU.add).then_inc(yo_ready, 1)


def kernel(**inputs):
    import numpy as np
    import concourse.bacc as bacc
    from concourse import mybir as mb
    from concourse.bass_utils import run_bass_kernel_spmd

    g = {k: np.asarray(v) for k, v in inputs.items()}
    col = lambda a: np.asarray(a).reshape(-1, P).T
    per = {
        "x": g["x"].reshape(T, P, P).transpose(1, 0, 2),
        "ctx": g["ctx_1024"],
        "ctx_t": g["ctx_1024"].reshape(BJ, P).T,
        "cols": np.concatenate([col(g[k]) for k in ("L0_xattn_ln1_w", "L0_xattn_ln1_b", "L0_xattn_ln2_w",
                                                    "L0_xattn_ln2_b", "L1_xattn_bq", "L1_xattn_bk",
                                                    "L0_ffn_b1")], 1),
        "f_pair": g["fside_Bx16_0"].reshape(B, PAIRS, 2).transpose(2, 1, 0).reshape(2, 2 * PAIRS),
        "f_head": g["fside_Bx16_0"].T,
        "row": np.concatenate([g["L0_ffn_bs"], g["L1_xattn_bv"], g["L1_ffn_router_bias"]]).reshape(1, -1),
        "w_kv": g["L0_xattn_Wkv"],
        "wq_t": g["L0_xattn_Wq"].T,
        "w_out": g["L0_xattn_Wout"],
        "w1": g["L0_ffn_W1"].transpose(1, 0, 2).reshape(P, -1),
        "w2": g["L0_ffn_W2"].reshape(E0, FC, P, P).transpose(2, 0, 1, 3).reshape(P, -1),
        "b2": g["L0_ffn_b2"].reshape(1, -1),
        "l1w": np.concatenate([g["L1_xattn_Wq"], g["L1_xattn_Wk"].T, g["L1_xattn_Wv"].T,
                               g["L1_ffn_router_weight"].T, g["L0_ffn_Ws"]], 1),
        "gate": np.concatenate([g["L1_ffn_gate_w"].reshape(-1, P), g["L1_ffn_shared_gate_w"]]).T,
        "up": np.concatenate([g["L1_ffn_up_w"].reshape(-1, P), g["L1_ffn_shared_up_w"]]).T,
        "down": np.concatenate([g["L1_ffn_down_w"].transpose(0, 2, 1).reshape(CH, P, P),
                                g["L1_ffn_shared_down_w"].T[None]]).transpose(1, 0, 2).reshape(P, -1),
    }
    nc = bacc.Bacc("TRN2", target_bir_lowering=False, num_devices=1)
    arrays, args = {}, []
    for name, a in per.items():
        a = np.ascontiguousarray(a)
        arrays[f"in_{name}_dram"] = a
        args.append(nc.dram_tensor(f"in_{name}_dram", a.shape, mb.dt.from_np(a.dtype), kind="ExternalInput").ap())
    args.append(nc.dram_tensor("out_0_dram", (B, TB * P, P), F32, kind="ExternalOutput").ap())
    block_kernel(nc, *args)
    r = run_bass_kernel_spmd(nc, [arrays], core_ids=[0])
    return r.results[0]["out_0_dram"]
```

```python
from contextlib import ExitStack

import concourse.bass as bass
from concourse import mybir

ALU = mybir.AluOpType
ACT = mybir.ActivationFunctionType
X = mybir.AxisListType.X
F32 = mybir.dt.float32
BF16 = mybir.dt.bfloat16
I32 = mybir.dt.int32

P = 128
B = 2
T = 8
TB = T // B
N = T * P
J = 77
BJ = B * J
H, DH = 16, 64
PAIRS = H // 2
JM, JR = 64, J - 64
RG = 8 * JR
NC = PAIRS + 2
HB = [6, 6, 4]
E0, F0 = 8, 512
FC = F0 // P
CAP = N // E0
SEARCH = 10
NM = 7
E1, I1 = 32, 64
NG, GE = 4, 8
CH = E1 * I1 // P
CHS = CH + 1
LEAD = 6
NHU, NHW = LEAD + 2, 3
EPS = 1e-5


def block_kernel(nc, x, ctx, ctx_t, cols, f_pair, f_head, row, w_kv, wq_t, w_out, w1, w2, b2, l1w, gate, up, down,
                 out):
    es = ExitStack()
    with es:
        def sb(name, shape, dt=F32):
            return es.enter_context(nc.sbuf_tensor(name, shape, dt))

        def sem(name):
            return es.enter_context(nc.semaphore(name))

        ps = es.enter_context(nc.psum_tensor("ps", [P, 8, 512], F32))

        def bank(b, a=0, n=512, p=P):
            return ps[0:p, b, a:a + n]

        def bank16(b):
            return ps[:, b, :].bitcast(BF16)

        xs = sb("xs", [P, T, P])
        z = sb("z", [P, T, P])
        zT = sb("zT", [P, N])
        st = sb("st", [P, T, 6])
        mv = sb("mv", [P, T, 2])
        veps = sb("veps", [P, T])
        rstd = sb("rstd", [P, T])
        rsq = sb("rsq", [P, T])
        rstd2 = sb("rstd2", [P, T])
        neghalf = sb("neghalf", [P, T])
        ident = sb("ident", [P, P])
        ident16 = sb("ident16", [P, P], BF16)
        ones16 = sb("ones16", [P, P], BF16)
        ones_row = sb("ones_row", [1, P])
        tri16 = sb("tri16", [P, P], BF16)
        slot_no = sb("slot_no", [P, P], BF16)
        pair_sel = sb("pair_sel", [2, P])
        digit_i = sb("digit_i", [P, NM], I32)
        digits = sb("digits", [P, SEARCH, NM], I32)
        esel = sb("esel", [3 * E1, CH * P], BF16)
        earlier = sb("earlier", [P, NG, NG])
        scan_keep = sb("scan_keep", [P, TB, E1])
        c_nat = sb("c_nat", [J, B, P])
        cT = sb("cT", [P, BJ])
        cl = sb("cl", [P, 6 + E0 * FC])
        fp = sb("fp", [2, 2 * PAIRS])
        fh = sb("fh", [H, B])
        rw = sb("rw", [P, E0 + P + E1])
        bs_b, bv_b, rb_b = rw[:, 0:E0], rw[:, E0:E0 + P], rw[:, E0 + P:E0 + P + E1]
        wk = sb("wk", [P, H * DH])
        wv = sb("wv", [P, H * DH])
        wqT = sb("wqT", [P, PAIRS, P])
        wo = sb("wo", [P, PAIRS, P])
        lw = sb("lw", [P, 3 * P + E1 + E0])
        l1q, l1kT, l1vT, rwT = lw[:, 0:P], lw[:, P:2 * P], lw[:, 2 * P:3 * P], lw[:, 3 * P:3 * P + E1]
        rwS = lw[:, 3 * P + E1:3 * P + E1 + E0]
        w1s = sb("w1s", [P, E0, F0])
        w2s = sb("w2s", [P, E0, FC, P])
        b2s = sb("b2s", [P, E0, P])
        gs = sb("gs", [P, CHS * P])
        us = sb("us", [P, CHS * P])
        dn = sb("dn", [P, CHS * P])
        region = sb("region", [P, 2 * T * E0 * P // 2])

        def part_of(at, size, pattern, dt=F32, **dims):
            return region[:, at:at + size].bitcast(dt).rearrange(pattern, **dims)

        stc = sb("stc", [J, B, 6])
        mvc = sb("mvc", [J, B, 2])
        rstdc = sb("rstdc", [J, B])
        zc = sb("zc", [J, B, P])
        xnT = sb("xnT", [P, BJ])
        scl = sb("scl", [P, PAIRS, B])
        kT = sb("kT", [P, PAIRS, B, J])
        wks = sb("wks", [P, H])
        cr = sb("cr", [H, 3, B, J])
        crp = sb("crp", [H, 3, B, J], BF16)
        crow = sb("crow", [3, B, H, J], BF16)
        vmain = part_of(0, PAIRS * B * P, "p (c b k) -> p c b k", c=PAIRS, b=B)
        vrem = part_of(PAIRS * B * P, 2 * B * 5 * RG, "p (q b k) -> p q b k", q=2, b=B)
        M = sb("M", [P, B, H, J])
        U = sb("U", [P, B, NC, P])
        mx1 = sb("mx1", [P, 2, H])
        sm1 = sb("sm1", [P, 2, H])
        rc1 = sb("rc1", [P, 2, H])
        pe_ = part_of(0, 2 * H * J, "p (s h j) -> p s h j", s=2, h=H)
        pn = part_of(2 * H * J, 2 * H * J, "p (s k) -> p s k", s=2)
        pT = part_of(4 * H * J, 2 * NC * P, "p (s c q) -> p s c q", s=2, c=NC)
        lg = sb("lg", [P, T, E0])
        pr = sb("pr", [P, T, E0])
        sm8 = sb("sm8", [P, 3, T])
        prr = sb("prr", [P, 2, T, E0])
        prp = sb("prp", [P, T, E0, 3], BF16)
        zr = wqT
        zp = sb("zp", [P, 3, T, P], BF16)
        cand = sb("cand", [P, NM, E0], I32)
        best = sb("best", [P, 2, NM + 1, E0])
        cmp = sb("cmp", [P, NM, T, E0], BF16)
        ge = sb("ge", [P, 2, T, E0], BF16)
        need = sb("need", [P, E0])
        ceq = sb("ceq", [P, T, E0])
        q1 = sb("q1", [P, T, E0])
        q2 = sb("q2", [P, T, E0])
        slot = sb("slot", [P, T, E0])
        S = part_of(0, T * E0 * P // 2, "p (t e s) -> p t e s", BF16, t=T, e=E0)
        ST = part_of(T * E0 * P // 2, T * E0 * P // 2, "p (t e s) -> p t e s", BF16, t=T, e=E0)
        xin = wv[:].rearrange("p (e s) -> p e s", e=E0)
        pv = sb("pv", [P, E0])
        hg = wk[:].rearrange("p (s f q) -> p s f q", s=2, f=FC)
        y1 = sb("y1", [P, P])
        y2 = sb("y2", [P, P])
        y3 = sb("y3", [P, P])
        yp = sb("yp", [P, 2, 3, P], BF16)
        k1T = sb("k1T", [P, BJ])
        c1 = sb("c1", [1, BJ])
        M1 = sb("M1", [P, BJ])
        v1 = sb("v1", [J, B, P])
        p1 = sb("p1", [P, B, TB, J])
        p1T = sb("p1T", [J, B, TB * P])
        sm4 = sb("sm4", [P, B, 3, TB])
        sc = sb("sc", [P, B, TB, E1])
        sf = sb("sf", [P, TB, E1])
        a4 = sb("a4", [P, 2, TB, NG, 4])
        a2 = sb("a2", [P, 4, TB, NG, 2])
        a1 = sb("a1", [P, 4, TB, NG])
        gg = sb("gg", [P, 2, TB, NG, NG])
        gm = sb("gm", [P, 2, TB, NG])
        top8 = sb("top8", [P, TB, 8])
        r1 = sb("r1", [P, TB, E1])
        r2 = sb("r2", [P, TB, E1])
        r3 = sb("r3", [P, TB, E1])
        n4 = sb("n4", [P, 2, TB])
        wp = sb("wp", [P, TB, 3, E1], BF16)
        wT = sb("wT", [3 * E1, N], BF16)
        W = TB * P
        hu = part_of(0, NHU * W, "p (s q) -> p s q", s=NHU)
        hw = part_of(NHU * W, NHW * W, "p (s q) -> p s q", s=NHW)
        sg = part_of((NHU + NHW) * W, 2 * W, "p (s q) -> p s q", s=2)
        yT = region[:, (NHU + NHW + 2) * W:(NHU + NHW + 3) * W]

        ld = {k: sem("ld_" + k) for k in ("x", "ctx", "ctx_t", "cols", "fp", "fh", "row", "wk", "wv", "wq", "wo",
                                          "l1w", "w1", "w2", "b2", "gate", "up", "down")}
        pool_step = sem("pool_step")
        consts_ready = sem("consts_ready")
        moe_consts_ready = sem("moe_consts_ready")
        dve_step = sem("dve_step")
        act_step = sem("act_step")
        ctx_stats = sem("ctx_stats")
        ctx_rstd = sem("ctx_rstd")
        ln_stats = sem("ln_stats")
        ln_rstd = sem("ln_rstd")
        z_ready = sem("z_ready")
        fexp_done = sem("fexp_done")
        zc_ready = sem("zc_ready")
        zcT_done = sem("zcT_done")
        scl_ready = sem("scl_ready")
        xnT_ready = sem("xnT_ready")
        k_done = sem("k_done")
        kT_ready = sem("kT_ready")
        v_done = sem("v_done")
        vmain_ready = sem("vmain_ready")
        vrem_ready = sem("vrem_ready")
        vzero = sem("vzero")
        wks_ready = sem("wks_ready")
        ks_done = sem("ks_done")
        ks_read = sem("ks_read")
        crp_ready = sem("crp_ready")
        crow_ready = sem("crow_ready")
        zT_done = sem("zT_done")
        zT_ready = sem("zT_ready")
        m_done = sem("m_done")
        m_even = sem("m_even")
        m_odd = sem("m_odd")
        u_done = sem("u_done")
        u_main = sem("u_main")
        u_rem = sem("u_rem")
        s_done = sem("s_done")
        sub_done = sem("sub_done")
        exp_done = sem("exp_done")
        rc_ready = sem("rc_ready")
        nrm_done = sem("nrm_done")
        t_done = sem("t_done")
        pT_ready = sem("pT_ready")
        pv_done = sem("pv_done")
        x1_ready = sem("x1_ready")
        l1k_done = sem("l1k_done")
        l1k_ready = sem("l1k_ready")
        l1v_done = sem("l1v_done")
        l1v_ready = sem("l1v_ready")
        l1m_done = sem("l1m_done")
        l1m_ready = sem("l1m_ready")
        lg_done = sem("lg_done")
        lgs_ready = sem("lgs_ready")
        lge_ready = sem("lge_ready")
        pr_ready = sem("pr_ready")
        zp_ready = sem("zp_ready")
        prp_ready = sem("prp_ready")
        cmp_ready = sem("cmp_ready")
        cnt_done = sem("cnt_done")
        ge_ready = sem("ge_ready")
        rank_done = sem("rank_done")
        S_ready = sem("S_ready")
        st_done = sem("st_done")
        ST_ready = sem("ST_ready")
        gather_done = sem("gather_done")
        xin_ready = sem("xin_ready")
        pv_sum = sem("pv_sum")
        h_done = sem("h_done")
        hg_ready = sem("hg_ready")
        y_done = sem("y_done")
        yp_ready = sem("yp_ready")
        sc_done = sem("sc_done")
        x2_ready = sem("x2_ready")
        s1_done = sem("s1_done")
        p1s_ready = sem("p1s_ready")
        p1_ready = sem("p1_ready")
        p1T_done = sem("p1T_done")
        p1T_ready = sem("p1T_ready")
        pv1_done = sem("pv1_done")
        x3_ready = sem("x3_ready")
        rl_done = sem("rl_done")
        sig_ready = sem("sig_ready")
        wp_ready = sem("wp_ready")
        wt_done = sem("wt_done")
        wT_ready = sem("wT_ready")
        g_done = sem("g_done")
        u1_done = sem("u1_done")
        wb_done = sem("wb_done")
        sg_ready = sem("sg_ready")
        hu_ready = sem("hu_ready")
        hw_ready = sem("hw_ready")
        dn_done = sem("dn_done")
        yT_ready = sem("yT_ready")
        yt_done = sem("yt_done")
        yo_ready = sem("yo_ready")
        stored = sem("stored")

        block = es.enter_context(nc.Block())

        @block.sync
        def _(sp):
            sp.dma_start(c_nat[:], ctx.rearrange("b j d -> j b d")).then_inc(ld["ctx"], 16)
            sp.dma_start(cl[:], cols).then_inc(ld["cols"], 16)
            sp.dma_start(fp[:], f_pair).then_inc(ld["fp"], 16)
            sp.dma_start(xs[:], x).then_inc(ld["x"], 16)
            sp.dma_start(wqT[:], wq_t.rearrange("(c p) d -> p c d", p=P)).then_inc(ld["wq"], 16)
            sp.dma_start(fh[:], f_head).then_inc(ld["fh"], 16)
            sp.dma_start(cT[:], ctx_t).then_inc(ld["ctx_t"], 16)
            sp.dma_start(lw[:], l1w).then_inc(ld["l1w"], 16)
            sp.wait_ge(crp_ready, 1)
            for part in range(3):
                for b in range(B):
                    sp.dma_start(crow[part:part + 1, b, :, :], crp[:, part, b, :]).then_inc(crow_ready, 16)
            sp.dma_start(rw[:], row.broadcast_to([P, E0 + P + E1])).then_inc(ld["row"], 16)
            sp.dma_start(w1s[:], w1.rearrange("p (e f) -> p e f", e=E0)).then_inc(ld["w1"], 16)
            sp.dma_start(w2s[:], w2.rearrange("p (e c d) -> p e c d", e=E0, c=FC)).then_inc(ld["w2"], 16)
            sp.dma_start(b2s[:].rearrange("p e d -> p (e d)"), b2.broadcast_to([P, E0 * P])).then_inc(ld["b2"], 16)
            sp.dma_start(gs[:], gate).then_inc(ld["gate"], 16)
            sp.dma_start(us[:], up).then_inc(ld["up"], 16)
            sp.dma_start(dn[:], down).then_inc(ld["down"], 16)
            for b in range(B):
                sp.wait_ge(yo_ready, b + 1)
                sp.dma_start(out[b].rearrange("(t p) d -> p t d", p=P), xs[:, TB * b:TB * b + TB, :])\
                  .then_inc(stored, 16)
            sp.wait_ge(stored, 16 * B)

        @block.gpsimd
        def _(pool):
            steps = [0]

            def link(ins):
                steps[0] += 1
                ins.then_inc(pool_step, 1)
                pool.wait_ge(pool_step, steps[0])

            g = nc.gpsimd
            link(g.memset(ident[:], 0.0))
            link(g.affine_select(out=ident[:], in_=ident[:], compare_op=ALU.not_equal, fill=1.0, base=0,
                                 pattern=[[-1, P]], channel_multiplier=1))
            link(g.memset(pair_sel[:], 1.0))
            link(g.affine_select(out=pair_sel[:], in_=pair_sel[:], compare_op=ALU.is_ge, fill=0.0, base=0,
                                 pattern=[[1, P]], channel_multiplier=-DH))
            link(g.affine_select(out=pair_sel[:], in_=pair_sel[:], compare_op=ALU.is_ge, fill=0.0, base=DH - 1,
                                 pattern=[[-1, P]], channel_multiplier=DH))
            link(g.memset(neghalf[:], -0.5))
            g.tensor_copy(ident16[:], ident[:])
            g.memset(ones_row[:], 1.0)
            g.memset(ones16[:], 1.0).then_inc(consts_ready, 1)

            pool.wait_ge(ctx_stats, 1)
            link(g.tensor_scalar(rstdc[:], mvc[:, :, 1], EPS, None, ALU.add))
            g.tensor_tensor(rstdc[:], rstdc[:], neghalf[0:J, 0:B], ALU.pow).then_inc(ctx_rstd, 1)
            g.memset(vmain, 0.0)

            def ln(a, b, count):
                pool.wait_ge(ln_stats, count)
                link(g.tensor_scalar(veps[:, a:b], mv[:, a:b, 1], EPS, None, ALU.add))
                return g.tensor_tensor(rstd[:, a:b], veps[:, a:b], neghalf[:, a:b], ALU.pow)

            link(ln(0, T, 1))
            link(g.tensor_tensor(rsq[:], rstd[:], rstd[:], ALU.mult))
            link(g.tensor_tensor(rsq[:], rsq[:], mv[:, :, 1], ALU.mult))
            link(g.tensor_scalar(rsq[:], rsq[:], EPS, None, ALU.add))
            link(g.tensor_tensor(rstd2[:], rsq[:], neghalf[:], ALU.pow))
            g.tensor_tensor(rstd[:], rstd[:], rstd2[:], ALU.mult).then_inc(ln_rstd, 1)
            g.memset(vrem, 0.0).then_inc(vzero, 1)

            link(g.memset(tri16[:], 1.0))
            g.affine_select(out=tri16[:], in_=tri16[:], compare_op=ALU.is_ge, fill=0.0, base=0,
                            pattern=[[1, P]], channel_multiplier=-1)
            g.iota(slot_no[:], [[1, P]], base=1, channel_multiplier=0, allow_small_or_imprecise_dtypes=True)
            g.iota(digit_i[:], [[1, NM]], base=1, channel_multiplier=0)
            link(g.memset(earlier[:], 1.0))
            g.affine_select(out=earlier[:], in_=earlier[:], compare_op=ALU.is_gt, fill=0.0, base=0,
                            pattern=[[1, NG], [-1, NG]], channel_multiplier=0)
            link(g.memset(scan_keep[:], 1.0))
            link(g.memset(scan_keep[:, :, 0:1], 0.0))
            link(g.memset(esel[:], 1.0))
            for part in range(3):
                e = esel[part * E1:(part + 1) * E1, :]
                link(g.affine_select(out=e, in_=e, compare_op=ALU.is_ge, fill=0.0, base=0,
                                     pattern=[[1, CH * P]], channel_multiplier=-I1))
                link(g.affine_select(out=e, in_=e, compare_op=ALU.is_ge, fill=0.0, base=I1 - 1,
                                     pattern=[[-1, CH * P]], channel_multiplier=I1))
            g.memset(veps[:], 0.0).then_inc(moe_consts_ready, 1)

            for i in range(T):
                s = i % 2
                pool.wait_ge(rc_ready, i + 1)
                pool.wait_ge(exp_done, 2 * i + 2)
                if i >= 2:
                    pool.wait_ge(t_done, 3 * (i - 1))
                for j0, nj, at in ((0, JM, 0), (JM, JR, H * JM)):
                    ins = g.tensor_tensor(pn[:, s, at:at + H * nj].rearrange("p (h j) -> p h j", h=H),
                                          pe_[:, s, :, j0:j0 + nj],
                                          rc1[:, s].unsqueeze(2).broadcast_to([P, H, nj]), ALU.mult)
                ins.then_inc(nrm_done, 1)
            ln(0, T, 2).then_inc(ln_rstd, 1)

            pool.wait_ge(z_ready, 2 * T)
            for part in range(2):
                src = z if part == 0 else zr
                link(g.tensor_copy(zp[:, part], src[:]))
                link(g.tensor_tensor(zr[:], src[:], zp[:, part], ALU.subtract))
            g.tensor_copy(zp[:, 2], zr[:]).then_inc(zp_ready, 1)
            pool.wait_ge(pr_ready, 1)
            for part in range(2):
                src = pr[:] if part == 0 else prr[:, 0]
                link(g.tensor_copy(prp[:, :, :, part], src))
                link(g.tensor_tensor(prr[:, 0], src, prp[:, :, :, part], ALU.subtract))
            g.tensor_copy(prp[:, :, :, 2], prr[:, 0]).then_inc(prp_ready, 1)

            for k in range(2):
                for b in range(B):
                    ln(TB * b, TB * b + TB, 3 + 2 * k + b).then_inc(ln_rstd, 1)

        @block.scalar
        def _(act):
            a = nc.scalar
            act.dma_start(wk[:], w_kv[:, 0:H * DH]).then_inc(ld["wk"], 16)
            act.dma_start(wv[:], w_kv[:, H * DH:2 * H * DH]).then_inc(ld["wv"], 16)
            act.dma_start(wo[:], w_out.rearrange("(c p) d -> p c d", p=P)).then_inc(ld["wo"], 16)

            act.wait_ge(vzero, 1)
            for k in range(4):
                act.wait_ge(v_done, k + 1)
                for h2 in range(2):
                    r = slice(DH * h2, DH * h2 + DH)
                    src = ps[r, 3 + k, 0:2 * BJ].rearrange("p (c b j) -> p c b j", c=2, b=B)
                    ins = a.activation(vmain[r, 2 * k:2 * k + 2, :, JM * h2:JM * h2 + JM], src[:, :, :, 0:JM], ACT.Copy)
                ins.then_inc(vmain_ready, 1)
            act.wait_ge(ld["cols"], 16)
            for half in range(2):
                act.wait_ge(zT_done, half + 1)
                a.activation(zT[:, 512 * half:512 * half + 512], bank(7), ACT.Identity, bias=cl[:, 3:4],
                             scale=cl[:, 2:3]).then_inc(zT_ready, 1)
            for k in range(3):
                act.wait_ge(m_done, 2 * k + 1)
                nh = min(3, 8 - 3 * k)
                for b in range(B):
                    src = bank(k, 0, nh * BJ).rearrange("p (h b j) -> p h b j", h=nh, b=B)
                    ins = a.activation(M[:, b, 6 * k:6 * k + 2 * nh:2, :], src[:, :, b, :], ACT.Copy)
                ins.then_inc(m_even, 1)
            for b in range(B):
                for half in range(2):
                    act.wait_ge(u_done, 2 * b + half + 1)
                    a.activation(U[:, b, 4 * half:4 * half + 4, :],
                                 bank([6, 7, 3, 4][2 * b + half]).rearrange("p (c d) -> p c d", c=4), ACT.Copy)\
                     .then_inc(u_main, 1)

            def exps(i):
                s = i % 2
                act.wait_ge(sub_done, 2 * i + 1)
                a.activation(pe_[:, s, 0:12, :], pe_[:, s, 0:12, :], ACT.Exp).then_inc(exp_done, 1)
                act.wait_ge(sub_done, 2 * i + 2)
                a.activation(pe_[:, s, 12:16, :], pe_[:, s, 12:16, :], ACT.Exp).then_inc(exp_done, 1)

            def evac(i):
                s = i % 2
                if i >= 2:
                    act.wait_ge(pv_done, i - 1)
                for k in range(3):
                    act.wait_ge(t_done, 3 * i + k + 1)
                    if k < 2:
                        a.activation(pT[:, s, 4 * k:4 * k + 4, :], bank(3 + k).rearrange("p (c q) -> p c q", c=4),
                                     ACT.Copy).then_inc(pT_ready, 1)
                    else:
                        a.activation(pT[0:RG, s, 8:10, :],
                                     bank(5, 0, 256, RG).rearrange("p (c q) -> p c q", c=2),
                                     ACT.Copy).then_inc(pT_ready, 1)

            for i in range(T + 2):
                if i >= 2:
                    evac(i - 2)
                if i < T:
                    exps(i)

            def zcopy(half, k):
                act.wait_ge(zT_done, 2 * k + half + 1)
                a.activation(zT[:, 512 * half:512 * half + 512], bank(half), ACT.Copy).then_inc(zT_ready, 1)

            for half in range(2):
                zcopy(half, 1)
            act.wait_ge(lgs_ready, 1)
            a.activation(lg[:], lg[:], ACT.Exp).then_inc(lge_ready, 1)
            for t in range(T):
                act.wait_ge(st_done, t + 1)
                a.activation(ST[:, t].rearrange("p e s -> p (e s)"), bank16(3 + t % 2), ACT.Copy)\
                 .then_inc(ST_ready, 1)
            act.wait_ge(gather_done, 1)
            for half in range(2):
                a.activation(xin[:, 4 * half:4 * half + 4, :], bank(half).rearrange("p (e s) -> p e s", e=4),
                             ACT.Copy).then_inc(xin_ready, 1)
            for e in range(E0):
                act.wait_ge(h_done, e + 1)
                if e >= 2:
                    act.wait_ge(y_done, e - 1)
                for f in range(FC):
                    ins = a.activation(hg[:, e % 2, f, :], bank(5 + e % 2, P * f, P), ACT.Gelu_apprx_tanh,
                                       bias=cl[:, 6 + FC * e + f:7 + FC * e + f])
                ins.then_inc(hg_ready, 1)

            for b in range(B):
                zcopy(b, 2)
            for b in range(B):
                act.wait_ge(p1s_ready, b + 1)
                a.activation(p1[:, b], p1[:, b], ACT.Exp).then_inc(p1_ready, 1)
            for b in range(B):
                act.wait_ge(p1T_done, b + 1)
                a.activation(p1T[:, b], bank(3 + 3 * b, 0, TB * P, J), ACT.Copy).then_inc(p1T_ready, 1)
            for b in range(B):
                zcopy(b, 3)
            for b in range(B):
                act.wait_ge(rl_done, b + 1)
                a.activation(sc[:, b], bank(7, TB * E1 * b, TB * E1).rearrange("p (t e) -> p t e", t=TB), ACT.Sigmoid)\
                 .then_inc(sig_ready, 1)

            def weights_copy(b):
                act.wait_ge(wt_done, b + 1)
                a.activation(wT[:, 512 * b:512 * b + 512], bank16(7)[0:3 * E1, 512:1024], ACT.Copy)\
                 .then_inc(wT_ready, 1)

            for n in range(B * CHS):
                if n in (LEAD, CHS):
                    weights_copy(int(n == CHS))
                act.wait_ge(g_done, n + 1)
                if n >= 2:
                    act.wait_ge(hu_ready, n - 1)
                a.activation(sg[:, n % 2, :], bank(n % 2), ACT.Silu).then_inc(sg_ready, 1)

        @block.tensor
        def _(pe):
            mm = nc.tensor.matmul
            tr = nc.tensor.transpose
            pe.wait_ge(consts_ready, 1)
            pe.wait_ge(ld["fp"], 16)
            mm(bank(7, 0, 16), pair_sel[:], fp[:], start=True, stop=True).then_inc(fexp_done, 1)
            pe.wait_ge(zc_ready, 1)
            pe.wait_ge(scl_ready, 1)
            for b in range(B):
                ins = tr(bank(7, 64 + J * b, J), zc[:, b, :], ident[0:J, 0:J])
            ins.then_inc(zcT_done, 1)
            pe.wait_ge(xnT_ready, 1)
            pe.wait_ge(ld["wk"], 16)
            for k in range(3):
                for c in range(3 * k, min(3 * k + 3, PAIRS)):
                    ins = mm(bank(k, BJ * (c - 3 * k), BJ), wk[:, P * c:P * c + P], xnT[:], start=True, stop=True)
                ins.then_inc(k_done, 1)
            pe.wait_ge(wks_ready, 1)
            mm(bank(7, 0, BJ, H), wks[:], xnT[:], start=True, stop=True).then_inc(ks_done, 1)
            pe.wait_ge(ld["wv"], 16)
            for k in range(4):
                for c in range(2 * k, 2 * k + 2):
                    ins = mm(bank(3 + k, BJ * (c - 2 * k), BJ), wv[:, P * c:P * c + P], xnT[:], start=True, stop=True)
                ins.then_inc(v_done, 1)

            def trans_half(half, b, count):
                pe.wait_ge(z_ready, count)
                for t in range(4):
                    ins = tr(bank(b, P * t, P), z[:, 4 * half + t, :], ident[:])
                ins.then_inc(zT_done, 1)

            pe.wait_ge(ks_read, 1)
            trans_half(0, 7, 4)
            pe.wait_ge(zT_ready, 1)
            trans_half(1, 7, 8)
            pe.wait_ge(kT_ready, 3)
            pe.wait_ge(ld["wq"], 16)
            for k in range(3):
                for h2 in range(2):
                    if h2 == 1:
                        pe.wait_ge(vmain_ready, k + 1)
                        pe.wait_ge(vrem_ready, k + 1)
                    r = slice(DH * h2, DH * h2 + DH)
                    for c in range(3 * k, min(3 * k + 3, PAIRS)):
                        ins = mm(bank(3 * h2 + k, BJ * (c - 3 * k), BJ), wqT[r, c, :],
                                 kT[r, c].rearrange("p b j -> p (b j)"), start=True, stop=True)
                    ins.then_inc(m_done, 1)
            pe.wait_ge(ld["wo"], 16)
            pe.wait_ge(vmain_ready, 4)
            pe.wait_ge(vrem_ready, 4)
            pe.wait_ge(zT_ready, 2)
            for b in range(B):
                for half in range(2):
                    if b == 1:
                        pe.wait_ge(m_odd, half + 1)
                    for c in range(4):
                        p = 4 * half + c
                        ins = mm(bank([6, 7, 3, 4][2 * b + half], P * c, P), vmain[:, p, b, :], wo[:, p, :],
                                 start=True, stop=True)
                    ins.then_inc(u_done, 1)
            pe.wait_ge(m_odd, 3)
            for b in range(B):
                for q in range(2):
                    for c in range(4):
                        ins = mm(bank(5, P * (2 * b + q), P, RG), vrem[:, q, b, RG * c:RG * c + RG], wo[:, 4 * q + c, :],
                                 start=(c == 0), stop=(c == 3))
            ins.then_inc(u_done, 1)

            pe.wait_ge(m_even, 3)
            pe.wait_ge(crow_ready, 16 * 6)

            def scores(i):
                b = i // TB
                if i > 0:
                    pe.wait_ge(sub_done, 2 * i)
                h0 = 0
                for k, nh in enumerate(HB):
                    mm(bank(k, 0, nh * J), zT[:, P * i:P * i + P], M[:, b, h0:h0 + nh, :].rearrange("p h j -> p (h j)"),
                       start=True, stop=False)
                    ins = mm(bank(k, 0, nh * J), ones16[0:3, :],
                             crow[:, b, h0:h0 + nh, :].rearrange("p h j -> p (h j)"), start=False, stop=True)
                    if k >= 1:
                        ins.then_inc(s_done, 1)
                    h0 += nh

            def turn(i):
                s = i % 2
                pe.wait_ge(nrm_done, i + 1)
                if i == 0:
                    pe.wait_ge(u_main, 4)
                    pe.wait_ge(u_rem, 1)
                else:
                    pe.wait_ge(pT_ready, 3 * i)
                for k in range(3):
                    for c in range(4 * k, min(4 * k + 4, NC)):
                        if c < PAIRS:
                            ins = tr(bank(3 + k, P * (c % 4), P), pn[:, s, P * c:P * c + P], ident[:])
                        else:
                            q = c - PAIRS
                            ins = tr(bank(5, P * q, P, RG), pn[:, s, H * JM + RG * q:H * JM + RG * q + RG], ident[:])
                    ins.then_inc(t_done, 1)

            def attend(i):
                s, b = i % 2, i // TB
                if i >= 2:
                    pe.wait_ge(x1_ready, i - 1)
                for c in range(NC):
                    if c % 4 == 0:
                        pe.wait_ge(pT_ready, 3 * i + c // 4 + 1)
                    r = P if c < PAIRS else RG
                    ins = mm(bank(6 + s, 0, P), pT[0:r, s, c, :], U[0:r, b, c, :], start=(c == 0), stop=(c == NC - 1))
                ins.then_inc(pv_done, 1)

            for i in range(T + 2):
                if i < T:
                    scores(i)
                if i >= 2:
                    turn(i - 2)
                    attend(i - 2)

            pe.wait_ge(ld["l1w"], 16)
            pe.wait_ge(ld["ctx_t"], 16)
            mm(bank(3, 0, BJ), l1kT, cT[:], start=True, stop=True).then_inc(l1k_done, 1)
            for b in range(B):
                ins = mm(bank(4, P * b, P, J), cT[:, J * b:J * b + J], l1vT, start=True, stop=True)
            ins.then_inc(l1v_done, 1)
            pe.wait_ge(l1k_ready, 1)
            mm(bank(5, 0, BJ), l1q, k1T[:], start=True, stop=True)
            mm(bank(5, 256, BJ, 1), cl[:, 4:5], k1T[:], start=True, stop=True).then_inc(l1m_done, 1)

            for half in range(2):
                trans_half(half, half, T + 4 * half + 4)
            pe.wait_ge(zT_ready, 4)
            for t in range(T):
                ins = mm(bank(2, E0 * t, E0), zT[:, P * t:P * t + P], rwS, start=True, stop=True)
            ins.then_inc(lg_done, 1)
            for k in range(SEARCH):
                pe.wait_ge(cmp_ready, k + 1)
                for t in range(T):
                    ins = mm(bank(7, 0, NM * E0), ones16[:], cmp[:, :, t, :], start=(t == 0), stop=(t == T - 1))
                ins.then_inc(cnt_done, 1)
            pe.wait_ge(ge_ready, 1)
            rank = bank(6, 0, 2 * T * E0).rearrange("p (g t e) -> p g t e", g=2, t=T)
            mm(rank, tri16[:], ge[:], start=True, stop=False, skip_group_check=True)
            for k in range(T - 1):
                for w in range(2):
                    mm(rank[:, w, k + 1:T, :], ones16[:],
                       ge[:, w, k, :].unsqueeze(1).broadcast_to([P, T - 1 - k, E0]),
                       start=False, stop=(k == T - 2), skip_group_check=True)
            for t in range(T):
                ins = mm(bank(7, 64, E0), ones16[:], ge[:, 0, t, :], start=(t == 0), stop=(t == T - 1))
            ins.then_inc(rank_done, 1)
            pe.wait_ge(zp_ready, 1)
            pe.wait_ge(prp_ready, 1)
            for t in range(T):
                pe.wait_ge(S_ready, t + 1)
                for half in range(2):
                    for part in range(3):
                        ins = mm(bank(half), zp[:, part, t, :],
                                 S[:, t, 4 * half:4 * half + 4, :].rearrange("p e s -> p (e s)"),
                                 start=(t == 0 and part == 0), stop=(t == T - 1 and part == 2))
                for e in range(E0):
                    ins = mm(bank(2, 3 * e, 3), S[:, t, e, :], prp[:, t, e, :], start=(t == 0 and e == 0),
                             stop=(t == T - 1), skip_group_check=True)
                if t == T - 1:
                    ins.then_inc(gather_done, 1)
                if t >= 2:
                    pe.wait_ge(ST_ready, t - 1)
                for e in range(E0):
                    ins = tr(bank16(3 + t % 2)[:, P * e:P * e + P], S[:, t, e, :], ident16[:])
                ins.then_inc(st_done, 1)

            def expert_h(e):
                if e == 0:
                    pe.wait_ge(ld["w1"], 16)
                pe.wait_ge(xin_ready, e // 4 + 1)
                if e >= 2:
                    pe.wait_ge(hg_ready, e - 1)
                for f in range(FC):
                    ins = mm(bank(5 + e % 2, P * f, P), w1s[:, e, P * f:P * f + P], xin[:, e, :], start=True, stop=True)
                ins.then_inc(h_done, 1)

            def expert_y(e):
                if e == 0:
                    pe.wait_ge(ld["w2"], 16)
                pe.wait_ge(hg_ready, e + 1)
                if e >= 1:
                    pe.wait_ge(yp_ready, e)
                for f in range(FC):
                    ins = mm(bank(7, 128, P), hg[:, e % 2, f, :], w2s[:, e, f, :], start=(f == 0), stop=(f == FC - 1))
                ins.then_inc(y_done, 1)

            def scatter(e):
                pe.wait_ge(yp_ready, e + 1)
                if e == 0:
                    pe.wait_ge(ST_ready, T)
                for t in range(T):
                    for part in range(3):
                        ins = mm(bank(3 + t // 4, P * (t % 4), P), ST[:, t, e, :], yp[:, e % 2, part, :],
                                 start=(e == 0 and part == 0 and t % 4 == 0), stop=(e == E0 - 1),
                                 skip_group_check=True)
                    if t % 4 == 3:
                        ins.then_inc(sc_done, 1)

            expert_h(0)
            for e in range(E0):
                if e + 1 < E0:
                    expert_h(e + 1)
                expert_y(e)
                if e > 0:
                    scatter(e - 1)
            scatter(E0 - 1)

            pe.wait_ge(l1m_ready, 1)
            pe.wait_ge(l1v_ready, 1)
            pe.wait_ge(x2_ready, 1)
            for b in range(B):
                trans_half(b, b, 2 * T + 4 * b + 4)
            for b in range(B):
                pe.wait_ge(zT_ready, 5 + b)
                for t in range(TB):
                    mm(bank(2 + 2 * b, J * t, J), zT[:, P * (TB * b + t):P * (TB * b + t) + P], M1[:, J * b:J * b + J],
                       start=True, stop=False)
                    ins = mm(bank(2 + 2 * b, J * t, J), ones_row[:], c1[:, J * b:J * b + J], start=False, stop=True)
                ins.then_inc(s1_done, 1)
            for b in range(B):
                pe.wait_ge(p1_ready, b + 1)
                for t in range(TB):
                    ins = tr(bank(3 + 3 * b, P * t, P, J), p1[:, b, t, :], ident[:])
                ins.then_inc(p1T_done, 1)
            for b in range(B):
                pe.wait_ge(p1T_ready, b + 1)
                for t in range(TB):
                    ins = mm(bank(5 + 2 * b, P * t, P), p1T[:, b, P * t:P * t + P], v1[:, b, :], start=True, stop=True)
                ins.then_inc(pv1_done, 1)

            for b in range(B):
                trans_half(b, b, 3 * T + 4 * b + 4)
            pe.wait_ge(zT_ready, 8)
            pe.wait_ge(ld["gate"], 16)
            pe.wait_ge(ld["up"], 16)
            pe.wait_ge(ld["down"], 16)
            pe.wait_ge(moe_consts_ready, 1)

            for b in range(B):
                if b == 1:
                    pe.wait_ge(sig_ready, 1)
                for t in range(TB):
                    q = TB * b + t
                    ins = mm(bank(7, E1 * q, E1), zT[:, P * q:P * q + P], rwT, start=True, stop=True)
                ins.then_inc(rl_done, 1)
            pe.wait_ge(sig_ready, 2)

            def weights(b):
                pe.wait_ge(wp_ready, b + 1)
                for t in range(TB):
                    ins = tr(bank16(7)[0:3 * E1, 512 + P * t:512 + P * t + P],
                             wp[:, t].rearrange("p a e -> p (a e)"), ident16[:])
                ins.then_inc(wt_done, 1)

            def gate_up(n):
                b, c = divmod(n, CHS)
                zb = zT[:, 512 * b:512 * b + 512]
                if n >= 2:
                    pe.wait_ge(sg_ready, n - 1)
                mm(bank(n % 2), gs[:, P * c:P * c + P], zb, start=True, stop=True).then_inc(g_done, 1)
                if n >= 2:
                    pe.wait_ge(hu_ready, n - 1)
                mm(bank(2 + n % 2), us[:, P * c:P * c + P], zb, start=True, stop=True).then_inc(u1_done, 1)

            def spread(n):
                b, c = divmod(n, CHS)
                if c == CH:
                    return
                m = CH * b + c
                if m >= 2:
                    pe.wait_ge(hw_ready, m - 1)
                pe.wait_ge(wT_ready, b + 1)
                mm(bank(4 + m % 2), esel[:, P * c:P * c + P], wT[:, 512 * b:512 * b + 512], start=True, stop=True)\
                    .then_inc(wb_done, 1)

            def down_mm(n):
                b, c = divmod(n, CHS)
                if c < CH:
                    pe.wait_ge(hw_ready, CH * b + c + 1)
                    rhs = hw[:, (CH * b + c) % NHW, :]
                else:
                    pe.wait_ge(hu_ready, n + 1)
                    rhs = hu[:, n % NHU, :]
                if c == 0 and b == 1:
                    pe.wait_ge(yT_ready, 1)
                mm(bank(6), dn[:, P * c:P * c + P], rhs, start=(c == 0), stop=(c == CH)).then_inc(dn_done, 1)

            def turn_back(b):
                pe.wait_ge(yT_ready, b + 1)
                pe.wait_ge(wT_ready, 2)
                for t in range(TB):
                    ins = tr(bank(7, P * t, P), yT[:, P * t:P * t + P], ident[:])
                ins.then_inc(yt_done, 1)

            for n in range(B * CHS + LEAD + 1):
                if n == CHS:
                    weights(1)
                if n < B * CHS:
                    gate_up(n)
                if n == LEAD - 1:
                    weights(0)
                if LEAD <= n < B * CHS + LEAD:
                    spread(n - LEAD)
                if n > LEAD:
                    down_mm(n - LEAD - 1)
                if n == CHS + LEAD + 2:
                    turn_back(0)
            turn_back(1)

        @block.vector
        def _(dve):
            v = nc.vector
            steps = [0]

            def link(ins):
                steps[0] += 1
                ins.then_inc(dve_step, 1)
                dve.wait_ge(dve_step, steps[0])

            def stats(t0, t1):
                for t in range(t0, t1):
                    ins = v.bn_stats(st[:, t, :], xs[:, t, :])
                link(ins)
                for t in range(t0, t1):
                    ins = v.bn_aggr(mv[:, t, :], st[:, t, :])
                return ins

            def norm(t0, t1, r):
                for t in range(t0, t1):
                    v.tensor_scalar(z[:, t, :], xs[:, t, :], mv[:, t, 0:1], r[:, t:t + 1], ALU.subtract, ALU.mult)\
                     .then_inc(z_ready, 1)

            dve.wait_ge(ld["ctx"], 16)
            for b in range(B):
                ins = v.bn_stats(stc[:, b, :], c_nat[:, b, :])
            link(ins)
            for b in range(B):
                ins = v.bn_aggr(mvc[:, b, :], stc[:, b, :])
            ins.then_inc(ctx_stats, 1)
            dve.wait_ge(ctx_rstd, 1)
            dve.wait_ge(ctx_stats, 1)
            for b in range(B):
                ins = v.tensor_scalar(zc[:, b, :], c_nat[:, b, :], mvc[:, b, 0:1], rstdc[:, b:b + 1], ALU.subtract,
                                      ALU.mult)
            ins.then_inc(zc_ready, 1)
            dve.wait_ge(fexp_done, 1)
            v.tensor_scalar(scl[:], bank(7, 0, 16).rearrange("p (c b) -> p c b", b=B), 1.0, DH ** -0.5, ALU.add,
                            ALU.mult).then_inc(scl_ready, 1)
            dve.wait_ge(ld["cols"], 16)
            dve.wait_ge(zcT_done, 1)
            v.tensor_scalar(xnT[:], bank(7, 64, BJ), cl[:, 0:1], cl[:, 1:2], ALU.mult, ALU.add).then_inc(xnT_ready, 1)
            dve.wait_ge(ld["x"], 16)
            stats(0, T).then_inc(ln_stats, 1)
            dve.wait_ge(ld["wk"], 16)
            v.tensor_reduce(wks[:], wk[:].rearrange("p (h d) -> p h d", h=H), X, ALU.add).then_inc(wks_ready, 1)
            dve.wait_ge(ks_done, 1)
            dve.wait_ge(ld["fh"], 16)
            for b in range(B):
                ins = v.tensor_scalar(cr[:, 0, b, :], bank(7, J * b, J, H), fh[:, b:b + 1], DH ** -0.5, ALU.mult,
                                      ALU.mult)
            ins.then_inc(ks_read, 1)
            dve.wait_ge(ln_rstd, 1)
            norm(0, T, rstd)
            dve.wait_ge(scl_ready, 1)
            for k in range(3):
                dve.wait_ge(k_done, k + 1)
                c0, c1_ = 3 * k, min(3 * k + 3, PAIRS)
                v.tensor_tensor(kT[:, c0:c1_], bank(k, 0, BJ * (c1_ - c0)).rearrange("p (c b j) -> p c b j", b=B, j=J),
                                scl[:, c0:c1_, :].unsqueeze(3).broadcast_to([P, c1_ - c0, B, J]), ALU.mult)\
                 .then_inc(kT_ready, 1)
            dve.wait_ge(ks_read, 1)
            for part in range(2):
                link(v.tensor_copy(crp[:, part], cr[:, part]))
                link(v.tensor_tensor(cr[:, part + 1], cr[:, part], crp[:, part], ALU.subtract))
            v.tensor_copy(crp[:, 2], cr[:, 2]).then_inc(crp_ready, 1)
            for k in range(4):
                dve.wait_ge(vmain_ready, k + 1)
                for h2 in range(2):
                    r = slice(DH * h2, DH * h2 + DH)
                    src = ps[r, 3 + k, 0:2 * BJ].rearrange("p (c b j) -> p c b j", c=2, b=B)
                    for c in range(2):
                        pp = (2 * k + c) % 4
                        at = RG * pp + 2 * JR * pp + JR * h2
                        ins = v.tensor_copy(vrem[r, k // 2, :, at:at + JR], src[:, c, :, JM:J])
                ins.then_inc(vrem_ready, 1)
            for k in range(3):
                dve.wait_ge(m_done, 2 * k + 2)
                nh = min(3, 8 - 3 * k)
                for b in range(B):
                    src = bank(3 + k, 0, nh * BJ).rearrange("p (h b j) -> p h b j", h=nh, b=B)
                    ins = v.tensor_copy(M[:, b, 6 * k + 1:6 * k + 2 * nh:2, :], src[:, :, b, :])
                ins.then_inc(m_odd, 1)
            dve.wait_ge(u_done, 5)
            v.tensor_copy(U[0:RG, :, 8:10, :], bank(5, 0, 512, RG).rearrange("p (b q d) -> p b q d", b=B, q=2))\
             .then_inc(u_rem, 1)

            SG = [(0, 12), (12, 16)]

            def sbank(g):
                if g == 0:
                    return ps[:, 0:2, 0:6 * J].rearrange("p k (h j) -> p k h j", j=J)
                return ps[:, 2:3, 0:4 * J].rearrange("p k (h j) -> p k h j", j=J)

            def submax(i):
                s = i % 2
                for g, (a, b) in enumerate(SG):
                    dve.wait_ge(s_done, 2 * i + g + 1)
                    k = 2 - g
                    link(v.tensor_reduce(mx1[:, s, a:b].rearrange("p (k h) -> p k h", k=k), sbank(g), X, ALU.max))
                    if i >= 2:
                        dve.wait_ge(nrm_done, i - 1)
                    h = (b - a) // k
                    v.tensor_tensor(pe_[:, s, a:b, :].rearrange("p (k h) j -> p k h j", k=k), sbank(g),
                                    mx1[:, s, a:b].rearrange("p (k h) -> p k h", k=k).unsqueeze(3)
                                    .broadcast_to([P, k, h, J]), ALU.subtract).then_inc(sub_done, 1)

            def sums(i):
                s = i % 2
                dve.wait_ge(exp_done, 2 * i + 2)
                link(v.tensor_reduce(sm1[:, s, :], pe_[:, s], X, ALU.add))
                v.reciprocal(rc1[:, s, :], sm1[:, s, :]).then_inc(rc_ready, 1)

            def resid(i):
                dve.wait_ge(pv_done, i + 1)
                v.tensor_tensor(xs[:, i, :], xs[:, i, :], bank(6 + i % 2, 0, P), ALU.add).then_inc(x1_ready, 1)
                if i > 0:
                    dve.wait_ge(x1_ready, i)
                    v.bn_stats(st[:, i - 1, :], xs[:, i - 1, :])

            for i in range(T + 3):
                if 1 <= i <= T:
                    sums(i - 1)
                if i < T:
                    submax(i)
                if i >= 3:
                    resid(i - 3)
            dve.wait_ge(x1_ready, T)
            link(v.bn_stats(st[:, T - 1, :], xs[:, T - 1, :]))
            for t in range(T):
                ins = v.bn_aggr(mv[:, t, :], st[:, t, :])
            ins.then_inc(ln_stats, 1)

            dve.wait_ge(l1k_done, 1)
            v.tensor_scalar(k1T[:], bank(3, 0, BJ), cl[:, 5:6], None, ALU.add).then_inc(l1k_ready, 1)
            dve.wait_ge(l1v_done, 1)
            dve.wait_ge(ld["row"], 16)
            v.tensor_tensor(v1[:], bank(4, 0, 2 * P, J).rearrange("p (b d) -> p b d", b=B),
                            bv_b[0:J].unsqueeze(1).broadcast_to([J, B, P]), ALU.add).then_inc(l1v_ready, 1)
            dve.wait_ge(l1m_done, 1)
            v.tensor_copy(c1[:], bank(5, 256, BJ, 1))
            v.tensor_copy(M1[:], bank(5, 0, BJ)).then_inc(l1m_ready, 1)

            dve.wait_ge(ln_rstd, 2)
            norm(0, T, rstd)
            dve.wait_ge(moe_consts_ready, 1)
            for k in range(SEARCH):
                ins = v.tensor_scalar(digits[:, k, :], digit_i[:], 3 * (SEARCH - 1 - k), None, ALU.logical_shift_left)
            link(ins)
            link(v.memset(best[:], 0.0))
            dve.wait_ge(lg_done, 1)
            bt = lambda a: a.unsqueeze(2).broadcast_to([P, T, E0])
            link(v.tensor_tensor(lg[:], bank(2, 0, T * E0).rearrange("p (t e) -> p t e", t=T),
                                 bs_b.unsqueeze(1).broadcast_to([P, T, E0]), ALU.add))
            link(v.tensor_reduce(sm8[:, 0, :], lg[:], X, ALU.max))
            v.tensor_tensor(lg[:], lg[:], bt(sm8[:, 0, :]), ALU.subtract).then_inc(lgs_ready, 1)
            dve.wait_ge(lge_ready, 1)
            link(v.tensor_reduce(sm8[:, 1, :], lg[:], X, ALU.add))
            link(v.reciprocal(sm8[:, 2, :], sm8[:, 1, :]))
            v.tensor_tensor(pr[:], lg[:], bt(sm8[:, 2, :]), ALU.mult).then_inc(pr_ready, 1)
            dve.wait_ge(pr_ready, 1)
            for k in range(SEARCH):
                cur, nxt = best[:, k % 2], best[:, (k + 1) % 2]
                link(v.tensor_tensor(cand[:], cur[:, 0, :].bitcast(I32).unsqueeze(1).broadcast_to([P, NM, E0]),
                                     digits[:, k, :].unsqueeze(2).broadcast_to([P, NM, E0]), ALU.bitwise_or))
                v.tensor_tensor(cmp[:], pr[:].unsqueeze(1).broadcast_to([P, NM, T, E0]),
                                cand[:].bitcast(F32).unsqueeze(2).broadcast_to([P, NM, T, E0]), ALU.is_ge)\
                 .then_inc(cmp_ready, 1)
                dve.wait_ge(cnt_done, k + 1)
                link(v.scalar_tensor_tensor(out=cur[:, 1:NM + 1, :],
                                            in0=bank(7, 0, NM * E0).rearrange("p (m e) -> p m e", m=NM),
                                            scalar=float(CAP), in1=cand[:].bitcast(F32), op0=ALU.is_ge, op1=ALU.mult))
                link(v.tensor_reduce(nxt[:, 0, :], cur.rearrange("p m e -> p e m"), X, ALU.max))
            thr = best[:, SEARCH % 2, 0, :].unsqueeze(1).broadcast_to([P, T, E0])
            v.tensor_tensor(ge[:, 0], pr[:], thr, ALU.is_gt)
            v.tensor_tensor(ge[:, 1], pr[:], thr, ALU.is_equal).then_inc(ge_ready, 1)
            dve.wait_ge(rank_done, 1)
            dve.wait_ge(ge_ready, 1)
            rank = bank(6, 0, 2 * T * E0).rearrange("p (g t e) -> p g t e", g=2, t=T)
            link(v.tensor_scalar(need[:], bank(7, 64, E0), -1.0, float(CAP), ALU.mult, ALU.add))
            nb = need[:].unsqueeze(1).broadcast_to([P, T, E0])
            v.tensor_tensor(q1[:], rank[:, 1], nb, ALU.is_le)
            link(v.tensor_tensor(ceq[:], rank[:, 1], nb, ALU.min))
            v.tensor_tensor(q2[:], q1[:], ge[:, 1], ALU.mult)
            link(v.tensor_tensor(ceq[:], rank[:, 0], ceq[:], ALU.add))
            link(v.tensor_tensor(q2[:], q2[:], ge[:, 0], ALU.add))
            link(v.tensor_tensor(slot[:], q2[:], ceq[:], ALU.mult))
            for t in range(T):
                for e in range(E0):
                    ins = v.tensor_scalar(S[:, t, e, :], slot_no[:], slot[:, t, e:e + 1], None, ALU.is_equal)
                ins.then_inc(S_ready, 1)
            dve.wait_ge(gather_done, 1)
            v.tensor_reduce(pv[:], bank(2, 0, 3 * E0).rearrange("p (e a) -> p e a", a=3), X, ALU.add)\
             .then_inc(pv_sum, 1)
            dve.wait_ge(pv_sum, 1)
            dve.wait_ge(ld["b2"], 16)
            for e in range(E0):
                s = e % 2
                dve.wait_ge(y_done, e + 1)
                link(v.tensor_tensor(y1[:], bank(7, 128, P), b2s[:, e, :], ALU.add))
                link(v.tensor_scalar(y2[:], y1[:], pv[:, e:e + 1], None, ALU.mult))
                if e >= 2:
                    dve.wait_ge(sc_done, 2 * (e - 1))
                link(v.tensor_copy(yp[:, s, 0], y2[:]))
                link(v.tensor_tensor(y3[:], y2[:], yp[:, s, 0], ALU.subtract))
                link(v.tensor_copy(yp[:, s, 1], y3[:]))
                v.tensor_tensor(yp[:, s, 2], y3[:], yp[:, s, 1], ALU.subtract).then_inc(yp_ready, 1)
            for b in range(B):
                dve.wait_ge(sc_done, 2 * (E0 - 1) + b + 1)
                link(v.tensor_tensor(xs[:, TB * b:TB * b + TB, :], xs[:, TB * b:TB * b + TB, :],
                                     bank(3 + b).rearrange("p (t d) -> p t d", t=TB), ALU.add))
                stats(TB * b, TB * b + TB).then_inc(ln_stats, 1)
            v.memset(sm4[:], 0.0).then_inc(x2_ready, 1)

            for b in range(B):
                dve.wait_ge(ln_rstd, 3 + b)
                norm(TB * b, TB * b + TB, rstd)
            dve.wait_ge(x2_ready, 1)
            for b in range(B):
                dve.wait_ge(s1_done, b + 1)
                s1 = bank(2 + 2 * b, 0, TB * J).rearrange("p (t j) -> p t j", t=TB)
                link(v.tensor_reduce(sm4[:, b, 0, :], s1, X, ALU.max))
                v.tensor_tensor(p1[:, b], s1, sm4[:, b, 0, :].unsqueeze(2).broadcast_to([P, TB, J]), ALU.subtract)\
                 .then_inc(p1s_ready, 1)
            for b in range(B):
                dve.wait_ge(p1_ready, b + 1)
                link(v.tensor_reduce(sm4[:, b, 1, :], p1[:, b], X, ALU.add))
                link(v.reciprocal(sm4[:, b, 2, :], sm4[:, b, 1, :]))
            for b in range(B):
                dve.wait_ge(pv1_done, b + 1)
                for t in range(TB):
                    q = TB * b + t
                    ins = v.scalar_tensor_tensor(out=xs[:, q, :], in0=bank(5 + 2 * b, P * t, P),
                                                 scalar=sm4[:, b, 2, t:t + 1], in1=xs[:, q, :], op0=ALU.mult,
                                                 op1=ALU.add)
                ins.then_inc(x3_ready, 1)
                dve.wait_ge(x3_ready, b + 1)
                stats(TB * b, TB * b + TB).then_inc(ln_stats, 1)
            for b in range(B):
                dve.wait_ge(ln_rstd, 5 + b)
                norm(TB * b, TB * b + TB, rstd)

            by_group = sf[:].rearrange("p t (g k) -> p (t g) k", g=NG)

            def route_groups(b):
                dve.wait_ge(sig_ready, b + 1)
                link(v.tensor_tensor(sf[:], sc[:, b], rb_b.unsqueeze(1).broadcast_to([P, TB, E1]), ALU.add))
                hi4 = a4[:, 0].rearrange("p t g k -> p (t g) k")
                lo4 = a4[:, 1].rearrange("p t g k -> p (t g) k")
                v.tensor_tensor(hi4, by_group[:, :, 0:4], by_group[:, :, 4:8], ALU.max)
                link(v.tensor_tensor(lo4, by_group[:, :, 0:4], by_group[:, :, 4:8], ALU.min))
                two = [a2[:, k].rearrange("p t g k -> p (t g) k") for k in range(4)]
                v.tensor_tensor(two[0], hi4[:, :, 0:2], hi4[:, :, 2:4], ALU.max)
                v.tensor_tensor(two[1], hi4[:, :, 0:2], hi4[:, :, 2:4], ALU.min)
                link(v.tensor_tensor(two[2], lo4[:, :, 0:2], lo4[:, :, 2:4], ALU.max))
                link(v.tensor_tensor(two[1], two[1], two[2], ALU.max))
                one = [a1[:, k].rearrange("p t g -> p (t g)").unsqueeze(2) for k in range(4)]
                v.tensor_tensor(one[0], two[0][:, :, 0:1], two[0][:, :, 1:2], ALU.max)
                v.tensor_tensor(one[1], two[0][:, :, 0:1], two[0][:, :, 1:2], ALU.min)
                link(v.tensor_tensor(one[2], two[1][:, :, 0:1], two[1][:, :, 1:2], ALU.max))
                link(v.tensor_tensor(one[1], one[1], one[2], ALU.max))
                link(v.tensor_tensor(one[0], one[0], one[1], ALU.add))

            def route_mask(b):
                mine = a1[:, 0].unsqueeze(3).broadcast_to([P, TB, NG, NG])
                other = a1[:, 0].unsqueeze(2).broadcast_to([P, TB, NG, NG])
                v.tensor_tensor(gg[:, 0], other, mine, ALU.is_gt)
                link(v.tensor_tensor(gg[:, 1], other, mine, ALU.is_equal))
                link(v.tensor_tensor(gg[:, 1], gg[:, 1], earlier[:].unsqueeze(1).broadcast_to([P, TB, NG, NG]),
                                     ALU.mult))
                link(v.tensor_tensor(gg[:, 0], gg[:, 0], gg[:, 1], ALU.add))
                link(v.tensor_reduce(gm[:, 0], gg[:, 0], X, ALU.add))
                link(v.tensor_scalar(gm[:, 1], gm[:, 0], 2.0, None, ALU.is_lt))
                link(v.tensor_tensor(by_group, by_group, gm[:, 1].rearrange("p t g -> p (t g)").unsqueeze(2)
                                     .broadcast_to([P, TB * NG, GE]), ALU.mult))

            def route_top(b):
                for t in range(TB):
                    ins = v.max(top8[:, t, :], sf[:, t, :])
                link(ins)
                fourth = top8[:, :, 3:4].broadcast_to([P, TB, E1])
                v.tensor_tensor(r1[:], sf[:], fourth, ALU.is_gt)
                link(v.tensor_tensor(r2[:], sf[:], fourth, ALU.is_equal))
                v.tensor_reduce(n4[:, 0, :], r1[:], X, ALU.add)
                link(v.tensor_tensor_scan(r3[:].rearrange("p t e -> p (t e)"),
                                          scan_keep[:].rearrange("p t e -> p (t e)"),
                                          r2[:].rearrange("p t e -> p (t e)"), 0.0, ALU.mult, ALU.add))
                link(v.tensor_tensor(r3[:], r3[:], n4[:, 0, :].unsqueeze(2).broadcast_to([P, TB, E1]), ALU.add))
                link(v.scalar_tensor_tensor(out=r3[:], in0=r3[:], scalar=4.0, in1=r2[:], op0=ALU.is_le, op1=ALU.mult))
                link(v.tensor_tensor(r3[:], r3[:], r1[:], ALU.add))

            def route_weights(b):
                link(v.tensor_tensor(r3[:], r3[:], sc[:, b], ALU.mult))
                link(v.tensor_reduce(n4[:, 0, :], r3[:], X, ALU.add))
                link(v.tensor_scalar(n4[:, 0, :], n4[:, 0, :], 1e-20, None, ALU.add))
                link(v.reciprocal(n4[:, 1, :], n4[:, 0, :]))
                link(v.scalar_tensor_tensor(out=r3[:], in0=r3[:], scalar=2.5,
                                            in1=n4[:, 1, :].unsqueeze(2).broadcast_to([P, TB, E1]),
                                            op0=ALU.mult, op1=ALU.mult))
                if b == 1:
                    dve.wait_ge(wt_done, 1)
                link(v.tensor_copy(wp[:, :, 0, :], r3[:]))
                link(v.tensor_tensor(r1[:], r3[:], wp[:, :, 0, :], ALU.subtract))
                link(v.tensor_copy(wp[:, :, 1, :], r1[:]))
                v.tensor_tensor(wp[:, :, 2, :], r1[:], wp[:, :, 1, :], ALU.subtract).then_inc(wp_ready, 1)

            def mul_up(n):
                dve.wait_ge(sg_ready, n + 1)
                dve.wait_ge(u1_done, n + 1)
                if n >= NHU and (n - NHU) % CHS == CH:
                    dve.wait_ge(dn_done, n - NHU + 1)
                v.tensor_tensor(hu[:, n % NHU, :], sg[:, n % 2, :], bank(2 + n % 2), ALU.mult).then_inc(hu_ready, 1)

            def mul_w(n):
                b, c = divmod(n, CHS)
                if c == CH:
                    return
                m = CH * b + c
                dve.wait_ge(hu_ready, n + 1)
                dve.wait_ge(wb_done, m + 1)
                if m >= NHW:
                    dve.wait_ge(dn_done, n - NHW + 1)
                v.tensor_tensor(hw[:, m % NHW, :], hu[:, n % NHU, :], bank(4 + m % 2), ALU.mult).then_inc(hw_ready, 1)

            def add_out(b):
                dve.wait_ge(yt_done, b + 1)
                v.tensor_tensor(xs[:, TB * b:TB * b + TB, :], xs[:, TB * b:TB * b + TB, :],
                                bank(7).rearrange("p (t d) -> p t d", t=TB), ALU.add).then_inc(yo_ready, 1)

            ROUTE = [route_groups, route_mask, route_top, route_weights]
            for k, step in enumerate(ROUTE):
                step(0)
                mul_up(k)
            for n in range(len(ROUTE), B * CHS + LEAD):
                if n >= LEAD:
                    mul_w(n - LEAD)
                    if n - LEAD == CH:
                        dve.wait_ge(dn_done, CHS)
                        v.tensor_copy(yT, bank(6)).then_inc(yT_ready, 1)
                if n < B * CHS:
                    mul_up(n)
                if n >= LEAD + 1 and n % 2 == 1 and (n - LEAD - 1) // 2 < len(ROUTE):
                    ROUTE[(n - LEAD - 1) // 2](1)
                if n == CHS + LEAD + 3:
                    add_out(0)
            dve.wait_ge(dn_done, B * CHS)
            v.tensor_copy(yT, bank(6)).then_inc(yT_ready, 1)
            add_out(1)


def kernel(**inputs):
    import numpy as np
    import concourse.bacc as bacc
    from concourse import mybir as mb
    from concourse.bass_utils import run_bass_kernel_spmd

    g = {k: np.asarray(v) for k, v in inputs.items()}
    col = lambda a: np.asarray(a).reshape(-1, P).T
    per = {
        "x": g["x"].reshape(T, P, P).transpose(1, 0, 2),
        "ctx": g["ctx_1024"],
        "ctx_t": g["ctx_1024"].reshape(BJ, P).T,
        "cols": np.concatenate([col(g[k]) for k in ("L0_xattn_ln1_w", "L0_xattn_ln1_b", "L0_xattn_ln2_w",
                                                    "L0_xattn_ln2_b", "L1_xattn_bq", "L1_xattn_bk",
                                                    "L0_ffn_b1")], 1),
        "f_pair": g["fside_Bx16_0"].reshape(B, PAIRS, 2).transpose(2, 1, 0).reshape(2, 2 * PAIRS),
        "f_head": g["fside_Bx16_0"].T,
        "row": np.concatenate([g["L0_ffn_bs"], g["L1_xattn_bv"], g["L1_ffn_router_bias"]]).reshape(1, -1),
        "w_kv": g["L0_xattn_Wkv"],
        "wq_t": g["L0_xattn_Wq"].T,
        "w_out": g["L0_xattn_Wout"],
        "w1": g["L0_ffn_W1"].transpose(1, 0, 2).reshape(P, -1),
        "w2": g["L0_ffn_W2"].reshape(E0, FC, P, P).transpose(2, 0, 1, 3).reshape(P, -1),
        "b2": g["L0_ffn_b2"].reshape(1, -1),
        "l1w": np.concatenate([g["L1_xattn_Wq"], g["L1_xattn_Wk"].T, g["L1_xattn_Wv"].T,
                               g["L1_ffn_router_weight"].T, g["L0_ffn_Ws"]], 1),
        "gate": np.concatenate([g["L1_ffn_gate_w"].reshape(-1, P), g["L1_ffn_shared_gate_w"]]).T,
        "up": np.concatenate([g["L1_ffn_up_w"].reshape(-1, P), g["L1_ffn_shared_up_w"]]).T,
        "down": np.concatenate([g["L1_ffn_down_w"].transpose(0, 2, 1).reshape(CH, P, P),
                                g["L1_ffn_shared_down_w"].T[None]]).transpose(1, 0, 2).reshape(P, -1),
    }
    nc = bacc.Bacc("TRN2", target_bir_lowering=False, num_devices=1)
    arrays, args = {}, []
    for name, a in per.items():
        a = np.ascontiguousarray(a)
        arrays[f"in_{name}_dram"] = a
        args.append(nc.dram_tensor(f"in_{name}_dram", a.shape, mb.dt.from_np(a.dtype), kind="ExternalInput").ap())
    args.append(nc.dram_tensor("out_0_dram", (B, TB * P, P), F32, kind="ExternalOutput").ap())
    block_kernel(nc, *args)
    r = run_bass_kernel_spmd(nc, [arrays], core_ids=[0])
    return r.results[0]["out_0_dram"]
```

```python
from contextlib import ExitStack

import concourse.bass as bass
from concourse import mybir

ALU = mybir.AluOpType
ACT = mybir.ActivationFunctionType
X = mybir.AxisListType.X
F32 = mybir.dt.float32
BF16 = mybir.dt.bfloat16
I32 = mybir.dt.int32
F32R = mybir.dt.float32r

P = 128
B = 2
T = 8
TB = T // B
N = T * P
J = 77
BJ = B * J
H, DH = 16, 64
PAIRS = H // 2
JM, JR = 64, J - 64
RG = 8 * JR
NC = PAIRS + 2
HB = [6, 6, 4]
E0, F0 = 8, 512
FC = F0 // P
CAP = N // E0
SEARCH = 10
NM = 7
E1, I1 = 32, 64
NG, GE = 4, 8
CH = E1 * I1 // P
CHS = CH + 1
LEAD = 6
SECOND = 20
BY_DVE = 29
CATCH_UP = 24
KEEP = {"start": 5, "context": 2, "softmax": 8, "search": 4, "ranks": 14, "norm2": 18, "zT": 4, "keys": 3, "norm3": 15}
NHU, NHW = LEAD + 2, 3
EPS = 1e-5


def block_kernel(nc, x, ctx, ctx_t, cols, f_pair, f_head, row, w_kv, wq_t, w_out, w1, w2, b2, l1w, gate, up, down,
                 out):
    es = ExitStack()
    with es:
        def sb(name, shape, dt=F32):
            return es.enter_context(nc.sbuf_tensor(name, shape, dt))

        def sem(name):
            return es.enter_context(nc.semaphore(name))

        ps = es.enter_context(nc.psum_tensor("ps", [P, 8, 512], F32))

        def bank(b, a=0, n=512, p=P):
            return ps[0:p, b, a:a + n]

        def bank16(b):
            return ps[:, b, :].bitcast(BF16)

        xs = sb("xs", [P, T, P])
        z = sb("z", [P, T, P])
        zT = sb("zT", [P, N])
        st = sb("st", [P, T, 6])
        mv = sb("mv", [P, T, 2])
        veps = sb("veps", [P, T])
        rstd = sb("rstd", [P, T])
        neghalf = sb("neghalf", [P, T])
        ident = sb("ident", [P, P])
        ident16 = sb("ident16", [P, P], BF16)
        ones16 = sb("ones16", [P, P], BF16)
        ones_row = sb("ones_row", [1, P])
        tri16 = sb("tri16", [P, P], BF16)
        slot_no = sb("slot_no", [P, P], BF16)
        pair_sel = sb("pair_sel", [2, P])
        digit_i = sb("digit_i", [P, NM], I32)
        digits = sb("digits", [P, SEARCH, NM], I32)
        esel = sb("esel", [3 * E1, CH * P], BF16)
        earlier = sb("earlier", [P, NG, NG])
        scan_keep = sb("scan_keep", [P, TB, E1])
        c_nat = sb("c_nat", [J, B, P])
        cT = sb("cT", [P, BJ])
        cl = sb("cl", [P, 6 + E0 * FC])
        fp = sb("fp", [2, 2 * PAIRS])
        fh = sb("fh", [H, B])
        rw = sb("rw", [P, E0 + P + E1])
        bs_b, bv_b, rb_b = rw[:, 0:E0], rw[:, E0:E0 + P], rw[:, E0 + P:E0 + P + E1]
        wk = sb("wk", [P, H * DH])
        wv = sb("wv", [P, H * DH])
        wqT = sb("wqT", [P, PAIRS, P])
        lw = sb("lw", [P, 3 * P + E1 + E0])
        l1q, l1kT, l1vT, rwT = lw[:, 0:P], lw[:, P:2 * P], lw[:, 2 * P:3 * P], lw[:, 3 * P:3 * P + E1]
        rwS = lw[:, 3 * P + E1:3 * P + E1 + E0]
        b2s = sb("b2s", [P, E0, P])
        region = sb("region", [P, 2 * T * E0 * P // 2])

        def part_of(at, size, pattern, dt=F32, **dims):
            return region[:, at:at + size].bitcast(dt).rearrange(pattern, **dims)

        stc = sb("stc", [J, B, 6])
        mvc = sb("mvc", [J, B, 2])
        rstdc = sb("rstdc", [J, B])
        zc = sb("zc", [J, B, P])
        xnT = sb("xnT", [P, BJ])
        scl = sb("scl", [P, PAIRS, B])
        wks = sb("wks", [P, H])
        cr = sb("cr", [H, 3, B, J])
        crp = sb("crp", [H, 3, B, J], BF16)
        crow = sb("crow", [3, H, B, J], BF16)
        mx1 = sb("mx1", [P, 2, H])
        sm1 = sb("sm1", [P, 2, H])
        rc1 = sb("rc1", [P, 2, H])
        pe_ = part_of(0, 2 * H * J, "p (s h j) -> p s h j", s=2, h=H)
        pn = part_of(2 * H * J, 2 * H * J, "p (s k) -> p s k", s=2)
        pT = part_of(4 * H * J, 2 * NC * P, "p (s c q) -> p s c q", s=2, c=NC)
        lg = sb("lg", [P, T, E0])
        pr = sb("pr", [P, T, E0])
        sm8 = sb("sm8", [P, 3, T])
        prr = sb("prr", [P, 2, T, E0])
        prp = sb("prp", [P, T, E0, 3], BF16)
        zr = wqT
        zp = sb("zp", [P, 3, T, P], BF16)
        cand = sb("cand", [P, NM, E0], I32)
        best = sb("best", [P, 2, NM + 1, E0])
        cmp = sb("cmp", [P, NM, T, E0], BF16)
        ge = sb("ge", [P, 2, T, E0], BF16)
        need = sb("need", [P, E0])
        ceq = sb("ceq", [P, T, E0])
        q1 = sb("q1", [P, T, E0])
        q2 = sb("q2", [P, T, E0])
        slot = sb("slot", [P, T, E0])
        S = part_of(0, T * E0 * P // 2, "p (t e s) -> p t e s", BF16, t=T, e=E0)
        ST = part_of(T * E0 * P // 2, T * E0 * P // 2, "p (t e s) -> p t e s", BF16, t=T, e=E0)
        xin = wv[:].rearrange("p (e s) -> p e s", e=E0)
        pv = sb("pv", [P, E0])
        hg = wk[:].rearrange("p (s f q) -> p s f q", s=2, f=FC)
        y1 = sb("y1", [P, P])
        y2 = sb("y2", [P, P])
        y3 = sb("y3", [P, P])
        yp = sb("yp", [P, 2, 3, P], BF16)
        k1T = sb("k1T", [P, BJ])
        c1 = sb("c1", [1, BJ])
        M1 = sb("M1", [P, BJ])
        v1 = sb("v1", [J, B, P])
        p1 = sb("p1", [P, B, TB, J])
        p1T = sb("p1T", [J, B, TB * P])
        sm4 = sb("sm4", [P, B, 3, TB])
        sc = sb("sc", [P, B, TB, E1])
        sf = sb("sf", [P, TB, E1])
        best8 = sb("best8", [P, TB, NG, GE])
        sum2 = sb("sum2", [P, TB, NG])
        scrap = sb("scrap", [1, 1])
        gg = sb("gg", [P, 2, TB, NG, NG])
        gm = sb("gm", [P, 2, TB, NG])
        top8 = sb("top8", [P, TB, 8])
        r1 = sb("r1", [P, TB, E1])
        r2 = sb("r2", [P, TB, E1])
        r3 = sb("r3", [P, TB, E1])
        n4 = sb("n4", [P, 2, TB])
        wp = sb("wp", [P, TB, 3, E1], BF16)
        wT = sb("wT", [3 * E1, N], BF16)
        W = TB * P
        with ExitStack() as before:
            dn = before.enter_context(nc.sbuf_tensor("dn", [P, CHS * P], F32))
        dn_lo = sb("dn_lo", [P, CHS * P], F32R)
        with ExitStack() as before:
            gs = before.enter_context(nc.sbuf_tensor("gs", [P, CHS * P], F32))
            us = before.enter_context(nc.sbuf_tensor("us", [P, CHS * P], F32))
            vmain = gs[:, 0:PAIRS * B * P].rearrange("p (c b k) -> p c b k", c=PAIRS, b=B)
            vrem = us[:, 0:2 * B * 5 * RG].rearrange("p (q b k) -> p q b k", q=2, b=B)
            M = before.enter_context(nc.sbuf_tensor("M", [P, B, H, J], F32))
            U = before.enter_context(nc.sbuf_tensor("U", [P, B, NC, P], F32))
            kT = before.enter_context(nc.sbuf_tensor("kT", [P, PAIRS, B, J], F32))
            wo = before.enter_context(nc.sbuf_tensor("wo", [P, PAIRS, P], F32))
            M_hi = before.enter_context(nc.sbuf_tensor("M_hi", [P, B, H, J], F32R))
            M_lo = before.enter_context(nc.sbuf_tensor("M_lo", [P, B, H, J], F32R))
            zq_hi = before.enter_context(nc.sbuf_tensor("zq_hi", [P, N], F32R))
            zq_lo = before.enter_context(nc.sbuf_tensor("zq_lo", [P, N], F32R))
        gate_lo = sb("gate_lo", [P, CHS * P], F32R)
        up_lo = sb("up_lo", [P, CHS * P], F32R)
        gate_hi = sb("gate_hi", [P, CHS * P], F32R)
        up_hi = sb("up_hi", [P, CHS * P], F32R)
        z_hi = sb("z_hi", [P, N], F32R)
        z_lo = sb("z_lo", [P, N], F32R)
        with ExitStack() as before:
            w1s = before.enter_context(nc.sbuf_tensor("w1s", [P, E0, F0], F32))
            w2s = before.enter_context(nc.sbuf_tensor("w2s", [P, E0, FC, P], F32))
        dn_hi = sb("dn_hi", [P, CHS * P], F32R)
        hw_hi = sb("hw_hi", [P, 3, W], F32R)
        hw_lo = sb("hw_lo", [P, 3, W], F32R)
        hu = part_of(0, NHU * W, "p (s q) -> p s q", s=NHU)
        hw = part_of(NHU * W, NHW * W, "p (s q) -> p s q", s=NHW)
        sg = part_of((NHU + NHW) * W, 2 * W, "p (s q) -> p s q", s=2)
        yT = region[:, (NHU + NHW + 2) * W:(NHU + NHW + 3) * W]

        UB = [7, 3, 4, 6]

        PIECES = [(0, 0, TB), (1, 0, TB // 2), (1, TB // 2, TB)]
        weigh, chunk = [], 0
        for step in range(B * CHS + 3):
            many = 0 if step < LEAD else 2 if step >= CATCH_UP and step % 2 == 0 else 1
            many = min(many, step - chunk, B * CHS - chunk)
            weigh.append(list(range(chunk, chunk + many)))
            chunk += many
        weigh += [[], []]
        BACK = next(step for step in range(len(weigh)) if CH in weigh[step]) + 2

        def hidden(n):
            return hu[:, n % NHU, :] if n % CHS == CH else hw[:, (n - n // CHS) % NHW, :]

        def wait_lo(engine, n):
            if n < BY_DVE:
                engine.wait_ge(hwlo_ready, n + 1)
            else:
                engine.wait_ge(hwlo_last, n - BY_DVE + 1)

        ld = {k: sem("ld_" + k) for k in ("x", "ctx", "ctx_t", "cols", "fp", "fh", "row", "wk", "wv", "wq", "wo",
                                          "l1w", "w1", "w2", "b2", "gate", "up", "down")}
        pool_step = sem("pool_step")
        consts_ready = sem("consts_ready")
        moe_consts_ready = sem("moe_consts_ready")
        dve_step = sem("dve_step")
        ctx_stats = sem("ctx_stats")
        ctx_rstd = sem("ctx_rstd")
        ln_stats = sem("ln_stats")
        ln_rstd = sem("ln_rstd")
        z_ready = sem("z_ready")
        fexp_done = sem("fexp_done")
        zc_ready = sem("zc_ready")
        zcT_done = sem("zcT_done")
        scl_ready = sem("scl_ready")
        xnT_ready = sem("xnT_ready")
        k_done = sem("k_done")
        kT_ready = sem("kT_ready")
        v_done = sem("v_done")
        vmain_ready = sem("vmain_ready")
        vrem_ready = sem("vrem_ready")
        vzero = sem("vzero")
        wks_ready = sem("wks_ready")
        ks_done = sem("ks_done")
        ks_read = sem("ks_read")
        crp_ready = sem("crp_ready")
        crow_ready = sem("crow_ready")
        zT_done = sem("zT_done")
        zT_ready = sem("zT_ready")
        m_done = sem("m_done")
        m_even = sem("m_even")
        m_odd = sem("m_odd")
        u_done = sem("u_done")
        u_main = sem("u_main")
        u_rem = sem("u_rem")
        s_done = sem("s_done")
        sub_done = sem("sub_done")
        exp_done = sem("exp_done")
        rc_ready = sem("rc_ready")
        nrm_done = sem("nrm_done")
        t_done = sem("t_done")
        pT_ready = sem("pT_ready")
        pv_done = sem("pv_done")
        x1_ready = sem("x1_ready")
        l1k_done = sem("l1k_done")
        l1k_ready = sem("l1k_ready")
        l1v_done = sem("l1v_done")
        l1v_ready = sem("l1v_ready")
        l1m_done = sem("l1m_done")
        l1m_ready = sem("l1m_ready")
        lg_done = sem("lg_done")
        lgs_ready = sem("lgs_ready")
        lge_ready = sem("lge_ready")
        pr_ready = sem("pr_ready")
        zp_ready = sem("zp_ready")
        prp_ready = sem("prp_ready")
        cmp_ready = sem("cmp_ready")
        cnt_done = sem("cnt_done")
        ge_ready = sem("ge_ready")
        rank_done = sem("rank_done")
        S_ready = sem("S_ready")
        st_done = sem("st_done")
        ST_ready = sem("ST_ready")
        gather_done = sem("gather_done")
        xin_ready = sem("xin_ready")
        pv_sum = sem("pv_sum")
        h_done = sem("h_done")
        hg_ready = sem("hg_ready")
        y_done = sem("y_done")
        yp_ready = sem("yp_ready")
        sc_done = sem("sc_done")
        gate_split = sem("gate_split")
        mhi_ready = sem("mhi_ready")
        mlo_ready = sem("mlo_ready")
        zqhi_ready = sem("zqhi_ready")
        zqlo_ready = sem("zqlo_ready")
        ident16_ready = sem("ident16_ready")
        esel_ready = sem("esel_ready")
        dnhi_ready = sem("dnhi_ready")
        dnlo_ready = sem("dnlo_ready")
        hwhi_ready = sem("hwhi_ready")
        hwlo_ready = sem("hwlo_ready")
        hwlo_last = sem("hwlo_last")
        zhi_ready = sem("zhi_ready")
        zlo_ready = sem("zlo_ready")
        x2_ready = sem("x2_ready")
        s1_done = sem("s1_done")
        p1s_ready = sem("p1s_ready")
        p1_ready = sem("p1_ready")
        p1T_done = sem("p1T_done")
        p1T_ready = sem("p1T_ready")
        pv1_done = sem("pv1_done")
        x3_ready = sem("x3_ready")
        rl_done = sem("rl_done")
        sig_ready = sem("sig_ready")
        wp_ready = sem("wp_ready")
        wt_done = sem("wt_done")
        wT_ready = sem("wT_ready")
        g_done = sem("g_done")
        u1_done = sem("u1_done")
        wb_done = sem("wb_done")
        sg_ready = sem("sg_ready")
        hu_ready = sem("hu_ready")
        hw_ready = sem("hw_ready")
        dn_done = sem("dn_done")
        yT_ready = sem("yT_ready")
        yt_done = sem("yt_done")
        yo_ready = sem("yo_ready")
        stored = sem("stored")

        block = es.enter_context(nc.Block())

        @block.sync
        def _(sp):
            sp.dma_start(c_nat[:], ctx.rearrange("b j d -> j b d")).then_inc(ld["ctx"], 16)
            sp.dma_start(cl[:], cols).then_inc(ld["cols"], 16)
            sp.dma_start(wqT[:], wq_t.rearrange("(c p) d -> p c d", p=P)).then_inc(ld["wq"], 16)
            sp.dma_start(wv[:], w_kv[:, H * DH:2 * H * DH]).then_inc(ld["wv"], 16)
            sp.dma_start(fh[:], f_head).then_inc(ld["fh"], 16)
            sp.dma_start(wo[:], w_out.rearrange("(c p) d -> p c d", p=P)).then_inc(ld["wo"], 16)
            sp.dma_start(rw[:], row.broadcast_to([P, E0 + P + E1])).then_inc(ld["row"], 16)
            sp.wait_ge(crp_ready, 1)
            for part in range(3):
                sp.dma_start(crow[part:part + 1, :, :, :], crp[:, part, :, :]).then_inc(crow_ready, 16)
            sp.dma_start(cT[:], ctx_t).then_inc(ld["ctx_t"], 16)
            sp.dma_start(lw[:], l1w).then_inc(ld["l1w"], 16)
            sp.dma_start(b2s[:].rearrange("p e d -> p (e d)"), b2.broadcast_to([P, E0 * P])).then_inc(ld["b2"], 16)
            sp.wait_ge(u_done, 5)
            sp.dma_start(gs[:], gate).then_inc(ld["gate"], 16)
            sp.dma_start(us[:], up).then_inc(ld["up"], 16)
            sp.dma_start(dn[:], down).then_inc(ld["down"], 16)
            sp.wait_ge(s_done, 2 * T)
            sp.wait_ge(pv_done, T)
            sp.dma_start(w1s[:], w1.rearrange("p (e f) -> p e f", e=E0)).then_inc(ld["w1"], 16)
            sp.dma_start(w2s[:], w2.rearrange("p (e c d) -> p e c d", e=E0, c=FC)).then_inc(ld["w2"], 16)
            for k, (b, t0, t1) in enumerate(PIECES):
                sp.wait_ge(yo_ready, k + 1)
                sp.dma_start(out[b].rearrange("(t p) d -> p t d", p=P)[:, t0:t1, :], xs[:, TB * b + t0:TB * b + t1, :])\
                  .then_inc(stored, 16)
            sp.wait_ge(stored, 16 * len(PIECES))

        @block.gpsimd
        def _(pool):
            steps = [0]

            def link(ins):
                steps[0] += 1
                ins.then_inc(pool_step, 1)
                pool.wait_ge(pool_step, steps[0])

            g = nc.gpsimd
            link(g.memset(ident[:], 0.0))
            link(g.affine_select(out=ident[:], in_=ident[:], compare_op=ALU.not_equal, fill=1.0, base=0,
                                 pattern=[[-1, P]], channel_multiplier=1))
            link(g.memset(pair_sel[:], 1.0))
            link(g.affine_select(out=pair_sel[:], in_=pair_sel[:], compare_op=ALU.is_ge, fill=0.0, base=0,
                                 pattern=[[1, P]], channel_multiplier=-DH))
            link(g.affine_select(out=pair_sel[:], in_=pair_sel[:], compare_op=ALU.is_ge, fill=0.0, base=DH - 1,
                                 pattern=[[-1, P]], channel_multiplier=DH))
            link(g.memset(neghalf[:], -0.5))
            g.memset(ones_row[:], 1.0)
            g.memset(ones16[:], 1.0).then_inc(consts_ready, 1)

            pool.wait_ge(ctx_stats, 1)
            link(g.tensor_scalar(rstdc[:], mvc[:, :, 1], EPS, None, ALU.add))
            g.tensor_tensor(rstdc[:], rstdc[:], neghalf[0:J, 0:B], ALU.pow).then_inc(ctx_rstd, 1)
            g.memset(vmain, 0.0)
            g.memset(vrem, 0.0).then_inc(vzero, 1)

            def ln(a, b, count):
                pool.wait_ge(ln_stats, count)
                link(g.tensor_scalar(veps[:, a:b], mv[:, a:b, 1], EPS, None, ALU.add))
                return g.tensor_tensor(rstd[:, a:b], veps[:, a:b], neghalf[:, a:b], ALU.pow)

            pool.wait_ge(ln_stats, 1)
            link(g.tensor_scalar(veps[:], mv[:, :, 1], 1.0 + EPS, EPS * EPS, ALU.mult, ALU.add))
            g.tensor_tensor(rstd[:], veps[:], neghalf[:], ALU.pow).then_inc(ln_rstd, 1)

            link(g.memset(tri16[:], 1.0))
            g.affine_select(out=tri16[:], in_=tri16[:], compare_op=ALU.is_ge, fill=0.0, base=0,
                            pattern=[[1, P]], channel_multiplier=-1)
            g.iota(slot_no[:], [[1, P]], base=1, channel_multiplier=0, allow_small_or_imprecise_dtypes=True)
            g.iota(digit_i[:], [[1, NM]], base=1, channel_multiplier=0)
            link(g.memset(earlier[:], 1.0))
            g.affine_select(out=earlier[:], in_=earlier[:], compare_op=ALU.is_gt, fill=0.0, base=0,
                            pattern=[[1, NG], [-1, NG]], channel_multiplier=0)
            link(g.memset(scan_keep[:], 1.0))
            g.memset(scan_keep[:, :, 0:1], 0.0).then_inc(moe_consts_ready, 1)

            def low_parts(b):
                pool.wait_ge(mhi_ready, b + 1)
                g.tensor_tensor(M_lo[:, b], M[:, b], M_hi[:, b].bitcast(F32), ALU.subtract).then_inc(mlo_ready, 1)
                pool.wait_ge(zqhi_ready, b + 1)
                r = slice(512 * b, 512 * b + 512)
                g.tensor_tensor(zq_lo[:, r], zT[:, r], zq_hi[:, r].bitcast(F32), ALU.subtract).then_inc(zqlo_ready, 1)

            low_parts(0)
            for i in range(T):
                s = i % 2
                pool.wait_ge(rc_ready, i + 1)
                pool.wait_ge(exp_done, 2 * i + 2)
                if i >= 2:
                    pool.wait_ge(t_done, 3 * (i - 1))
                for j0, nj, at in ((0, JM, 0), (JM, JR, H * JM)):
                    ins = g.tensor_tensor(pn[:, s, at:at + H * nj].rearrange("p (h j) -> p h j", h=H),
                                          pe_[:, s, :, j0:j0 + nj],
                                          rc1[:, s].unsqueeze(2).broadcast_to([P, H, nj]), ALU.mult)
                ins.then_inc(nrm_done, 1)
                if i == 1:
                    low_parts(1)
                if i == T - 2:
                    ln(0, TB, 2).then_inc(ln_rstd, 1)
            ln(TB, T - 1, 3).then_inc(ln_rstd, 1)
            ln(T - 1, T, 4).then_inc(ln_rstd, 1)

            pool.wait_ge(z_ready, 2 * T)
            for part in range(2):
                src = z if part == 0 else zr
                link(g.tensor_copy(zp[:, part], src[:]))
                link(g.tensor_tensor(zr[:], src[:], zp[:, part], ALU.subtract))
            g.tensor_copy(zp[:, 2], zr[:]).then_inc(zp_ready, 1)
            pool.wait_ge(pr_ready, 1)
            for part in range(2):
                src = pr[:] if part == 0 else prr[:, 0]
                link(g.tensor_copy(prp[:, :, :, part], src))
                link(g.tensor_tensor(prr[:, 0], src, prp[:, :, :, part], ALU.subtract))
            g.tensor_copy(prp[:, :, :, 2], prr[:, 0]).then_inc(prp_ready, 1)

            for whole, hi, lo, name in ((gs, gate_hi, gate_lo, "gate"), (us, up_hi, up_lo, "up")):
                pool.wait_ge(ld[name], 16)
                link(g.tensor_copy(hi[:], whole[:]))
                g.tensor_tensor(lo[:], whole[:], hi[:].bitcast(F32), ALU.subtract).then_inc(gate_split, 1)

            link(g.memset(esel[:], 1.0))
            for part in range(3):
                e = esel[part * E1:(part + 1) * E1, :]
                link(g.affine_select(out=e, in_=e, compare_op=ALU.is_ge, fill=0.0, base=0,
                                     pattern=[[1, CH * P]], channel_multiplier=-I1))
                g.affine_select(out=e, in_=e, compare_op=ALU.is_ge, fill=0.0, base=I1 - 1,
                                pattern=[[-1, CH * P]], channel_multiplier=I1).then_inc(esel_ready, 1)
                pool.wait_ge(esel_ready, part + 1)

            for k in range(2):
                for b in range(B):
                    ln(TB * b, TB * b + TB, 5 + 2 * k + b).then_inc(ln_rstd, 1)
                if k == 0:
                    pool.wait_ge(dnhi_ready, 1)
                    g.tensor_tensor(dn_lo[:], dn[:], dn_hi[:].bitcast(F32), ALU.subtract).then_inc(dnlo_ready, 1)
            for b in range(B):
                pool.wait_ge(zhi_ready, b + 1)
                r = slice(512 * b, 512 * b + 512)
                g.tensor_tensor(z_lo[:, r], zT[:, r], z_hi[:, r].bitcast(F32), ALU.subtract).then_inc(zlo_ready, 1)
            for n in range(BY_DVE):
                pool.wait_ge(hwhi_ready, n + 1)
                if n >= 3:
                    pool.wait_ge(dn_done, n - 2)
                g.tensor_tensor(hw_lo[:, n % 3, :], hidden(n), hw_hi[:, n % 3, :].bitcast(F32), ALU.subtract)\
                 .then_inc(hwlo_ready, 1)

        @block.scalar
        def _(act):
            a = nc.scalar
            act.dma_start(wk[:], w_kv[:, 0:H * DH]).then_inc(ld["wk"], 16)
            act.dma_start(fp[:], f_pair).then_inc(ld["fp"], 16)
            act.dma_start(xs[:], x).then_inc(ld["x"], 16)

            act.wait_ge(consts_ready, 1)
            a.activation(ident16[:], ident[:], ACT.Copy).then_inc(ident16_ready, 1)
            for k in range(3):
                act.wait_ge(m_done, 2 * k + 1)
                nh = min(3, 8 - 3 * k)
                for b in range(B):
                    src = bank(3 + k, 0, nh * BJ).rearrange("p (h b j) -> p h b j", h=nh, b=B)
                    ins = a.activation(M[:, b, 6 * k:6 * k + 2 * nh:2, :], src[:, :, b, :], ACT.Copy)
                ins.then_inc(m_even, 1)
            act.wait_ge(ld["cols"], 16)
            for half in range(2):
                act.wait_ge(zT_done, half + 1)
                a.activation(zT[:, 512 * half:512 * half + 512], bank(7 if half == 0 else 2), ACT.Identity,
                             bias=cl[:, 3:4], scale=cl[:, 2:3]).then_inc(zT_ready, 1)

            def high_parts(b):
                if b == 0:
                    act.wait_ge(m_even, 3)
                    act.wait_ge(m_odd, 3)
                    act.wait_ge(zT_ready, 2)
                a.activation(M_hi[:, b], M[:, b], ACT.Copy).then_inc(mhi_ready, 1)
                a.activation(zq_hi[:, 512 * b:512 * b + 512], zT[:, 512 * b:512 * b + 512], ACT.Copy)\
                 .then_inc(zqhi_ready, 1)

            act.wait_ge(vzero, 1)
            for k in range(4):
                act.wait_ge(vrem_ready, k + 1)
                for h2 in range(2):
                    r = slice(DH * h2, DH * h2 + DH)
                    src = ps[r, 3 + k, 0:2 * BJ].rearrange("p (c b j) -> p c b j", c=2, b=B)
                    ins = a.activation(vmain[r, 2 * k:2 * k + 2, :, JM * h2:JM * h2 + JM], src[:, :, :, 0:JM], ACT.Copy)
                ins.then_inc(vmain_ready, 1)

            def u_copy(k):
                b, half = divmod(k, 2)
                act.wait_ge(u_done, k + 1)
                a.activation(U[:, b, 4 * half:4 * half + 4, :],
                             bank(UB[k]).rearrange("p (c d) -> p c d", c=4), ACT.Copy).then_inc(u_main, 1)

            def load_table(func):
                a.activation(scrap[:], ident[0:1, 0:1], func)

            def exps(i):
                s = i % 2
                act.wait_ge(sub_done, 2 * i + 1)
                a.activation(pe_[:, s, 0:12, :], pe_[:, s, 0:12, :], ACT.Exp).then_inc(exp_done, 1)
                act.wait_ge(sub_done, 2 * i + 2)
                a.activation(pe_[:, s, 12:16, :], pe_[:, s, 12:16, :], ACT.Exp).then_inc(exp_done, 1)

            def evac(i):
                s = i % 2
                if i >= 2:
                    act.wait_ge(pv_done, i - 1)
                for k in range(3):
                    act.wait_ge(t_done, 3 * i + k + 1)
                    if k < 2:
                        a.activation(pT[:, s, 4 * k:4 * k + 4, :], bank(3 + k).rearrange("p (c q) -> p c q", c=4),
                                     ACT.Copy).then_inc(pT_ready, 1)
                    else:
                        a.activation(pT[0:RG, s, 8:10, :],
                                     bank(5, 0, 256, RG).rearrange("p (c q) -> p c q", c=2),
                                     ACT.Copy).then_inc(pT_ready, 1)

            def zcopy_tiles(t0, t1, b, count):
                act.wait_ge(zT_done, count)
                a.activation(zT[:, P * t0:P * t1], bank(b, P * (t0 % TB), P * (t1 - t0)), ACT.Copy)\
                 .then_inc(zT_ready, 1)

            def zcopy(half, k):
                zcopy_tiles(TB * half, TB * half + TB, half, 2 * k + half + 1 + (k > 1))

            high_parts(0)
            u_copy(0)
            exps(0)
            u_copy(1)
            u_copy(2)
            u_copy(3)
            exps(1)
            high_parts(1)
            for i in range(2, T + 2):
                evac(i - 2)
                if i == T + 1:
                    zcopy(0, 1)
                if i < T:
                    exps(i)
            zcopy_tiles(TB, T - 1, 1, 4)
            zcopy_tiles(T - 1, T, 0, 5)
            act.wait_ge(lgs_ready, 1)
            a.activation(lg[:], lg[:], ACT.Exp).then_inc(lge_ready, 1)
            load_table(ACT.Gelu_apprx_tanh)

            def st_copy(t):
                act.wait_ge(st_done, t + 1)
                a.activation(ST[:, t].rearrange("p e s -> p (e s)"), bank16(3 + t % 2), ACT.Copy)\
                 .then_inc(ST_ready, 1)

            for t in range(T - 2):
                st_copy(t)
            act.wait_ge(gather_done, 1)
            for half in range(2):
                a.activation(xin[:, 4 * half:4 * half + 4, :], bank(half).rearrange("p (e s) -> p e s", e=4),
                             ACT.Copy).then_inc(xin_ready, 1)
            for e in range(E0):
                act.wait_ge(h_done, e + 1)
                if e >= 2:
                    act.wait_ge(y_done, e - 1)
                for f in range(FC):
                    ins = a.activation(hg[:, e % 2, f, :], bank(5 + e % 2, P * f, P), ACT.Gelu_apprx_tanh,
                                       bias=cl[:, 6 + FC * e + f:7 + FC * e + f])
                ins.then_inc(hg_ready, 1)
                if e < 2:
                    st_copy(T - 2 + e)
            act.wait_ge(y_done, E0)
            act.wait_ge(ld["down"], 16)
            a.activation(dn_hi[:], dn[:], ACT.Copy).then_inc(dnhi_ready, 1)
            load_table(ACT.Exp)

            for b in range(B):
                zcopy(b, 2)
            for b in range(B):
                act.wait_ge(p1s_ready, b + 1)
                a.activation(p1[:, b], p1[:, b], ACT.Exp).then_inc(p1_ready, 1)
                act.wait_ge(p1T_done, b + 1)
                a.activation(p1T[:, b], bank(3 + 3 * b, 0, TB * P, J), ACT.Copy).then_inc(p1T_ready, 1)
            load_table(ACT.Sigmoid)

            def z_hi_copy(b):
                a.activation(z_hi[:, 512 * b:512 * b + 512], bank(b), ACT.Copy).then_inc(zhi_ready, 1)

            def scores_copy(b):
                act.wait_ge(rl_done, b + 1)
                a.activation(sc[:, b], bank(7 - 2 * b, 0, TB * E1).rearrange("p (t e) -> p t e", t=TB), ACT.Sigmoid)\
                 .then_inc(sig_ready, 1)

            zcopy(0, 3)
            z_hi_copy(0)
            zcopy(1, 3)
            scores_copy(0)
            z_hi_copy(1)
            scores_copy(1)

            def weights_copy(b):
                act.wait_ge(wt_done, b + 1)
                a.activation(wT[:, 512 * b:512 * b + 512], bank16(7)[0:3 * E1, 512:1024], ACT.Copy)\
                 .then_inc(wT_ready, 1)

            def hidden_hi(n):
                if n % CHS == CH:
                    act.wait_ge(hu_ready, n + 1)
                else:
                    act.wait_ge(hw_ready, n - n // CHS + 1)
                if n >= 3:
                    act.wait_ge(dn_done, n - 2)
                a.activation(hw_hi[:, n % 3, :], hidden(n), ACT.Copy).then_inc(hwhi_ready, 1)

            for n in range(len(weigh)):
                if n in (LEAD, SECOND):
                    weights_copy(int(n == SECOND))
                if n < B * CHS:
                    act.wait_ge(g_done, n + 1)
                    if n >= 2:
                        act.wait_ge(hu_ready, n - 1)
                    a.activation(sg[:, n % 2, :], bank(n % 2), ACT.Silu).then_inc(sg_ready, 1)
                for m in weigh[n - 1] if n > 0 else []:
                    hidden_hi(m)

        @block.tensor
        def _(pe):
            mm = nc.tensor.matmul
            tr = nc.tensor.transpose
            def keep_clock(n, b):
                for _ in range(n):
                    mm(bank(b), ones16[:], ones16[:].unsqueeze(1).broadcast_to([P, 4, P]), start=True, stop=True)

            pe.wait_ge(consts_ready, 1)
            keep_clock(KEEP["start"], 6)
            pe.wait_ge(ld["fp"], 16)
            mm(bank(7, 0, 16), pair_sel[:], fp[:], start=True, stop=True).then_inc(fexp_done, 1)
            pe.wait_ge(zc_ready, 1)
            for b in range(B):
                ins = tr(bank(7, 64 + J * b, J), zc[:, b, :], ident[0:J, 0:J])
            ins.then_inc(zcT_done, 1)
            keep_clock(KEEP["context"], 6)
            pe.wait_ge(xnT_ready, 1)
            pe.wait_ge(ld["wk"], 16)
            for k in range(3):
                for c in range(3 * k, min(3 * k + 3, PAIRS)):
                    ins = mm(bank(k, BJ * (c - 3 * k), BJ), wk[:, P * c:P * c + P], xnT[:], start=True, stop=True)
                ins.then_inc(k_done, 1)
            pe.wait_ge(wks_ready, 1)
            pe.wait_ge(scl_ready, 1)
            mm(bank(7, 0, BJ, H), wks[:], xnT[:], start=True, stop=True).then_inc(ks_done, 1)
            def trans_tiles(t0, t1, b, count):
                pe.wait_ge(z_ready, count)
                for t in range(t0, t1):
                    ins = tr(bank(b, P * (t % TB), P), z[:, t, :], ident[:])
                ins.then_inc(zT_done, 1)

            def trans_half(half, b, count):
                trans_tiles(TB * half, TB * half + TB, b, count)

            pe.wait_ge(ld["wq"], 16)
            for k in range(3):
                pe.wait_ge(kT_ready, k + 1)
                for h2 in range(2):
                    r = slice(DH * h2, DH * h2 + DH)
                    for c in range(3 * k, min(3 * k + 3, PAIRS)):
                        ins = mm(bank(3 + k if h2 == 0 else [6, 0, 1][k], BJ * (c - 3 * k), BJ), wqT[r, c, :],
                                 kT[r, c].rearrange("p b j -> p (b j)"), start=True, stop=True)
                    ins.then_inc(m_done, 1)
            pe.wait_ge(ld["wv"], 16)
            pe.wait_ge(ks_read, 1)
            for k in range(4):
                if k >= 2:
                    trans_half(k - 2, 7 if k == 2 else 2, TB * (k - 1))
                if k < 3:
                    pe.wait_ge(m_even, k + 1)
                else:
                    pe.wait_ge(m_odd, 1)
                for c in range(2 * k, 2 * k + 2):
                    ins = mm(bank(3 + k, BJ * (c - 2 * k), BJ), wv[:, P * c:P * c + P], xnT[:], start=True, stop=True)
                ins.then_inc(v_done, 1)

            def u_mains(ks):
                pe.wait_ge(ld["wo"], 16)
                pe.wait_ge(vmain_ready, 4)
                pe.wait_ge(vrem_ready, 4)
                for k in ks:
                    b, half = divmod(k, 2)
                    for c in range(4):
                        p = 4 * half + c
                        ins = mm(bank(UB[k], P * c, P), vmain[:, p, b, :], wo[:, p, :], start=True, stop=True)
                    ins.then_inc(u_done, 1)

            def u_rems():
                for b in range(B):
                    for q in range(2):
                        for c in range(4):
                            ins = mm(bank(5, P * (2 * b + q), P, RG), vrem[:, q, b, RG * c:RG * c + RG],
                                     wo[:, 4 * q + c, :], start=(c == 0), stop=(c == 3))
                ins.then_inc(u_done, 1)

            def scores(i, banks=(0, 1, 2)):
                b = i // TB
                if i == 0:
                    pe.wait_ge(m_even, 3)
                    pe.wait_ge(m_odd, 3)
                    pe.wait_ge(zT_ready, 2)
                    pe.wait_ge(crow_ready, 16 * 3)
                if i in (2, TB) and 0 in banks:
                    pe.wait_ge(mlo_ready, b + 1)
                    pe.wait_ge(zqlo_ready, b + 1)
                for k in banks:
                    nh, h0 = HB[k], sum(HB[:k])
                    if i > 0 and k != 1:
                        pe.wait_ge(sub_done, 2 * i - 1 if k == 0 else 2 * i)
                    cols = lambda m: m[:, b, h0:h0 + nh, :].rearrange("p h j -> p (h j)")
                    r = slice(P * i, P * i + P)
                    if i < 2:
                        mm(bank(k, 0, nh * J), zT[:, r], cols(M), start=True, stop=False)
                    else:
                        mm(bank(k, 0, nh * J), zq_hi[:, r], cols(M_hi), start=True, stop=False)
                        mm(bank(k, 0, nh * J), zq_hi[:, r], cols(M_lo), start=False, stop=False)
                        mm(bank(k, 0, nh * J), zq_lo[:, r], cols(M_hi), start=False, stop=False)
                    ins = mm(bank(k, 0, nh * J).rearrange("p (h j) -> p h j", h=nh), ones16[0:3, :],
                             crow[:, h0:h0 + nh, b, :], start=False, stop=True)
                    if k >= 1:
                        ins.then_inc(s_done, 1)

            def turn(i):
                s = i % 2
                pe.wait_ge(nrm_done, i + 1)
                if i == 0:
                    pe.wait_ge(u_main, 4)
                    pe.wait_ge(u_rem, 1)
                else:
                    pe.wait_ge(pT_ready, 3 * i)
                for k in range(3):
                    for c in range(4 * k, min(4 * k + 4, NC)):
                        if c < PAIRS:
                            ins = tr(bank(3 + k, P * (c % 4), P), pn[:, s, P * c:P * c + P], ident[:])
                        else:
                            q = c - PAIRS
                            ins = tr(bank(5, P * q, P, RG), pn[:, s, H * JM + RG * q:H * JM + RG * q + RG], ident[:])
                    ins.then_inc(t_done, 1)

            def attend(i):
                s, b = i % 2, i // TB
                if i >= 2:
                    pe.wait_ge(x1_ready, i - 1)
                for c in range(NC):
                    if c % 4 == 0:
                        pe.wait_ge(pT_ready, 3 * i + c // 4 + 1)
                    r = P if c < PAIRS else RG
                    ins = mm(bank(6 + s, 0, P), pT[0:r, s, c, :], U[0:r, b, c, :], start=(c == 0), stop=(c == NC - 1))
                ins.then_inc(pv_done, 1)

            scores(0)
            u_mains((0, 1))
            scores(1)
            u_mains((2, 3))
            u_rems()
            for i in range(2, T + 2):
                if i < T:
                    scores(i, (0, 1))
                turn(i - 2)
                if i < T:
                    scores(i, (2,))
                if i == T + 1:
                    pe.wait_ge(sub_done, 2 * T)
                    trans_half(0, 0, T + 4)
                attend(i - 2)

            def logits(t0, t1, count):
                pe.wait_ge(zT_ready, count)
                for t in range(t0, t1):
                    ins = mm(bank(2, E0 * t, E0), zT[:, P * t:P * t + P], rwS, start=True, stop=True)
                return ins

            trans_tiles(TB, T - 1, 1, 2 * T - 1)
            pe.wait_ge(ld["l1w"], 16)
            logits(0, TB, 3)
            pe.wait_ge(ld["ctx_t"], 16)
            mm(bank(3, 0, BJ), l1kT, cT[:], start=True, stop=True).then_inc(l1k_done, 1)
            for b in range(B):
                ins = mm(bank(4, P * b, P, J), cT[:, J * b:J * b + J], l1vT, start=True, stop=True)
            ins.then_inc(l1v_done, 1)
            trans_tiles(T - 1, T, 0, 2 * T)
            pe.wait_ge(l1k_ready, 1)
            mm(bank(5, 0, BJ), l1q, k1T[:], start=True, stop=True)
            mm(bank(5, 256, BJ, 1), cl[:, 4:5], k1T[:], start=True, stop=True).then_inc(l1m_done, 1)

            logits(TB, T - 1, 4)
            logits(T - 1, T, 5).then_inc(lg_done, 1)
            keep_clock(KEEP["softmax"], 6)
            for k in range(SEARCH):
                pe.wait_ge(cmp_ready, k + 1)
                for t in range(T):
                    ins = mm(bank(7, 0, NM * E0), ones16[:], cmp[:, :, t, :], start=(t == 0), stop=(t == T - 1))
                ins.then_inc(cnt_done, 1)
                keep_clock(KEEP["search"], 6)
            pe.wait_ge(ge_ready, 1)
            rank = bank(6, 0, 2 * T * E0).rearrange("p (g t e) -> p g t e", g=2, t=T)
            mm(rank, tri16[:], ge[:], start=True, stop=False, skip_group_check=True)
            for k in range(T - 1):
                for w in range(2):
                    mm(rank[:, w, k + 1:T, :], ones16[:],
                       ge[:, w, k, :].unsqueeze(1).broadcast_to([P, T - 1 - k, E0]),
                       start=False, stop=(k == T - 2), skip_group_check=True)
            for t in range(T):
                ins = mm(bank(7, 64, E0), ones16[:], ge[:, 0, t, :], start=(t == 0), stop=(t == T - 1))
            ins.then_inc(rank_done, 1)
            keep_clock(KEEP["ranks"], 3)
            pe.wait_ge(zp_ready, 1)
            pe.wait_ge(prp_ready, 1)
            pe.wait_ge(ident16_ready, 1)

            def st_turn(t):
                if t >= 2:
                    pe.wait_ge(ST_ready, t - 1)
                for e in range(E0):
                    ins = tr(bank16(3 + t % 2)[:, P * e:P * e + P], S[:, t, e, :], ident16[:])
                ins.then_inc(st_done, 1)

            for t in range(T):
                pe.wait_ge(S_ready, t + 1)
                for half in range(2):
                    for part in range(3):
                        ins = mm(bank(half), zp[:, part, t, :],
                                 S[:, t, 4 * half:4 * half + 4, :].rearrange("p e s -> p (e s)"),
                                 start=(t == 0 and part == 0), stop=(t == T - 1 and part == 2))
                for e in range(E0):
                    ins = mm(bank(2, 3 * e, 3), S[:, t, e, :], prp[:, t, e, :], start=(t == 0 and e == 0),
                             stop=(t == T - 1), skip_group_check=True)
                if t == T - 1:
                    ins.then_inc(gather_done, 1)
                if t < T - 2:
                    st_turn(t)
            for t in range(T - 2, T):
                st_turn(t)

            def expert_h(e):
                if e == 0:
                    pe.wait_ge(ld["w1"], 16)
                pe.wait_ge(xin_ready, e // 4 + 1)
                if e >= 2:
                    pe.wait_ge(hg_ready, e - 1)
                for f in range(FC):
                    ins = mm(bank(5 + e % 2, P * f, P), w1s[:, e, P * f:P * f + P], xin[:, e, :], start=True, stop=True)
                ins.then_inc(h_done, 1)

            def expert_y(e):
                if e == 0:
                    pe.wait_ge(ld["w2"], 16)
                pe.wait_ge(hg_ready, e + 1)
                if e >= 2:
                    pe.wait_ge(yp_ready, e - 1)
                for f in range(FC):
                    ins = mm(bank(7 * (e % 2), 128, P), hg[:, e % 2, f, :], w2s[:, e, f, :], start=(f == 0), stop=(f == FC - 1))
                ins.then_inc(y_done, 1)

            def scatter(e):
                pe.wait_ge(yp_ready, e + 1)
                if e == 0:
                    pe.wait_ge(ST_ready, T)
                for t in range(T):
                    for part in range(3):
                        ins = mm(bank(3 + t // 4, P * (t % 4), P), ST[:, t, e, :], yp[:, e % 2, part, :],
                                 start=(e == 0 and part == 0 and t % 4 == 0), stop=(e == E0 - 1),
                                 skip_group_check=True)
                    if t % 4 == 3:
                        ins.then_inc(sc_done, 1)

            expert_h(0)
            for e in range(E0):
                if e + 1 < E0:
                    expert_h(e + 1)
                expert_y(e)
                if e > 0:
                    scatter(e - 1)
            scatter(E0 - 1)

            pe.wait_ge(l1m_ready, 1)
            pe.wait_ge(l1v_ready, 1)
            pe.wait_ge(pv_sum, 1)
            keep_clock(KEEP["norm2"], 7)

            def bias_scores(b):
                mm(bank(2 + 2 * b, 0, TB * J).rearrange("p (t j) -> p t j", t=TB), ones_row[:],
                   c1[:, J * b:J * b + J].unsqueeze(1).broadcast_to([1, TB, J]), start=True, stop=False,
                   skip_group_check=True)

            bias_scores(0)
            pe.wait_ge(x2_ready, B)
            for b in range(B):
                trans_half(b, b, 2 * T + 4 * b + 4)
                if b == 0:
                    bias_scores(1)
                else:
                    keep_clock(KEEP["zT"], 7)
                pe.wait_ge(zT_ready, 6 + b)
                for t in range(TB):
                    ins = mm(bank(2 + 2 * b, J * t, J), zT[:, P * (TB * b + t):P * (TB * b + t) + P],
                             M1[:, J * b:J * b + J], start=False, stop=(t == TB - 1), skip_group_check=True)
                ins.then_inc(s1_done, 1)
            for b in range(B):
                pe.wait_ge(p1_ready, b + 1)
                for t in range(TB):
                    ins = tr(bank(3 + 3 * b, P * t, P, J), p1[:, b, t, :], ident[:])
                ins.then_inc(p1T_done, 1)
                if b == 0:
                    keep_clock(KEEP["keys"], 7)
                pe.wait_ge(p1T_ready, b + 1)
                for t in range(TB):
                    ins = mm(bank(5 + 2 * b, P * t, P), p1T[:, b, P * t:P * t + P], v1[:, b, :], start=True, stop=True)
                ins.then_inc(pv1_done, 1)

            keep_clock(KEEP["norm3"], 2)
            for b in range(B):
                trans_half(b, b, 3 * T + 4 * b + 4)
                if b == 0:
                    keep_clock(KEEP["zT"], 2)
            for b in range(B):
                pe.wait_ge(zT_ready, 8 + b)
                for t in range(TB):
                    q = TB * b + t
                    ins = mm(bank(7 - 2 * b, E1 * t, E1), zT[:, P * q:P * q + P], rwT, start=True, stop=True)
                ins.then_inc(rl_done, 1)
            pe.wait_ge(gate_split, 2)
            pe.wait_ge(esel_ready, 3)

            def weights(b):
                pe.wait_ge(sig_ready, 2)
                pe.wait_ge(wp_ready, b + 1)
                for t in range(TB):
                    ins = tr(bank16(7)[0:3 * E1, 512 + P * t:512 + P * t + P],
                             wp[:, t].rearrange("p a e -> p (a e)"), ident16[:])
                ins.then_inc(wt_done, 1)

            def by_parts(to, hi, lo, c, b):
                w, r = slice(P * c, P * c + P), slice(512 * b, 512 * b + 512)
                mm(to, hi[:, w], z_hi[:, r], start=True, stop=False)
                mm(to, hi[:, w], z_lo[:, r], start=False, stop=False)
                return mm(to, lo[:, w], z_hi[:, r], start=False, stop=True)

            def gate_up(n):
                b, c = divmod(n, CHS)
                if n < 2:
                    pe.wait_ge(zhi_ready, n + 1)
                if c == 0:
                    pe.wait_ge(zlo_ready, b + 1)
                if n >= 2:
                    pe.wait_ge(sg_ready, n - 1)
                by_parts(bank(n % 2), gate_hi, gate_lo, c, b).then_inc(g_done, 1)
                if n >= 2:
                    pe.wait_ge(hu_ready, n - 1)
                by_parts(bank(2 + n % 2), up_hi, up_lo, c, b).then_inc(u1_done, 1)

            def spread(n):
                b, c = divmod(n, CHS)
                if c == CH:
                    return
                m = CH * b + c
                if m >= 2:
                    pe.wait_ge(hw_ready, m - 1)
                pe.wait_ge(wT_ready, b + 1)
                mm(bank(4 + m % 2), esel[:, P * c:P * c + P], wT[:, 512 * b:512 * b + 512], start=True, stop=True)\
                    .then_inc(wb_done, 1)

            def down_mm(n):
                b, c = divmod(n, CHS)
                if n == 0:
                    pe.wait_ge(dnlo_ready, 1)
                if c == 0 and b == 1:
                    pe.wait_ge(yT_ready, 1)
                w, k = slice(P * c, P * c + P), n % 3
                pe.wait_ge(hwhi_ready, n + 1)
                mm(bank(6), dn_lo[:, w], hw_hi[:, k, :], start=(c == 0), stop=False)
                mm(bank(6), dn_hi[:, w], hw_hi[:, k, :], start=False, stop=False)
                wait_lo(pe, n)
                mm(bank(6), dn_hi[:, w], hw_lo[:, k, :], start=False, stop=(c == CH)).then_inc(dn_done, 1)

            def turn_back(k):
                b, t0, t1 = PIECES[k]
                pe.wait_ge(yT_ready, k + 1)
                pe.wait_ge(wT_ready, 2)
                for t in range(t0, t1):
                    ins = tr(bank(7 if k < 2 else 0, P * t, P), yT[:, P * t:P * t + P], ident[:])
                ins.then_inc(yt_done, 1)

            for n in range(len(weigh)):
                if n == SECOND:
                    weights(1)
                if n < B * CHS:
                    gate_up(n)
                if n == LEAD - 1:
                    weights(0)
                for m in weigh[n]:
                    spread(m)
                for m in weigh[n - 2] if n > 1 else []:
                    down_mm(m)
                if n == BACK + 1:
                    turn_back(0)
            turn_back(1)
            turn_back(2)

        @block.vector
        def _(dve):
            v = nc.vector
            steps = [0]

            def link(ins):
                steps[0] += 1
                ins.then_inc(dve_step, 1)
                dve.wait_ge(dve_step, steps[0])

            def stats(t0, t1):
                for t in range(t0, t1):
                    ins = v.bn_stats(st[:, t, :], xs[:, t, :])
                link(ins)
                for t in range(t0, t1):
                    ins = v.bn_aggr(mv[:, t, :], st[:, t, :])
                return ins

            def norm(t0, t1, r):
                for t in range(t0, t1):
                    v.tensor_scalar(z[:, t, :], xs[:, t, :], mv[:, t, 0:1], r[:, t:t + 1], ALU.subtract, ALU.mult)\
                     .then_inc(z_ready, 1)

            dve.wait_ge(ld["ctx"], 16)
            for b in range(B):
                ins = v.bn_stats(stc[:, b, :], c_nat[:, b, :])
            link(ins)
            for b in range(B):
                ins = v.bn_aggr(mvc[:, b, :], stc[:, b, :])
            ins.then_inc(ctx_stats, 1)
            dve.wait_ge(ctx_rstd, 1)
            dve.wait_ge(ctx_stats, 1)
            for b in range(B):
                ins = v.tensor_scalar(zc[:, b, :], c_nat[:, b, :], mvc[:, b, 0:1], rstdc[:, b:b + 1], ALU.subtract,
                                      ALU.mult)
            ins.then_inc(zc_ready, 1)
            dve.wait_ge(ld["cols"], 16)
            dve.wait_ge(zcT_done, 1)
            v.tensor_scalar(xnT[:], bank(7, 64, BJ), cl[:, 0:1], cl[:, 1:2], ALU.mult, ALU.add).then_inc(xnT_ready, 1)
            dve.wait_ge(ld["wk"], 16)
            v.tensor_reduce(wks[:], wk[:].rearrange("p (h d) -> p h d", h=H), X, ALU.add).then_inc(wks_ready, 1)
            dve.wait_ge(fexp_done, 1)
            v.tensor_scalar(scl[:], bank(7, 0, 16).rearrange("p (c b) -> p c b", b=B), 1.0, DH ** -0.5, ALU.add,
                            ALU.mult).then_inc(scl_ready, 1)
            dve.wait_ge(scl_ready, 1)
            dve.wait_ge(ld["x"], 16)
            for k in range(3):
                for t in range(TB * k, min(TB * k + TB, T)):
                    ins = v.bn_stats(st[:, t, :], xs[:, t, :])
                if k == 1:
                    link(ins)
                dve.wait_ge(k_done, k + 1)
                c0, c1_ = 3 * k, min(3 * k + 3, PAIRS)
                v.tensor_tensor(kT[:, c0:c1_], bank(k, 0, BJ * (c1_ - c0)).rearrange("p (c b j) -> p c b j", b=B, j=J),
                                scl[:, c0:c1_, :].unsqueeze(3).broadcast_to([P, c1_ - c0, B, J]), ALU.mult)\
                 .then_inc(kT_ready, 1)
            for t in range(T):
                ins = v.bn_aggr(mv[:, t, :], st[:, t, :])
            ins.then_inc(ln_stats, 1)
            dve.wait_ge(ks_done, 1)
            dve.wait_ge(ld["fh"], 16)
            for b in range(B):
                ins = v.tensor_scalar(cr[:, 0, b, :], bank(7, J * b, J, H), fh[:, b:b + 1], DH ** -0.5, ALU.mult,
                                      ALU.mult)
            ins.then_inc(ks_read, 1)
            dve.wait_ge(ks_read, 1)
            for part in range(2):
                link(v.tensor_copy(crp[:, part], cr[:, part]))
                link(v.tensor_tensor(cr[:, part + 1], cr[:, part], crp[:, part], ALU.subtract))
            v.tensor_copy(crp[:, 2], cr[:, 2]).then_inc(crp_ready, 1)
            dve.wait_ge(ln_rstd, 1)
            dve.wait_ge(ln_stats, 1)
            norm(0, T, rstd)
            for k in range(3):
                dve.wait_ge(m_done, 2 * k + 2)
                nh = min(3, 8 - 3 * k)
                for b in range(B):
                    src = bank([6, 0, 1][k], 0, nh * BJ).rearrange("p (h b j) -> p h b j", h=nh, b=B)
                    ins = v.tensor_copy(M[:, b, 6 * k + 1:6 * k + 2 * nh:2, :], src[:, :, b, :])
                ins.then_inc(m_odd, 1)
            dve.wait_ge(vzero, 1)
            for k in range(4):
                dve.wait_ge(v_done, k + 1)
                for h2 in range(2):
                    r = slice(DH * h2, DH * h2 + DH)
                    src = ps[r, 3 + k, 0:2 * BJ].rearrange("p (c b j) -> p c b j", c=2, b=B)
                    for c in range(2):
                        pp = (2 * k + c) % 4
                        at = RG * pp + 2 * JR * pp + JR * h2
                        ins = v.tensor_copy(vrem[r, k // 2, :, at:at + JR], src[:, c, :, JM:J])
                ins.then_inc(vrem_ready, 1)

            SG = [(0, 12), (12, 16)]

            def sbank(g):
                if g == 0:
                    return ps[:, 0:2, 0:6 * J].rearrange("p k (h j) -> p k h j", j=J)
                return ps[:, 2:3, 0:4 * J].rearrange("p k (h j) -> p k h j", j=J)

            def submax(i):
                s = i % 2
                for g, (a, b) in enumerate(SG):
                    dve.wait_ge(s_done, 2 * i + g + 1)
                    k = 2 - g
                    link(v.tensor_reduce(mx1[:, s, a:b].rearrange("p (k h) -> p k h", k=k), sbank(g), X, ALU.max))
                    if i >= 2:
                        dve.wait_ge(nrm_done, i - 1)
                    h = (b - a) // k
                    v.tensor_tensor(pe_[:, s, a:b, :].rearrange("p (k h) j -> p k h j", k=k), sbank(g),
                                    mx1[:, s, a:b].rearrange("p (k h) -> p k h", k=k).unsqueeze(3)
                                    .broadcast_to([P, k, h, J]), ALU.subtract).then_inc(sub_done, 1)

            def sums(i):
                s = i % 2
                dve.wait_ge(exp_done, 2 * i + 2)
                link(v.tensor_reduce(sm1[:, s, :], pe_[:, s], X, ALU.add))
                v.reciprocal(rc1[:, s, :], sm1[:, s, :]).then_inc(rc_ready, 1)

            def resid(i):
                dve.wait_ge(pv_done, i + 1)
                v.tensor_tensor(xs[:, i, :], xs[:, i, :], bank(6 + i % 2, 0, P), ALU.add).then_inc(x1_ready, 1)
                if 0 < i < T - 1:
                    dve.wait_ge(x1_ready, i)
                    ins = v.bn_stats(st[:, i - 1, :], xs[:, i - 1, :])
                    if i == TB:
                        link(ins)

            def aggregate(t0, t1):
                for t in range(t0, t1):
                    ins = v.bn_aggr(mv[:, t, :], st[:, t, :])
                ins.then_inc(ln_stats, 1)

            for i in range(T + 3):
                if 1 <= i <= T:
                    sums(i - 1)
                if i < T:
                    submax(i)
                if i == 1:
                    dve.wait_ge(u_done, 5)
                    v.tensor_copy(U[0:RG, :, 8:10, :], bank(5, 0, 512, RG).rearrange("p (b q d) -> p b q d", b=B, q=2))\
                     .then_inc(u_rem, 1)
                if i >= 3:
                    resid(i - 3)
                if i == T + 1:
                    dve.wait_ge(x1_ready, T - 1)
                    link(v.bn_stats(st[:, T - 2, :], xs[:, T - 2, :]))
                    aggregate(TB, T - 1)
                    dve.wait_ge(ln_rstd, 3)
                    dve.wait_ge(ln_stats, 3)
                    norm(TB, T - 1, rstd)
                    dve.wait_ge(moe_consts_ready, 1)
                    for k in range(SEARCH):
                        ins = v.tensor_scalar(digits[:, k, :], digit_i[:], 3 * (SEARCH - 1 - k), None,
                                              ALU.logical_shift_left)
                    link(ins)
                    link(v.memset(best[:], 0.0))
                if i == TB + 3:
                    aggregate(0, TB)
                if i == T:
                    dve.wait_ge(ln_rstd, 2)
                    dve.wait_ge(ln_stats, 2)
                    norm(0, TB, rstd)
            dve.wait_ge(x1_ready, T)
            link(v.bn_stats(st[:, T - 1, :], xs[:, T - 1, :]))
            aggregate(T - 1, T)

            dve.wait_ge(l1k_done, 1)
            v.tensor_scalar(k1T[:], bank(3, 0, BJ), cl[:, 5:6], None, ALU.add).then_inc(l1k_ready, 1)
            dve.wait_ge(l1v_done, 1)
            dve.wait_ge(ld["row"], 16)
            v.tensor_tensor(v1[:], bank(4, 0, 2 * P, J).rearrange("p (b d) -> p b d", b=B),
                            bv_b[0:J].unsqueeze(1).broadcast_to([J, B, P]), ALU.add).then_inc(l1v_ready, 1)
            dve.wait_ge(ln_rstd, 4)
            dve.wait_ge(ln_stats, 4)
            norm(T - 1, T, rstd)
            dve.wait_ge(lg_done, 1)
            bt = lambda a: a.unsqueeze(2).broadcast_to([P, T, E0])
            link(v.tensor_tensor(lg[:], bank(2, 0, T * E0).rearrange("p (t e) -> p t e", t=T),
                                 bs_b.unsqueeze(1).broadcast_to([P, T, E0]), ALU.add))
            link(v.tensor_reduce(sm8[:, 0, :], lg[:], X, ALU.max))
            v.tensor_tensor(lg[:], lg[:], bt(sm8[:, 0, :]), ALU.subtract).then_inc(lgs_ready, 1)
            dve.wait_ge(lge_ready, 1)
            link(v.tensor_reduce(sm8[:, 1, :], lg[:], X, ALU.add))
            link(v.reciprocal(sm8[:, 2, :], sm8[:, 1, :]))
            v.tensor_tensor(pr[:], lg[:], bt(sm8[:, 2, :]), ALU.mult).then_inc(pr_ready, 1)
            dve.wait_ge(pr_ready, 1)
            for k in range(SEARCH):
                cur, nxt = best[:, k % 2], best[:, (k + 1) % 2]
                link(v.tensor_tensor(cand[:], cur[:, 0, :].bitcast(I32).unsqueeze(1).broadcast_to([P, NM, E0]),
                                     digits[:, k, :].unsqueeze(2).broadcast_to([P, NM, E0]), ALU.bitwise_or))
                v.tensor_tensor(cmp[:], pr[:].unsqueeze(1).broadcast_to([P, NM, T, E0]),
                                cand[:].bitcast(F32).unsqueeze(2).broadcast_to([P, NM, T, E0]), ALU.is_ge)\
                 .then_inc(cmp_ready, 1)
                if k == 0:
                    dve.wait_ge(l1m_done, 1)
                    v.tensor_copy(c1[:], bank(5, 256, BJ, 1))
                if k == 1:
                    v.tensor_copy(M1[:], bank(5, 0, BJ)).then_inc(l1m_ready, 1)
                dve.wait_ge(cnt_done, k + 1)
                link(v.scalar_tensor_tensor(out=cur[:, 1:NM + 1, :],
                                            in0=bank(7, 0, NM * E0).rearrange("p (m e) -> p m e", m=NM),
                                            scalar=float(CAP), in1=cand[:].bitcast(F32), op0=ALU.is_ge, op1=ALU.mult))
                link(v.tensor_reduce(nxt[:, 0, :], cur.rearrange("p m e -> p e m"), X, ALU.max))
            thr = best[:, SEARCH % 2, 0, :].unsqueeze(1).broadcast_to([P, T, E0])
            v.tensor_tensor(ge[:, 0], pr[:], thr, ALU.is_gt)
            v.tensor_tensor(ge[:, 1], pr[:], thr, ALU.is_equal).then_inc(ge_ready, 1)
            dve.wait_ge(rank_done, 1)
            dve.wait_ge(ge_ready, 1)
            rank = bank(6, 0, 2 * T * E0).rearrange("p (g t e) -> p g t e", g=2, t=T)
            link(v.tensor_scalar(need[:], bank(7, 64, E0), -1.0, float(CAP), ALU.mult, ALU.add))
            nb = need[:].unsqueeze(1).broadcast_to([P, T, E0])
            v.tensor_tensor(q1[:], rank[:, 1], nb, ALU.is_le)
            link(v.tensor_tensor(ceq[:], rank[:, 1], nb, ALU.min))
            v.tensor_tensor(q2[:], q1[:], ge[:, 1], ALU.mult)
            link(v.tensor_tensor(ceq[:], rank[:, 0], ceq[:], ALU.add))
            link(v.tensor_tensor(q2[:], q2[:], ge[:, 0], ALU.add))
            link(v.tensor_tensor(slot[:], q2[:], ceq[:], ALU.mult))
            for t in range(T):
                for e in range(E0):
                    ins = v.tensor_scalar(S[:, t, e, :], slot_no[:], slot[:, t, e:e + 1], None, ALU.is_equal)
                ins.then_inc(S_ready, 1)
            dve.wait_ge(gather_done, 1)
            v.tensor_reduce(pv[:], bank(2, 0, 3 * E0).rearrange("p (e a) -> p e a", a=3), X, ALU.add)\
             .then_inc(pv_sum, 1)
            dve.wait_ge(pv_sum, 1)
            dve.wait_ge(ld["b2"], 16)
            for e in range(E0):
                s = e % 2
                dve.wait_ge(y_done, e + 1)
                link(v.tensor_tensor(y1[:], bank(7 * (e % 2), 128, P), b2s[:, e, :], ALU.add))
                link(v.tensor_scalar(y2[:], y1[:], pv[:, e:e + 1], None, ALU.mult))
                if e >= 2:
                    dve.wait_ge(sc_done, 2 * (e - 1))
                link(v.tensor_copy(yp[:, s, 0], y2[:]))
                link(v.tensor_tensor(y3[:], y2[:], yp[:, s, 0], ALU.subtract))
                link(v.tensor_copy(yp[:, s, 1], y3[:]))
                v.tensor_tensor(yp[:, s, 2], y3[:], yp[:, s, 1], ALU.subtract).then_inc(yp_ready, 1)
            for b in range(B):
                dve.wait_ge(sc_done, 2 * (E0 - 1) + b + 1)
                v.tensor_tensor(xs[:, TB * b:TB * b + TB, :], xs[:, TB * b:TB * b + TB, :],
                                bank(3 + b).rearrange("p (t d) -> p t d", t=TB), ALU.add).then_inc(x2_ready, 1)
                dve.wait_ge(x2_ready, b + 1)
                stats(TB * b, TB * b + TB).then_inc(ln_stats, 1)

            for b in range(B):
                dve.wait_ge(ln_rstd, 5 + b)
                norm(TB * b, TB * b + TB, rstd)
            for b in range(B):
                dve.wait_ge(s1_done, b + 1)
                s1 = bank(2 + 2 * b, 0, TB * J).rearrange("p (t j) -> p t j", t=TB)
                link(v.tensor_reduce(sm4[:, b, 0, :], s1, X, ALU.max))
                v.tensor_tensor(p1[:, b], s1, sm4[:, b, 0, :].unsqueeze(2).broadcast_to([P, TB, J]), ALU.subtract)\
                 .then_inc(p1s_ready, 1)
            for b in range(B):
                dve.wait_ge(p1_ready, b + 1)
                link(v.tensor_reduce(sm4[:, b, 1, :], p1[:, b], X, ALU.add))
                link(v.reciprocal(sm4[:, b, 2, :], sm4[:, b, 1, :]))
                dve.wait_ge(pv1_done, b + 1)
                for t in range(TB):
                    q = TB * b + t
                    ins = v.scalar_tensor_tensor(out=xs[:, q, :], in0=bank(5 + 2 * b, P * t, P),
                                                 scalar=sm4[:, b, 2, t:t + 1], in1=xs[:, q, :], op0=ALU.mult,
                                                 op1=ALU.add)
                ins.then_inc(x3_ready, 1)
                dve.wait_ge(x3_ready, b + 1)
                stats(TB * b, TB * b + TB).then_inc(ln_stats, 1)
            for b in range(B):
                dve.wait_ge(ln_rstd, 7 + b)
                norm(TB * b, TB * b + TB, rstd)

            by_group = sf[:].rearrange("p t (g k) -> p (t g) k", g=NG)

            def route_groups(b):
                dve.wait_ge(sig_ready, b + 1)
                link(v.tensor_tensor(sf[:], sc[:, b], rb_b.unsqueeze(1).broadcast_to([P, TB, E1]), ALU.add))
                for t in range(TB):
                    for k in range(NG):
                        ins = v.max(best8[:, t, k, :], sf[:, t, GE * k:GE * k + GE])
                link(ins)
                link(v.tensor_tensor(sum2[:].unsqueeze(3), best8[:, :, :, 0:1], best8[:, :, :, 1:2], ALU.add))

            def route_mask(b):
                mine = sum2[:].unsqueeze(3).broadcast_to([P, TB, NG, NG])
                other = sum2[:].unsqueeze(2).broadcast_to([P, TB, NG, NG])
                v.tensor_tensor(gg[:, 0], other, mine, ALU.is_gt)
                link(v.tensor_tensor(gg[:, 1], other, mine, ALU.is_equal))
                link(v.tensor_tensor(gg[:, 1], gg[:, 1], earlier[:].unsqueeze(1).broadcast_to([P, TB, NG, NG]),
                                     ALU.mult))
                link(v.tensor_tensor(gg[:, 0], gg[:, 0], gg[:, 1], ALU.add))
                link(v.tensor_reduce(gm[:, 0], gg[:, 0], X, ALU.add))
                link(v.tensor_scalar(gm[:, 1], gm[:, 0], 2.0, None, ALU.is_lt))
                link(v.tensor_tensor(by_group, by_group, gm[:, 1].rearrange("p t g -> p (t g)").unsqueeze(2)
                                     .broadcast_to([P, TB * NG, GE]), ALU.mult))

            def route_top(b):
                for t in range(TB):
                    ins = v.max(top8[:, t, :], sf[:, t, :])
                link(ins)
                fourth = top8[:, :, 3:4].broadcast_to([P, TB, E1])
                v.tensor_tensor(r1[:], sf[:], fourth, ALU.is_gt)
                link(v.tensor_tensor(r2[:], sf[:], fourth, ALU.is_equal))
                v.tensor_reduce(n4[:, 0, :], r1[:], X, ALU.add)
                link(v.tensor_tensor_scan(r3[:].rearrange("p t e -> p (t e)"),
                                          scan_keep[:].rearrange("p t e -> p (t e)"),
                                          r2[:].rearrange("p t e -> p (t e)"), 0.0, ALU.mult, ALU.add))
                link(v.tensor_tensor(r3[:], r3[:], n4[:, 0, :].unsqueeze(2).broadcast_to([P, TB, E1]), ALU.add))
                link(v.scalar_tensor_tensor(out=r3[:], in0=r3[:], scalar=4.0, in1=r2[:], op0=ALU.is_le, op1=ALU.mult))
                link(v.tensor_tensor(r3[:], r3[:], r1[:], ALU.add))

            def route_weights(b):
                link(v.tensor_tensor(r3[:], r3[:], sc[:, b], ALU.mult))
                link(v.tensor_reduce(n4[:, 0, :], r3[:], X, ALU.add))
                link(v.tensor_scalar(n4[:, 0, :], n4[:, 0, :], 1e-20, None, ALU.add))
                link(v.reciprocal(n4[:, 1, :], n4[:, 0, :]))
                link(v.scalar_tensor_tensor(out=r3[:], in0=r3[:], scalar=2.5,
                                            in1=n4[:, 1, :].unsqueeze(2).broadcast_to([P, TB, E1]),
                                            op0=ALU.mult, op1=ALU.mult))
                if b == 1:
                    dve.wait_ge(wt_done, 1)
                link(v.tensor_copy(wp[:, :, 0, :], r3[:]))
                link(v.tensor_tensor(r1[:], r3[:], wp[:, :, 0, :], ALU.subtract))
                link(v.tensor_copy(wp[:, :, 1, :], r1[:]))
                v.tensor_tensor(wp[:, :, 2, :], r1[:], wp[:, :, 1, :], ALU.subtract).then_inc(wp_ready, 1)

            def mul_up(n):
                dve.wait_ge(sg_ready, n + 1)
                dve.wait_ge(u1_done, n + 1)
                if n >= NHU and (n - NHU) % CHS == CH:
                    wait_lo(dve, n - NHU)
                v.tensor_tensor(hu[:, n % NHU, :], sg[:, n % 2, :], bank(2 + n % 2), ALU.mult).then_inc(hu_ready, 1)

            def mul_w(n):
                b, c = divmod(n, CHS)
                if c == CH:
                    return
                m = CH * b + c
                dve.wait_ge(hu_ready, n + 1)
                dve.wait_ge(wb_done, m + 1)
                if m >= NHW:
                    last = n - NHW - (1 if (n - NHW) % CHS == CH or (n - NHW) // CHS != b else 0)
                    wait_lo(dve, last)
                v.tensor_tensor(hw[:, m % NHW, :], hu[:, n % NHU, :], bank(4 + m % 2), ALU.mult).then_inc(hw_ready, 1)

            def low_last(n):
                dve.wait_ge(hwhi_ready, n + 1)
                dve.wait_ge(dn_done, n - 2)
                v.tensor_tensor(hw_lo[:, n % 3, :], hidden(n), hw_hi[:, n % 3, :].bitcast(F32), ALU.subtract)\
                 .then_inc(hwlo_last, 1)

            def sum_copy(k):
                b, t0, t1 = PIECES[k]
                v.tensor_copy(yT[:, P * t0:P * t1], bank(6, P * t0, P * (t1 - t0))).then_inc(yT_ready, 1)

            def add_out(k):
                b, t0, t1 = PIECES[k]
                dve.wait_ge(yt_done, k + 1)
                here = xs[:, TB * b + t0:TB * b + t1, :]
                v.tensor_tensor(here, here, bank(7 if k < 2 else 0, P * t0, P * (t1 - t0))
                                .rearrange("p (t d) -> p t d", d=P), ALU.add).then_inc(yo_ready, 1)

            ROUTE = [route_groups, route_mask, route_top, route_weights]
            route_groups(0)
            route_mask(0)
            mul_up(0)
            route_top(0)
            mul_up(1)
            mul_up(2)
            route_weights(0)
            for n in range(3, len(weigh)):
                for m in weigh[n]:
                    mul_w(m)
                if n == BACK:
                    dve.wait_ge(dn_done, CHS)
                    sum_copy(0)
                if n < B * CHS:
                    mul_up(n)
                for m in weigh[n - 1] if n > 0 else []:
                    if m >= BY_DVE:
                        low_last(m)
                if n > LEAD and (n - LEAD) % 2 == 0 and (n - LEAD) // 2 <= len(ROUTE):
                    ROUTE[(n - LEAD) // 2 - 1](1)
                if n == BACK + 2:
                    add_out(0)
            dve.wait_ge(dn_done, B * CHS)
            dve.wait_ge(yt_done, 1)
            sum_copy(1)
            sum_copy(2)
            add_out(1)
            add_out(2)


def kernel(**inputs):
    import numpy as np
    import concourse.bacc as bacc
    from concourse import mybir as mb
    from concourse.bass_utils import run_bass_kernel_spmd

    g = {k: np.asarray(v) for k, v in inputs.items()}
    col = lambda a: np.asarray(a).reshape(-1, P).T
    per = {
        "x": g["x"].reshape(T, P, P).transpose(1, 0, 2),
        "ctx": g["ctx_1024"],
        "ctx_t": g["ctx_1024"].reshape(BJ, P).T,
        "cols": np.concatenate([col(g[k]) for k in ("L0_xattn_ln1_w", "L0_xattn_ln1_b", "L0_xattn_ln2_w",
                                                    "L0_xattn_ln2_b", "L1_xattn_bq", "L1_xattn_bk",
                                                    "L0_ffn_b1")], 1),
        "f_pair": g["fside_Bx16_0"].reshape(B, PAIRS, 2).transpose(2, 1, 0).reshape(2, 2 * PAIRS),
        "f_head": g["fside_Bx16_0"].T,
        "row": np.concatenate([g["L0_ffn_bs"], g["L1_xattn_bv"], g["L1_ffn_router_bias"]]).reshape(1, -1),
        "w_kv": g["L0_xattn_Wkv"],
        "wq_t": g["L0_xattn_Wq"].T,
        "w_out": g["L0_xattn_Wout"],
        "w1": g["L0_ffn_W1"].transpose(1, 0, 2).reshape(P, -1),
        "w2": g["L0_ffn_W2"].reshape(E0, FC, P, P).transpose(2, 0, 1, 3).reshape(P, -1),
        "b2": g["L0_ffn_b2"].reshape(1, -1),
        "l1w": np.concatenate([g["L1_xattn_Wq"], g["L1_xattn_Wk"].T, g["L1_xattn_Wv"].T,
                               g["L1_ffn_router_weight"].T, g["L0_ffn_Ws"]], 1),
        "gate": np.concatenate([g["L1_ffn_gate_w"].reshape(-1, P), g["L1_ffn_shared_gate_w"]]).T,
        "up": np.concatenate([g["L1_ffn_up_w"].reshape(-1, P), g["L1_ffn_shared_up_w"]]).T,
        "down": np.concatenate([g["L1_ffn_down_w"].transpose(0, 2, 1).reshape(CH, P, P),
                                g["L1_ffn_shared_down_w"].T[None]]).transpose(1, 0, 2).reshape(P, -1),
    }
    nc = bacc.Bacc("TRN2", target_bir_lowering=False, num_devices=1)
    arrays, args = {}, []
    for name, a in per.items():
        a = np.ascontiguousarray(a)
        arrays[f"in_{name}_dram"] = a
        args.append(nc.dram_tensor(f"in_{name}_dram", a.shape, mb.dt.from_np(a.dtype), kind="ExternalInput").ap())
    args.append(nc.dram_tensor("out_0_dram", (B, TB * P, P), F32, kind="ExternalOutput").ap())
    block_kernel(nc, *args)
    r = run_bass_kernel_spmd(nc, [arrays], core_ids=[0])
    return r.results[0]["out_0_dram"]
```
